# Optimizing a Trainium2 kernel written in Bass

```python
import numpy as np
import jax
import jax.numpy as jnp

def _softmax(x, axis=-1):
    return jax.nn.softmax(x, axis=axis)

def _gelu(x):
    return jax.nn.gelu(x, approximate=True)

def _silu(x):
    return jax.nn.silu(x)

def _sigmoid(x):
    return jax.nn.sigmoid(x)

def _layernorm(x, axis=-1, eps=1e-05):
    m = jnp.mean(x, axis=axis, keepdims=True)
    v = jnp.var(x, axis=axis, keepdims=True)
    return (x - m) / jnp.sqrt(v + eps)

def _scatter_add(tgt, idx, src, axis=0):
    return tgt.at[idx].add(src)

def _segment_sum(src, seg, n):
    return jax.ops.segment_sum(src, seg, n)
kernel_name = 'mk_adaln_d2_jaxref_r8_d861df'

def setup_inputs(seed: int=0):
    np.random.seed(seed)
    _w = jnp.asarray

    def _L0_attn_setup():
        import jax, jax.numpy as jnp
        import numpy as np
        H = 16
        key = jax.random.key(seed)
        k1, k2, k3, k4, k5 = jax.random.split(key, 5)
        B, S, D = (2, 256, 256)
        scale = 1.0 / np.sqrt(D)
        x = jax.random.normal(k1, (B, S, D), dtype=jnp.float32)
        Wq = jax.random.normal(k2, (D, D), dtype=jnp.float32) * scale
        Wk = jax.random.normal(k3, (D, D), dtype=jnp.float32) * scale
        Wv = jax.random.normal(k4, (D, D), dtype=jnp.float32) * scale
        Wo = jax.random.normal(k5, (D, D), dtype=jnp.float32) * scale
        return {'x': x, 'Wq': Wq, 'Wk': Wk, 'Wv': Wv, 'Wo': Wo}
    _L0_attn_in = _L0_attn_setup()

    def _L0_ffn_setup():
        import jax, jax.numpy as jnp
        import numpy as np
        E, TOP_K, D, H = (8, 2, 256, 176)
        B, S = (2, 256)
        key = jax.random.key(seed)
        ks = jax.random.split(key, 8)
        x = jax.random.normal(ks[0], (B, S, D), dtype=jnp.float32)
        gate_w = jax.random.normal(ks[1], (E, D), dtype=jnp.float32) * (1.0 / np.sqrt(D))
        gate_b = jax.random.normal(ks[2], (E,), dtype=jnp.float32) * 0.01
        bias = jnp.zeros((E,), dtype=jnp.float32)
        w1 = jax.random.normal(ks[3], (E, H, D), dtype=jnp.float32) * (1.0 / np.sqrt(D))
        b1 = jax.random.normal(ks[4], (E, H), dtype=jnp.float32) * 0.01
        w2 = jax.random.normal(ks[5], (E, D, H), dtype=jnp.float32) * (1.0 / np.sqrt(H))
        b2 = jax.random.normal(ks[6], (E, D), dtype=jnp.float32) * 0.01
        return {'x': x, 'gate_w': gate_w, 'gate_b': gate_b, 'bias': bias, 'w1': w1, 'b1': b1, 'w2': w2, 'b2': b2}
    _L0_ffn_in = _L0_ffn_setup()
    _L0_c = _w((lambda *s: np.random.randn(*s).astype(np.float32) * 0.05)(2, 256))
    _L0_wmod = _w((lambda *s: np.random.randn(*s).astype(np.float32) * 0.05)(256, 6 * 256) * 256 ** (-0.5))

    def _L1_attn_setup():
        import jax, jax.numpy as jnp
        import numpy as np
        HIDDEN = 256
        HEADS = 16
        HEAD_SIZE = HIDDEN // HEADS
        key = jax.random.key(seed)
        ks = jax.random.split(key, 9)
        s = 1.0 / np.sqrt(HIDDEN)
        inp = {'x': jax.random.normal(ks[0], (2, 256, HIDDEN), dtype=jnp.float32)}
        for i, name in enumerate(['q', 'k', 'v', 'o']):
            inp[f'w{name}'] = jax.random.uniform(ks[1 + 2 * i], (HIDDEN, HIDDEN), jnp.float32, -s, s)
            inp[f'b{name}'] = jax.random.uniform(ks[2 + 2 * i], (HIDDEN,), jnp.float32, -s, s)
        return inp
    _L1_attn_in = _L1_attn_setup()

    def _L1_ffn_setup():
        import jax, jax.numpy as jnp
        import numpy as np
        ALPHA = 1.702
        LIMIT = 7.0
        EPS = 1e-05
        TOP_K = 4
        key = jax.random.key(seed)
        ks = jax.random.split(key, 8)
        B, S, H, I, E = (2, 64, 256, 256, 16)
        return {'x': jax.random.normal(ks[0], (B, S, H), jnp.float32), 'norm_w': jnp.ones((H,), jnp.float32), 'gate_w': jax.random.normal(ks[1], (E, H), jnp.float32) * 0.02, 'gate_b': jax.random.normal(ks[2], (E,), jnp.float32) * 0.02, 'w1': jax.random.normal(ks[3], (E, 2 * I, H), jnp.float32) * 0.02, 'b1': jax.random.normal(ks[4], (E, 2 * I), jnp.float32) * 0.02, 'w2': jax.random.normal(ks[5], (E, H, I), jnp.float32) * 0.02, 'b2': jax.random.normal(ks[6], (E, H), jnp.float32) * 0.02}
    _L1_ffn_in = _L1_ffn_setup()
    _L1_c = _w((lambda *s: np.random.randn(*s).astype(np.float32) * 0.05)(2, 256))
    _L1_wmod = _w((lambda *s: np.random.randn(*s).astype(np.float32) * 0.05)(256, 6 * 256) * 256 ** (-0.5))
    _d = {'L0_attn_x': _L0_attn_in['x'], 'L0_attn_Wq': _L0_attn_in['Wq'], 'L0_attn_Wk': _L0_attn_in['Wk'], 'L0_attn_Wv': _L0_attn_in['Wv'], 'L0_attn_Wo': _L0_attn_in['Wo'], 'L0_ffn_gate_w': _L0_ffn_in['gate_w'], 'L0_ffn_gate_b': _L0_ffn_in['gate_b'], 'L0_ffn_bias': _L0_ffn_in['bias'], 'L0_ffn_w1': _L0_ffn_in['w1'], 'L0_ffn_b1': _L0_ffn_in['b1'], 'L0_ffn_w2': _L0_ffn_in['w2'], 'L0_ffn_b2': _L0_ffn_in['b2'], 'L0_c': _L0_c, 'L0_wmod': _L0_wmod, 'L1_attn_wq': _L1_attn_in['wq'], 'L1_attn_bq': _L1_attn_in['bq'], 'L1_attn_wk': _L1_attn_in['wk'], 'L1_attn_bk': _L1_attn_in['bk'], 'L1_attn_wv': _L1_attn_in['wv'], 'L1_attn_bv': _L1_attn_in['bv'], 'L1_attn_wo': _L1_attn_in['wo'], 'L1_attn_bo': _L1_attn_in['bo'], 'L1_ffn_norm_w': _L1_ffn_in['norm_w'], 'L1_ffn_gate_w': _L1_ffn_in['gate_w'], 'L1_ffn_gate_b': _L1_ffn_in['gate_b'], 'L1_ffn_w1': _L1_ffn_in['w1'], 'L1_ffn_b1': _L1_ffn_in['b1'], 'L1_ffn_w2': _L1_ffn_in['w2'], 'L1_ffn_b2': _L1_ffn_in['b2'], 'L1_c': _L1_c, 'L1_wmod': _L1_wmod}
    _x0 = _d['L0_attn_x']
    _d['L0_attn_x'] = jax.random.normal(jax.random.fold_in(jax.random.key(seed), 1), (2, 512, 256), dtype=_x0.dtype)
    del _x0
    return _d

def reference(L0_attn_x, L0_attn_Wq, L0_attn_Wk, L0_attn_Wv, L0_attn_Wo, L0_ffn_gate_w, L0_ffn_gate_b, L0_ffn_bias, L0_ffn_w1, L0_ffn_b1, L0_ffn_w2, L0_ffn_b2, L0_c, L0_wmod, L1_attn_wq, L1_attn_bq, L1_attn_wk, L1_attn_bk, L1_attn_wv, L1_attn_bv, L1_attn_wo, L1_attn_bo, L1_ffn_norm_w, L1_ffn_gate_w, L1_ffn_gate_b, L1_ffn_w1, L1_ffn_b1, L1_ffn_w2, L1_ffn_b2, L1_c, L1_wmod):

    def _L0_attn_ref(x, Wq, Wk, Wv, Wo):
        import jax, jax.numpy as jnp
        import numpy as np
        H = 16
        B, S, D = x.shape
        hd = D // H

        def split_heads(t):
            return t.reshape(B, S, H, hd).transpose(0, 2, 1, 3)
        q = split_heads(x @ Wq.T)
        k = split_heads(x @ Wk.T)
        v = split_heads(x @ Wv.T)
        scores = jnp.einsum('bhqd,bhkd->bhqk', q, k) / jnp.sqrt(jnp.asarray(hd, x.dtype))
        causal = jnp.tril(jnp.ones((S, S), dtype=bool))
        scores = jnp.where(causal, scores, -jnp.inf)
        attn = jax.nn.softmax(scores, axis=-1)
        out = jnp.einsum('bhqk,bhkd->bhqd', attn, v)
        out = out.transpose(0, 2, 1, 3).reshape(B, S, D)
        return out @ Wo.T

    def _L0_ffn_ref(x, gate_w, gate_b, bias, w1, b1, w2, b2):
        import jax, jax.numpy as jnp
        import numpy as np
        E, TOP_K, D, H = (8, 2, 256, 176)
        B, S = (2, 256)
        b, s, d = x.shape
        xf = x.reshape(-1, d)
        scores = xf @ gate_w.T + gate_b + bias
        top_scores, top_idx = jax.lax.top_k(scores, TOP_K)
        gates = jax.nn.softmax(top_scores, axis=-1)
        comb = jnp.sum(jax.nn.one_hot(top_idx, E, dtype=gates.dtype) * gates[..., None], axis=1)
        h = jax.nn.silu(jnp.einsum('td,ehd->teh', xf, w1) + b1)
        y = jnp.einsum('teh,edh->ted', h, w2) + b2
        out = jnp.einsum('ted,te->td', y, comb)
        return out.reshape(b, s, d)

    def _L1_attn_ref(x, wq, bq, wk, bk, wv, bv, wo, bo):
        import jax, jax.numpy as jnp
        import numpy as np
        HIDDEN = 256
        HEADS = 16
        HEAD_SIZE = HIDDEN // HEADS
        B, S, H = x.shape
        nh, hd = (HEADS, HEAD_SIZE)

        def proj(w, b):
            y = jnp.einsum('bsh,dh->bsd', x, w) + b
            return y.reshape(B, S, nh, hd).transpose(0, 2, 1, 3)
        q = proj(wq, bq)
        k = proj(wk, bk)
        v = proj(wv, bv)
        scores = jnp.einsum('bhqd,bhkd->bhqk', q, k) / jnp.sqrt(jnp.float32(hd))
        causal = jnp.tril(jnp.ones((S, S), dtype=bool))
        scores = jnp.where(causal, scores, -jnp.inf)
        attn = jax.nn.softmax(scores, axis=-1)
        ctx = jnp.einsum('bhqk,bhkd->bhqd', attn, v)
        ctx = ctx.transpose(0, 2, 1, 3).reshape(B, S, H)
        return jnp.einsum('bsh,dh->bsd', ctx, wo) + bo

    def _L1_ffn_ref(x, norm_w, gate_w, gate_b, w1, b1, w2, b2):
        import jax, jax.numpy as jnp
        import numpy as np
        ALPHA = 1.702
        LIMIT = 7.0
        EPS = 1e-05
        TOP_K = 4
        B, S, H = x.shape
        M = B * S
        E = gate_w.shape[0]
        xf = x.reshape(M, H)
        t = xf * jax.lax.rsqrt(jnp.mean(xf * xf, axis=-1, keepdims=True) + EPS) * norm_w
        logits = t @ gate_w.T + gate_b
        vals, idx = jax.lax.top_k(logits, TOP_K)
        gates_k = jax.nn.softmax(vals, axis=-1)
        G = jnp.zeros((M, E), x.dtype).at[jnp.arange(M)[:, None], idx].set(gates_k)
        h = jnp.einsum('mh,eoh->emo', t, w1) + b1[:, None, :]
        a = jnp.minimum(h[..., ::2], LIMIT)
        b = jnp.clip(h[..., 1::2], -LIMIT, LIMIT)
        act = a * jax.nn.sigmoid(ALPHA * a) * (b + 1.0)
        y = jnp.einsum('emi,edi->emd', act, w2) + b2[:, None, :]
        delta = jnp.einsum('me,emd->md', G, y)
        return x + delta.reshape(B, S, H)
    x = L0_attn_x
    mod = (_silu(L0_c) @ L0_wmod).reshape(L0_c.shape[0], 6, 1, -1)
    sa, ca, ga, sb, cb, gb = (mod[:, 0], mod[:, 1], mod[:, 2], mod[:, 3], mod[:, 4], mod[:, 5])
    ga = (2 * (ga >= 0) - 1) * jnp.maximum(jnp.abs(ga), 0.25)
    gb = (2 * (gb >= 0) - 1) * jnp.maximum(jnp.abs(gb), 0.25)
    h = _layernorm(x, axis=-1) * (1 + ca) + sa
    x = x + ga * _L0_attn_ref(h, L0_attn_Wq, L0_attn_Wk, L0_attn_Wv, L0_attn_Wo)
    h = _layernorm(x, axis=-1) * (1 + cb) + sb
    x = x + gb * _L0_ffn_ref(h, L0_ffn_gate_w, L0_ffn_gate_b, L0_ffn_bias, L0_ffn_w1, L0_ffn_b1, L0_ffn_w2, L0_ffn_b2)
    mod = (_silu(L1_c) @ L1_wmod).reshape(L1_c.shape[0], 6, 1, -1)
    sa, ca, ga, sb, cb, gb = (mod[:, 0], mod[:, 1], mod[:, 2], mod[:, 3], mod[:, 4], mod[:, 5])
    ga = (2 * (ga >= 0) - 1) * jnp.maximum(jnp.abs(ga), 0.25)
    gb = (2 * (gb >= 0) - 1) * jnp.maximum(jnp.abs(gb), 0.25)
    h = _layernorm(x, axis=-1) * (1 + ca) + sa
    x = x + ga * _L1_attn_ref(h, L1_attn_wq, L1_attn_bq, L1_attn_wk, L1_attn_bk, L1_attn_wv, L1_attn_bv, L1_attn_wo, L1_attn_bo)
    h = _layernorm(x, axis=-1) * (1 + cb) + sb
    x = x + gb * _L1_ffn_ref(h, L1_ffn_norm_w, L1_ffn_gate_w, L1_ffn_gate_b, L1_ffn_w1, L1_ffn_b1, L1_ffn_w2, L1_ffn_b2)
    return x

_drawn_inputs = setup_inputs


def setup_inputs(seed=0):
    import zlib

    import numpy as np

    out = dict(_drawn_inputs(seed))
    spreads = {'L0_ffn_bias': (0.0, 0.1), 'L1_ffn_norm_w': (1.0, 0.6)}
    factors = {'L0_ffn_gate_b': 7.588,
     'L0_ffn_b1': 8.0,
     'L0_ffn_b2': 8.0,
     'L1_attn_wq': 8.0,
     'L1_attn_bq': 8.0,
     'L1_attn_wk': 8.0,
     'L1_attn_bk': 64.0,
     'L1_attn_wv': 5.143,
     'L1_attn_bv': 8.0,
     'L1_attn_wo': 4.575,
     'L1_attn_bo': 6.428,
     'L1_ffn_gate_w': 8.0,
     'L1_ffn_gate_b': 8.0,
     'L1_ffn_w1': 7.596,
     'L1_ffn_b1': 8.0,
     'L1_ffn_w2': 7.396,
     'L1_ffn_b2': 62.05}
    for name, (base, spread) in spreads.items():
        noise = np.random.default_rng([zlib.crc32(name.encode()), seed]).standard_normal(out[name].shape)
        drawn = base * np.exp(spread * noise) if base else spread * noise
        out[name] = jnp.asarray(drawn.astype(out[name].dtype))
    for name, factor in factors.items():
        out[name] = (out[name] * factor).astype(out[name].dtype)
    return out
```

```python
from contextlib import ExitStack

import concourse.bass as bass
from concourse import mybir

P = 128
D = 256
KD = D // P
B = 2
S = 512
T = B * S
NT = T // P
TB = S // P
H = 16
HD = D // H
HG = 4
NG = B * H // HG
TERMS = 6
QSIDE = [0, 0, 1, 0, 2, 1]
KSIDE = [0, 1, 0, 2, 0, 1]
SROWS = TERMS * HD
MROWS = SROWS + 2
EPS = 1e-5
LN_CLAMP = 0.25
PK = [0, 512, 1024, 896]
PTW = 1280
BIG_NEG = -1e30

F32 = mybir.dt.float32
BF16 = mybir.dt.bfloat16
I32 = mybir.dt.int32
U32 = mybir.dt.uint32
ALU = mybir.AluOpType
ACT = mybir.ActivationFunctionType
AX = mybir.AxisListType

EXPERTS = [8, 16]
TOPK = [2, 4]
HB = [192, 512]
HK = [96, 128]
HALF = 256
ALPHA = 1.702
LIMIT = 7.0
SLOTS_T = [(T * k - e) // P + e for e, k in zip(EXPERTS, TOPK)]
WROW = [2 * HB[l] + 2 * D for l in range(2)]
BROW = [HB[l] + D for l in range(2)]
UNROLL = 4
STEADY = 7
LOADS_BEFORE = [[16 * sum(len(range(r, n + 1, 4)) for n in SLOTS_T[:l]) for r in range(4)] for l in range(3)]
STORES_BEFORE = [[16 * sum(len(range(r, n, 4)) for n in SLOTS_T[:l]) for r in range(4)] for l in range(3)]
CONST_W = P + 16 + 8 + 256 + 48
BIG_W = 16 * WROW[1]


def build_kernel(nc, dram, out):
    with ExitStack() as ctx:
        def sb(name, shape, dt=F32):
            return ctx.enter_context(nc.sbuf_tensor(name, shape, dt))

        def sem(name):
            return ctx.enter_context(nc.semaphore(name))

        def sems(name, n=2):
            return [sem(f"{name}{i}") for i in range(n)]

        x = sb("x", [P, NT, D])
        big = sb("big", [P, BIG_W])
        ptm = sb("ptm", [P, 2 * HG * PTW])
        tok = sb("tok", [P, NT, D])
        feat = sb("feat", [P, KD, T])
        modbc = sb("modbc", [P, B, 4, D])
        parts = sb("parts", [P, 2, 2, 3, S], BF16)
        tok_flat = tok[:, :, :].rearrange("p t c -> p (t c)")
        qkf = tok_flat[:, 0:2 * S].rearrange("p (n t) -> p n t", n=2)
        rest = tok_flat[:, 2 * S:3 * S]
        wqkv = sb("wqkv", [P, KD, 3 * D])
        wo = sb("wo", [P, KD, D])
        ctxden = sb("ctxden", [P, 2, S])
        consts = sb("consts", [P, CONST_W])
        constb_f = ptm[:, 0:3 * P]
        constb = sb("constb", [P, 3, P], BF16)
        cT = sb("cT", [P, 2, KD, B])
        silc = sb("silc", [P, 2, KD, B])
        silb = ptm[:, 4096:4096 + KD * B * P].rearrange("p (k b n) -> p k b n", k=KD, b=B)
        modcol = sb("modcol", [P, 2, 4, B])
        rows = sb("rows", [P, 3, D])
        qkb = sb("qkb", [P, 4])
        qkb4 = sb("qkb4", [P, 4])
        gbias = sb("gbias", [P, 3, 16])
        gw = sb("gw", [P, 2, KD, 16])
        stats = sb("stats", [P, NT, 6])
        mv = sb("mv", [P, NT, 2])
        rstd = sb("rstd", [P, NT])
        vareps = sb("vareps", [P, NT])
        neghalf = sb("neghalf", [P, NT])
        sumsq = sb("sumsq", [P, NT])
        mx = sb("mx", [P, 2, 16])
        mneg = sb("mneg", [P, 2, 32], BF16)
        mT = sb("mT", [32, 2, P], BF16)
        rden = sb("rden", [P, 2, 16])
        tmp = sb("tmp", [P, 2, D])
        parts_flat = parts[:, :, :, :, :].rearrange("p a b c d -> p (a b c d)")
        bfull = parts_flat[0:16, 0:2 * BROW[1]].bitcast(F32)
        bparts = parts_flat[0:16, 2 * BROW[1]:5 * BROW[1]].rearrange("p (r c) -> p r c", r=3)
        logit = sb("logit", [P, NT, 16])
        top8 = sb("top8", [P, NT, 8])
        idx8 = sb("idx8", [P, NT, 8], U32)
        idf = sb("idf", [P, NT, 4])
        feat_flat = feat[:, :, :].rearrange("p k t -> p (k t)")
        onehot = feat_flat[:, 0:NT * 4 * 16]
        picked = feat_flat[:, NT * 4 * 16:NT * 4 * 16 + 48 * 16]
        chosen = sb("chosen", [P, NT * 16], BF16)
        gate = sb("gate", [P, NT, 4])
        gexp = sb("gexp", [P, NT, 4])
        gsum = sb("gsum", [P, NT])
        grec = sb("grec", [P, NT])
        ntile = sb("ntile", [P, 16])
        excl = sb("excl", [P, 16])
        incl = sb("incl", [P, 16])
        slot = sb("slot", [P, NT * 16])
        slotf = sb("slotf", [P, NT * 4])
        slotk = sb("slotk", [P, NT * 4], U32)
        tef = sb("tef", [1, 48])
        te = sb("te", [1, 48], I32)

        half = BIG_W // 2
        qr = big[:, half:half + 4096].bitcast(BF16).rearrange("p (r h t) -> p r h t", r=2, h=8)
        kr = big[:, half + 4096:half + 8192].bitcast(BF16).rearrange("p (r h t) -> p r h t", r=2, h=8)
        vaug = big[:, half + 8192:half + 12288].rearrange("p (t h c) -> p t h c", t=NT, h=H)
        pt = ptm[:, :].rearrange("p (r j c) -> p r j c", r=2, j=HG)
        wmod = ptm[:, 512:512 + KD * 6 * D].rearrange("p (k n) -> p k n", k=KD)
        zeros = sb("zeros", [P, D])
        brows = ptm[:, 0:16 * BROW[1] // 2].bitcast(BF16)
        o = 16 * BROW[1] // 2
        xt = ptm[:, o:o + 4 * D].rearrange("p (r c) -> p r c", r=4)
        o += 4 * D
        xtT = ptm[:, o:o + 2 * D].rearrange("p (r k c) -> p r k c", r=2, k=KD)
        o += 2 * D
        hid = ptm[:, o:o + 2 * D].rearrange("p (r c) -> p r c", r=2)
        o += 2 * D
        hidT = ptm[:, o:o + 2 * D].rearrange("p (r k c) -> p r k c", r=2, k=KD)
        o += 2 * D
        yt = ptm[:, o:o + 4 * D].rearrange("p (r c) -> p r c", r=4)
        o += 4 * D
        assert o <= 2 * HG * PTW
        ga_ = qkf[:, :, 0:D]
        gb_ = qkf[:, :, D:2 * D]
        gs_ = ctxden[:, :, 0:D]
        gu_ = ctxden[:, :, D:2 * D]
        yg = ptm[:, 6144:6144 + 4 * D].rearrange("p (r c) -> p r c", r=4)

        ident = consts[:, 0:P]
        iota_e = consts[:, P:P + 16]
        c128 = consts[:, P + 16:P + 24]
        lower = consts[:, P + 24:P + 280].rearrange("p (a b) -> p a b", a=16)
        iota_t = consts[0:1, P + 280:P + 328]
        ident_b = constb[:, 0, :]
        causal_b = constb[:, 1, :]
        before_b = constb[:, 2, :]
        ones_b = sb("ones_b", [P, P], BF16)

        bank = [ctx.enter_context(nc.psum_tensor(f"bank{i}", [P, 1024], F32)) for i in range(2)]
        bank += [ctx.enter_context(nc.psum_tensor(f"bank{i}", [P, 512], F32)) for i in range(2, 6)]
        ps = [bank[0][:, 0:512], bank[0][:, 512:1024], bank[1][:, 0:512], bank[1][:, 512:1024]]
        ps += [bank[i][:, :] for i in range(2, 6)]

        xd = [nc.dram_tensor(f"dispatched{l}", [(SLOTS_T[l] + 1) * P, D], F32, kind="Internal") for l in range(2)]
        yd = [nc.dram_tensor(f"expert_rows{l}", [SLOTS_T[l] * P, D], F32, kind="Internal") for l in range(2)]

        ld_const = sem("ld_const")
        ld_x = sems("ld_x")
        ld_mod = sems("ld_mod")
        ld_wqkv = sems("ld_wqkv")
        ld_wo = sems("ld_wo")
        ld_small = sem("ld_small")
        ld_bias = sems("ld_bias")
        ld_w_lo = sems("ld_w_lo")
        ld_w_hi = sem("ld_w_hi")
        zeroed = sem("zeroed")
        set_up = sem("set_up")
        silu_done = sem("silu_done")
        silb_done = sems("silb_done")
        mod_ps = sems("mod_ps")
        mod_sb = sems("mod_sb")
        qkb_done = sem("qkb_done")
        dve_own = sem("dve_own")
        pool_own = sem("pool_own")
        act_own = sem("act_own")
        var_ready = [sems(f"var_ready{l}_") for l in range(2)]
        rstd_ready = [sems(f"rstd_ready{l}_") for l in range(2)]
        xhat_ready = [sems(f"xhat_ready{l}_") for l in range(2)]
        tr_ps = [sems(f"tr_ps{l}_", 3) for l in range(2)]
        feat_ready = [sems(f"feat_ready{l}_", 3) for l in range(2)]
        qkv_ps = sems("qkv_ps")
        qkf_ready = sems("qkf_ready")
        v_ready = sems("v_ready")
        parts_ready = sems("parts_ready")
        spread = sems("spread", 4)
        a_ps = sems("a_ps")
        a_max = sems("a_max")
        m_ready = sems("m_ready")
        m_tr = sems("m_tr")
        mT_ready = sems("mT_ready")
        m_rows = [sems(f"m_rows{l}_") for l in range(2)]
        b_ps = sems("b_ps")
        b_exp = sems("b_exp")
        pv_ps = sems("pv_ps")
        ctxden_ready = sems("ctxden_ready")
        c_tr = sems("c_tr")
        ctx_ready = sems("ctx_ready")
        wo_ps = sems("wo_ps")
        wo_added = sems("wo_added")
        gate_ps = sems("gate_ps")
        chosen_ready = sems("chosen_ready")
        gexp_in = sems("gexp_in")
        gexp_done = sems("gexp_done")
        rank_ps = sems("rank_ps")
        slots_ready = sems("slots_ready")
        bparts_ready = sems("bparts_ready")
        brows_ready = sems("brows_ready")
        scattered = sems("scattered")
        rms_in = sem("rms_in")
        rms_out = sem("rms_out")
        tok_ready = sems("tok_ready")
        xt_loaded = sems("xt_loaded", 4)
        xT_ps = sems("xT_ps")
        xT_sb = sems("xT_sb")
        h_ps = sems("h_ps")
        h_read = sem("h_read")
        sig_in = sem("sig_in")
        sig_done = sem("sig_done")
        gu_done = sem("gu_done")
        hid_ready = sems("hid_ready")
        hT_ps = sems("hT_ps")
        hT_sb = sems("hT_sb")
        y_ps = sems("y_ps")
        y_sb = sems("y_sb")
        y_stored = sems("y_stored", 4)
        gathered = sems("gathered", 4)
        y_added = sems("y_added")
        x_new = sems("x_new")
        stored = sem("stored")

        def moe_w1(l, k, e):
            v = big[:, 0:EXPERTS[l] * WROW[l]].rearrange("p (e c) -> p e c", e=EXPERTS[l])
            return v[:, bass.ds(e, 1), k * HB[l]:(k + 1) * HB[l]].rearrange("p a b -> p (a b)")

        def moe_w2(l, k, e):
            v = big[:, 0:EXPERTS[l] * WROW[l]].rearrange("p (e c) -> p e c", e=EXPERTS[l])
            lo = 2 * HB[l] + k * D
            return v[0:HK[l], bass.ds(e, 1), lo:lo + D].rearrange("p a b -> p (a b)")

        def moe_bias(l, lo, hi, e):
            v = brows[0:3, 0:EXPERTS[l] * BROW[l]].rearrange("p (e c) -> p e c", e=EXPERTS[l])
            return v[:, bass.ds(e, 1), lo:hi].rearrange("p a b -> p (a b)")

        A_CHUNKS = [(0, 0, 4), (1, 0, 4), (2, 0, 2), (2, 2, 2), (3, 0, 2), (3, 2, 2)]
        NA = len(A_CHUNKS)
        B_CHUNKS = []
        for j0 in (0, 2):
            B_CHUNKS += [[(j0, 0, 0)], [(j0, 1, 0), (j0, 3, 384)], [(j0 + 1, 0, 0)],
                         [(j0 + 1, 1, 0), (j0 + 1, 3, 384)], [(j0, 2, 0), (j0 + 1, 2, 256)]]
        NB = len(B_CHUNKS)

        def a_view(c):
            i, _, n = A_CHUNKS[c]
            w = (i + 1) * P
            full = bank[c % 2][:, :]
            if n == 4:
                return full[:, 0:4 * w].rearrange("p (j w) -> p j w", j=4)
            return full.rearrange("p (j w) -> p j w", j=2)[:, :, 0:w]


        def tile_at(ii, off):
            return 4 * ii + off, off % 4, ii + off // 4

        def qkv_fills():
            for b in range(B):
                yield from (("q", b, 0), ("k", b, 0), ("v", b, 0), ("v", b, 1), ("q", b, 1), ("k", b, 1))

        FILLS = list(qkv_fills())

        def wait_fill_read(eng, l, n):
            kind = FILLS[n][0]
            before = [f[0] == "v" for f in FILLS[:n + 1]]
            if kind == "v":
                eng.wait_ge(v_ready[l], sum(before))
            else:
                eng.wait_ge(qkf_ready[l], len(before) - sum(before))

        block = ctx.enter_context(nc.Block())

        @block.sync
        def _(sp):
            nc.sync.dma_start(x[:, 0:TB, :], dram["x"][0:S, :].rearrange("(t p) c -> p t c", p=P)).then_inc(ld_x[0], 16)
            nc.sync.dma_start(consts[:, :], dram["consts"]).then_inc(ld_const, 16)
            nc.sync.dma_start(constb_f, dram["constb"]).then_inc(ld_const, 16)
            nc.sync.dma_start(cT[:, :, :, :].rearrange("p l k b -> p (l k b)"), dram["cT"]).then_inc(ld_const, 16)
            nc.sync.dma_start(wmod, dram["wmod"][0]).then_inc(ld_mod[0], 16)
            nc.sync.dma_start(x[:, TB:NT, :], dram["x"][S:T, :].rearrange("(t p) c -> p t c", p=P)).then_inc(ld_x[1], 16)
            nc.sync.dma_start(wqkv[:, :, :], dram["wqkv"][0]).then_inc(ld_wqkv[0], 16)
            nc.sync.dma_start(wo[:, :, :], dram["wo"][0]).then_inc(ld_wo[0], 16)
            nc.sync.dma_start(rows[:, :, :], dram["rows"]).then_inc(ld_small, 16)
            nc.sync.dma_start(qkb[:, :], dram["qkb"]).then_inc(ld_small, 16)
            nc.sync.dma_start(gbias[:, :, :], dram["gbias"]).then_inc(ld_small, 16)
            nc.sync.dma_start(gw[:, :, :, :], dram["gw"]).then_inc(ld_small, 16)
            nc.sync.dma_start(big[:, 0:EXPERTS[0] * WROW[0]], dram["moe0"]).then_inc(ld_w_lo[0], 16)
            sp.wait_ge(set_up, 1)
            for l in range(2):
                nc.sync.dma_start(xd[l][:, :].rearrange("(t p) c -> p t c", p=P),
                                  zeros[:, :].unsqueeze(1).broadcast_to([P, SLOTS_T[l] + 1, D])).then_inc(zeroed, 16)

            def spread_unit(l, u):
                sp.wait_ge(parts_ready[l], 2 * (u + 1))
                if u >= 2:
                    sp.wait_ge(b_ps[l], NB * 2 * (u - 1))
                elif l == 1:
                    sp.wait_ge(b_ps[0], NB * NG)
                for n, (dst, side) in enumerate(((qr, QSIDE), (kr, KSIDE))):
                    for r in range(TERMS):
                        nc.sync.dma_start(
                            dst[r * HD:(r + 1) * HD, u % 2, :, :],
                            parts[:, n, u % 2, side[r], :],
                        ).then_inc(spread[u], 16)

            def send_maxima(l, g):
                sp.wait_ge(mT_ready[l], g + 1)
                hl = (g % 2) * HG
                for r in range(2):
                    nc.sync.dma_start(
                        qr[SROWS + r:SROWS + r + 1, (g // 2) % 2, hl:hl + HG, :],
                        mT[r * 16:(r + 1) * 16, g % 2, :]).then_inc(m_rows[l][g % 2], 16)

            for l in range(2):
                spread_unit(l, 0)
                spread_unit(l, 1)
                send_maxima(l, 0)
                send_maxima(l, 1)
                spread_unit(l, 2)
                send_maxima(l, 2)
                send_maxima(l, 3)
                spread_unit(l, 3)
                for u in range(4):
                    sp.wait_ge(spread[u], 16 * 2 * TERMS * (l + 1))
                nc.sync.dma_start(bfull[0:EXPERTS[l], 0:BROW[l]], dram[f"bias{l}"]).then_inc(ld_bias[l], 16)
                for g in range(4, NG):
                    send_maxima(l, g)
                if l == 1:
                    sp.wait_ge(pv_ps[1], NG)
                    nc.sync.dma_start(big[:, half:BIG_W], dram["moe1"][:, half:BIG_W]).then_inc(ld_w_hi, 16)
                else:
                    sp.wait_ge(qkv_ps[0], len(FILLS))
                    nc.sync.dma_start(wqkv[:, :, :], dram["wqkv"][1]).then_inc(ld_wqkv[1], 16)
                    sp.wait_ge(wo_ps[0], NT // 2)
                    nc.sync.dma_start(wo[:, :, :], dram["wo"][1]).then_inc(ld_wo[1], 16)
                sp.wait_ge(bparts_ready[l], 1)
                sp.wait_ge(pv_ps[l], NG)
                for r in range(3):
                    nc.sync.dma_start(
                        brows[r:r + 1, 0:EXPERTS[l] * BROW[l]].rearrange("p (e c) -> p e c", e=EXPERTS[l]),
                        bparts[0:EXPERTS[l], r, 0:BROW[l]]).then_inc(brows_ready[l], 16)
                n = SLOTS_T[l]
                sp.wait_ge(scattered[l], 16 * NT * TOPK[l])

                def load(s, r):
                    nc.sync.dma_start(xt[:, r, :], xd[l][bass.ds(s * P, P), :]).then_inc(xt_loaded[r], 16)

                def store(s, r):
                    sp.wait_ge(y_sb[l], s + 1)
                    nc.sync.dma_start(yd[l][bass.ds(s * P, P), :], yt[:, r, :]).then_inc(y_stored[r], 16)

                for s in range(4):
                    load(s, s)
                with sp.Fori(0, (n - 3) // UNROLL) as ii:
                    for q in range(UNROLL):
                        s, r, _ = tile_at(ii, q)
                        sp.wait_ge(xT_ps[l], s + 1)
                        load(s + 4, r)
                        store(s, r)
                for s in range(n - 3, n):
                    store(s, s % 4)
                if l == 0:
                    sp.wait_ge(y_ps[0], n)
                    nc.sync.dma_start(wmod, dram["wmod"][1]).then_inc(ld_mod[1], 16)
                    nc.sync.dma_start(big[:, 0:half], dram["moe1"][:, 0:half]).then_inc(ld_w_lo[1], 16)
            for t in range(NT):
                sp.wait_ge(x_new[1], t + 1)
                nc.sync.dma_start(out[t * P:(t + 1) * P, :], x[:, t, :]).then_inc(stored, 16)
            sp.wait_ge(stored, 16 * NT)
            for r in range(4):
                sp.wait_ge(y_stored[r], STORES_BEFORE[2][r])
                sp.wait_ge(xt_loaded[r], LOADS_BEFORE[2][r])

        @block.gpsimd
        def _(pool):
            nc.gpsimd.memset(zeros[:, :], 0.0).then_inc(set_up, 1)
            nc.gpsimd.memset(neghalf[:, :], -0.5).then_inc(pool_own, 1)
            pool.wait_ge(pool_own, 1)

            def inverse_root(l, which, b):
                pool.wait_ge(var_ready[l][which], b + 1)
                c = slice(b * TB, (b + 1) * TB)
                nc.gpsimd.tensor_tensor(rstd[:, c], vareps[:, c], neghalf[:, c], ALU.pow).then_inc(rstd_ready[l][which], 1)

            for l in range(2):
                inverse_root(l, 0, 0)
                inverse_root(l, 0, 1)
                for b in range(B):
                    inverse_root(l, 1, b)
                    if l == 1:
                        c = slice(b * TB, (b + 1) * TB)
                        pool.wait_ge(rms_in, b + 1)
                        nc.gpsimd.tensor_tensor(rstd[:, c], vareps[:, c], neghalf[:, c], ALU.pow).then_inc(rms_out, 1)
                pool.wait_ge(zeroed, 32)
                pool.wait_ge(slots_ready[l], 1)
                K = TOPK[l]
                for t in range(NT):
                    for k in range(K):
                        n = t * K + k
                        nc.gpsimd.indirect_dma_start(
                            out=xd[l][:, :], out_offset=bass.IndirectOffsetOnAxis(ap=slotk[:, n:n + 1], axis=0),
                            in_=tok[:, t, :], in_offset=None).then_inc(scattered[l], 16)
                for r in range(4):
                    pool.wait_ge(y_stored[r], STORES_BEFORE[l + 1][r])
                for n in range(NT * K):
                    if n >= 4:
                        pool.wait_ge(y_added[l], n - 3)
                    nc.gpsimd.indirect_dma_start(
                        out=yg[:, n % 4, :], out_offset=None, in_=yd[l][:, :],
                        in_offset=bass.IndirectOffsetOnAxis(ap=slotk[:, n:n + 1], axis=0)).then_inc(gathered[n % 4], 16)

        @block.scalar
        def _(act):
            act.wait_ge(ld_const, 48)
            nc.scalar.activation(silc[:, :, :, :].rearrange("p l k b -> p (l k b)"),
                                 cT[:, :, :, :].rearrange("p l k b -> p (l k b)"), ACT.Silu).then_inc(silu_done, 1)

            def move_transposed(l, which):
                for b in range(B):
                    for k in range(KD):
                        n = KD * b + k
                        if which == 0:
                            act.wait_ge(mod_sb[l], 1)
                        act.wait_ge(tr_ps[l][which], n + 1)
                        dst, src = feat[:, k, b * S:(b + 1) * S], ps[4 + n % 2]
                        if which == 0:
                            nc.scalar.activation(dst, src, ACT.Identity, scale=modcol[:, l, 2 + k, b:b + 1],
                                                 bias=modcol[:, l, k, b:b + 1]).then_inc(feat_ready[l][which], 1)
                        else:
                            nc.scalar.activation(dst, src, ACT.Copy).then_inc(feat_ready[l][which], 1)

            for l in range(2):
                move_transposed(l, 0)
                m = 0
                if l == 1:
                    act.wait_ge(qkb_done, 1)
                for n, (kind, b, u) in enumerate(FILLS):
                    if kind == "v" and l == 1:
                        continue
                    act.wait_ge(qkv_ps[l], n + 1)
                    src = ps[n % 4]
                    if kind == "v":
                        t = b * TB + 2 * u
                        nc.scalar.activation(vaug[:, t:t + 2, :, 0:HD],
                                             src.rearrange("p (t h d) -> p t h d", t=2, h=H), ACT.Copy).then_inc(v_ready[l], 1)
                        continue
                    side = 0 if kind == "q" else 1
                    unit = 2 * b + u
                    scale = HD ** -0.5 if side == 0 else 1.0
                    bias = 0.0 if l == 0 else qkb4[:, 2 * side + u:2 * side + u + 1]
                    if m >= 2:
                        act.wait_ge(parts_ready[l], m - 1)
                    if unit >= 2:
                        act.wait_ge(spread[unit - 2], 16 * 2 * TERMS * (l + 1))
                    nc.scalar.activation(qkf[:, side, :], src, ACT.Identity, scale=scale, bias=bias).then_inc(act_own, 1)
                    nc.scalar.activation(parts[:, side, unit % 2, 0, :], src, ACT.Identity, scale=scale,
                                         bias=bias).then_inc(qkf_ready[l], 1)
                    m += 1

                def move_context(g):
                    act.wait_ge(pv_ps[l], g + 1)
                    if g >= 2:
                        act.wait_ge(c_tr[l], g - 1)
                    nc.scalar.activation(ctxden[:, g % 2, :], ps[6], ACT.Copy).then_inc(ctxden_ready[l], 1)

                for s in range(NG + 2):
                    if 0 <= s - 2 < NG:
                        move_context(s - 2)
                    g = s - 1
                    if not 0 <= g < NG:
                        continue
                    for c, pieces in enumerate(B_CHUNKS):
                        n = NB * g + c
                        if c == 0 and g >= 2:
                            act.wait_ge(pv_ps[l], g - 1)
                        act.wait_ge(b_ps[l], n + 1)
                        src = ps[4 + c % 2]
                        j, k, _ = pieces[0]
                        if k == 2:
                            dst = pt[:, g % 2, j:j + 2, PK[2]:PK[2] + 256]
                            src = src.rearrange("p (j q) -> p j q", j=2)
                        else:
                            dst = pt[:, g % 2, j, PK[k]:PK[k] + 512]
                        nc.scalar.activation(dst, src, ACT.Exp).then_inc(b_exp[l], 1)
                move_transposed(l, 1)
                move_transposed(l, 2)
                act.wait_ge(gexp_in[l], 1)
                nc.scalar.activation(gexp[:, :, 0:TOPK[l]], gexp[:, :, 0:TOPK[l]], ACT.Exp).then_inc(gexp_done[l], 1)

                def act_x(ii, off):
                    i, _, _ = tile_at(ii, off)
                    act.wait_ge(xT_ps[l], i + 1)
                    if not (isinstance(i, int) and i < 2):
                        act.wait_ge(h_ps[l], i - 1)
                    nc.scalar.activation(xtT[:, off % 2, :, :].rearrange("p k c -> p (k c)"),
                                         ps[off % 2][:, 0:D], ACT.Copy).then_inc(xT_sb[l], 1)

                def act_hid(ii, off):
                    i, _, _ = tile_at(ii, off)
                    if l == 0:
                        act.wait_ge(h_ps[l], i + 1)
                        if not (isinstance(i, int) and i < 2):
                            act.wait_ge(hT_ps[l], i - 1)
                        nc.scalar.activation(hid[:, off % 2, 0:HB[0]], ps[2 + off % 2][:, 0:HB[0]],
                                             ACT.Silu).then_inc(hid_ready[l], 1)
                    else:
                        act.wait_ge(sig_in, i + 1)
                        nc.scalar.activation(gs_[:, off % 2, :], ga_[:, off % 2, :], ACT.Sigmoid,
                                             scale=ALPHA).then_inc(sig_done, 1)

                def act_hT(ii, off):
                    i, _, _ = tile_at(ii, off)
                    act.wait_ge(hT_ps[l], i + 1)
                    if not (isinstance(i, int) and i < 2):
                        act.wait_ge(y_ps[l], i - 1)
                    nc.scalar.activation(hidT[:, off % 2, :, :].rearrange("p k c -> p (k c)"),
                                         ps[4 + off % 2][:, 0:D], ACT.Copy).then_inc(hT_sb[l], 1)

                def act_y(ii, off):
                    i, r, rnd = tile_at(ii, off)
                    act.wait_ge(y_ps[l], i + 1)
                    if not (isinstance(i, int) and i < 4):
                        act.wait_ge(y_stored[r], STORES_BEFORE[l][r] + 16 * rnd)
                    nc.scalar.activation(yt[:, r, :], ps[6 + off % 2][:, 0:D], ACT.Copy).then_inc(y_sb[l], 1)

                def act_step(ii, off):
                    n = SLOTS_T[l]
                    known = isinstance(ii, int)
                    if l == 1 and (not known or off < n):
                        act_x(ii, off)
                    if not known or 0 <= off - 1 < n:
                        act_hid(ii, off - 1)
                    if l == 1 and (not known or 0 <= off - 2 < n):
                        act_hT(ii, off - 2)
                    if not known or 0 <= off - 3 < n:
                        act_y(ii, off - 3)

                for s in range(STEADY):
                    act_step(0, s)
                with act.Fori(0, (SLOTS_T[l] - STEADY) // UNROLL) as ii:
                    for q in range(UNROLL):
                        act_step(ii, STEADY + q)
                for s in range(SLOTS_T[l], SLOTS_T[l] + 3):
                    act_step(0, s)

        @block.vector
        def _(dve):
            links = [0]

            def link(ins):
                links[0] += 1
                ins.then_inc(dve_own, 1)
                dve.wait_ge(dve_own, links[0])

            link(nc.vector.memset(ones_b[:, :], 1.0))
            link(nc.vector.memset(vaug[:, :, :, :], 1.0))
            link(nc.vector.memset(kr[SROWS:MROWS, :, :, :], 1.0))
            dve.wait_ge(ld_const, 48)
            link(nc.vector.tensor_copy(constb[:, :, :].rearrange("p a c -> p (a c)"), constb_f))

            def spread_silu(l):
                dve.wait_ge(silu_done, 1)
                nc.vector.tensor_copy(
                    silb.rearrange("p k b n -> p (k b) n"),
                    silc[:, l, :, :].rearrange("p k b -> p (k b)").unsqueeze(2).broadcast_to([P, KD * B, P]),
                ).then_inc(silb_done[l], 1)

            def modulation(l):
                dve.wait_ge(mod_ps[l], 1)
                link(nc.vector.tensor_copy(modcol[:, l, 0:2, :].rearrange("p c b -> p (c b)"), ps[7][:, 0:4]))
                nc.vector.tensor_scalar(modcol[:, l, 2:4, :].rearrange("p c b -> p (c b)"), ps[7][:, 4:8], 1.0,
                                        None, ALU.add).then_inc(mod_sb[l], 1)
                for b in range(B):
                    for gi, src in ((0, ps[2 * b][:, 0:D]), (3, ps[2 * b + 1][:, D:2 * D])):
                        link(nc.vector.tensor_scalar(tmp[:, 0, :], src, 0.0, 2.0, ALU.is_ge, ALU.mult))
                        link(nc.vector.tensor_scalar(tmp[:, 0, :], tmp[:, 0, :], 1.0, None, ALU.subtract))
                        link(nc.vector.tensor_tensor(tmp[:, 1, :], src, tmp[:, 0, :], ALU.mult))
                        link(nc.vector.scalar_tensor_tensor(modbc[:, b, gi, :], tmp[:, 1, :], LN_CLAMP, tmp[:, 0, :],
                                                            ALU.max, ALU.mult))
                    link(nc.vector.tensor_copy(modbc[:, b, 1, :], ps[2 * b][:, D:2 * D]))
                    nc.vector.tensor_scalar(modbc[:, b, 2, :], ps[2 * b + 1][:, 0:D], 1.0, None,
                                            ALU.add).then_inc(mod_sb[l], 1)

            def normalise(l, which, b):
                for t in range(b * TB, (b + 1) * TB):
                    link(nc.vector.bn_stats(stats[:, t, :], x[:, t, :]))
                    link(nc.vector.bn_aggr(mv[:, t, :], stats[:, t, :]))
                c = slice(b * TB, (b + 1) * TB)
                nc.vector.tensor_scalar(vareps[:, c], mv[:, c, 1], EPS, None, ALU.add).then_inc(var_ready[l][which], 1)
                dve.wait_ge(rstd_ready[l][which], b + 1)
                for t in range(b * TB, (b + 1) * TB):
                    nc.vector.tensor_scalar(tok[:, t, :], x[:, t, :], mv[:, t, 0:1], rstd[:, t:t + 1],
                                            ALU.subtract, ALU.mult).then_inc(xhat_ready[l][which], 1)
                dve.wait_ge(xhat_ready[l][which], (b + 1) * TB)

            spread_silu(0)
            for l in range(2):
                if l == 1:
                    modulation(1)
                    dve.wait_ge(ld_small, 64)
                    link(nc.vector.tensor_scalar(qkb4[:, 0:2], qkb[:, 0:2], HD ** -0.5, None, ALU.mult))
                    nc.vector.tensor_copy(qkb4[:, 2:4], qkb[:, 2:4]).then_inc(qkb_done, 1)
                for b in range(B):
                    if l == 0:
                        dve.wait_ge(ld_x[b], 16)
                    normalise(l, 0, b)
                if l == 0:
                    modulation(0)
                m = 0
                for n, (kind, b, u) in enumerate(FILLS):
                    if kind == "v":
                        if l == 1:
                            dve.wait_ge(qkv_ps[l], n + 1)
                            t = b * TB + 2 * u
                            for half_t in range(2):
                                ins = nc.vector.tensor_tensor(
                                    vaug[:, t + half_t, :, 0:HD],
                                    ps[n % 4][:, half_t * D:(half_t + 1) * D].rearrange("p (h d) -> p h d", h=H),
                                    rows[:, 0, :].rearrange("p (h d) -> p h d", h=H), ALU.add)
                            ins.then_inc(v_ready[l], 1)
                        continue
                    side, r = (0 if kind == "q" else 1), (2 * b + u) % 2
                    dve.wait_ge(qkf_ready[l], m + 1)
                    link(nc.vector.tensor_tensor(rest, qkf[:, side, :], parts[:, side, r, 0, :], ALU.subtract))
                    link(nc.vector.tensor_copy(parts[:, side, r, 1, :], rest))
                    nc.vector.tensor_tensor(parts[:, side, r, 2, :], rest, parts[:, side, r, 1, :],
                                            ALU.subtract).then_inc(parts_ready[l], 1)
                    dve.wait_ge(parts_ready[l], m + 1)
                    m += 1

                def maxima(g, c):
                    dve.wait_ge(a_ps[l], NA * g + c + 1)
                    i, j0, n = A_CHUNKS[c]
                    if c == 0 and g >= 2:
                        dve.wait_ge(m_ready[l], g - 1)
                    nc.vector.tensor_reduce(mx[:, g % 2, :].rearrange("p (j i) -> p j i", j=HG)[:, j0:j0 + n, i], a_view(c), AX.X,
                                            ALU.max).then_inc(a_max[l], 1)

                def split_maxima(g):
                    dve.wait_ge(a_max[l], NA * (g + 1))
                    link(nc.vector.tensor_scalar(mneg[:, g % 2, 0:16], mx[:, g % 2, :], -1.0, None, ALU.mult))
                    nc.vector.scalar_tensor_tensor(mneg[:, g % 2, 16:32], mx[:, g % 2, :], -1.0, mneg[:, g % 2, 0:16],
                                                   ALU.mult, ALU.subtract).then_inc(m_ready[l], 1)

                def move_maxima(g):
                    dve.wait_ge(m_tr[l], g + 1)
                    if g >= 2:
                        dve.wait_ge(m_rows[l][g % 2], 32 * (g // 2))
                    nc.vector.tensor_copy(mT[:, g % 2, :], ps[7][0:32, 0:P // 2].bitcast(BF16)).then_inc(mT_ready[l], 1)

                def context(g):
                    dve.wait_ge(c_tr[l], g + 1)
                    view = ps[7].rearrange("p (t j c) -> p t j c", t=TB, j=HG)
                    rd = rden[:, g % 2, :].rearrange("p (t j) -> p t j", t=TB)
                    link(nc.vector.reciprocal(rd, view[:, :, :, HD]))
                    b, hg = g // 4, g % 4
                    nc.vector.tensor_tensor(
                        tok[:, b * TB:(b + 1) * TB, hg * 64:(hg + 1) * 64].rearrange("p t (j d) -> p t j d", j=HG),
                        view[:, :, :, 0:HD], rd.unsqueeze(3).broadcast_to([P, TB, HG, HD]),
                        ALU.mult).then_inc(ctx_ready[l], 1)

                for s in range(NG + 2):
                    if s < NG:
                        maxima(s, 0)
                        maxima(s, 1)
                    if 0 <= s - 1 < NG:
                        move_maxima(s - 1)
                    if s < NG:
                        maxima(s, 2)
                    if 0 <= s - 2 < NG:
                        context(s - 2)
                    if s < NG:
                        for c in range(3, NA):
                            maxima(s, c)
                        split_maxima(s)

                dve.wait_ge(ld_bias[l], 16)
                bf = bfull[0:EXPERTS[l], 0:BROW[l]]
                bp = [bparts[0:EXPERTS[l], r, 0:BROW[l]] for r in range(3)]
                link(nc.vector.tensor_copy(bp[0], bf))
                link(nc.vector.tensor_tensor(bf, bf, bp[0], ALU.subtract))
                link(nc.vector.tensor_copy(bp[1], bf))
                nc.vector.tensor_tensor(bp[2], bf, bp[1], ALU.subtract).then_inc(bparts_ready[l], 1)

                for m in range(NT // 2):
                    b = m // 2
                    dve.wait_ge(wo_ps[l], m + 1)
                    src = ps[m].rearrange("p (t c) -> p t c", t=2)
                    ga = modbc[:, b, 0, :].unsqueeze(1).broadcast_to([P, 2, D])
                    if l == 1:
                        link(nc.vector.tensor_tensor(tmp[:, :, :], src, rows[:, 1, :].unsqueeze(1).broadcast_to([P, 2, D]), ALU.add))
                        src = tmp[:, :, :]
                    link(nc.vector.tensor_tensor(tmp[:, :, :], src, ga, ALU.mult))
                    link(nc.vector.tensor_tensor(x[:, 2 * m:2 * m + 2, :], x[:, 2 * m:2 * m + 2, :], tmp[:, :, :], ALU.add))

                for b in range(B):
                    dve.wait_ge(tr_ps[l][1], KD * (b + 1))
                    normalise(l, 1, b)
                    rng = slice(b * TB, (b + 1) * TB)
                    wide = [P, TB, D]
                    link(nc.vector.tensor_tensor(tok[:, rng, :], tok[:, rng, :],
                                                 modbc[:, b, 2, :].unsqueeze(1).broadcast_to(wide), ALU.mult))
                    link(nc.vector.tensor_tensor(tok[:, rng, :], tok[:, rng, :],
                                                 modbc[:, b, 1, :].unsqueeze(1).broadcast_to(wide), ALU.add))
                    if l == 1:
                        t4 = xt
                        link(nc.vector.tensor_tensor(t4, tok[:, rng, :],
                                                     modbc[:, b, 3, :].unsqueeze(1).broadcast_to(wide), ALU.mult))
                        link(nc.vector.tensor_tensor(x[:, rng, :], x[:, rng, :], t4, ALU.add))
                        for t in range(b * TB, (b + 1) * TB):
                            link(nc.vector.tensor_tensor_reduce(tmp[:, 0, :], tok[:, t, :], tok[:, t, :], 1.0, 0.0,
                                                                ALU.mult, ALU.add, sumsq[:, t:t + 1]))
                        nc.vector.tensor_scalar(vareps[:, rng], sumsq[:, rng], 1.0 / D, EPS, ALU.mult,
                                                ALU.add).then_inc(rms_in, 1)
                        dve.wait_ge(rms_out, b + 1)
                        for t in range(b * TB, (b + 1) * TB):
                            link(nc.vector.scalar_tensor_tensor(tok[:, t, :], tok[:, t, :], rstd[:, t:t + 1],
                                                                rows[:, 2, :], ALU.mult, ALU.mult))
                    dve.sem_inc(tok_ready[l], 1)

                E, K = EXPERTS[l], TOPK[l]
                dve.wait_ge(gate_ps[l], 1)
                lg = logit[:, :, 0:E]
                if l == 0:
                    dve.wait_ge(ld_small, 64)
                src = ps[6][:, 0:NT * 16].rearrange("p (t e) -> p t e", t=NT)[:, :, 0:E]
                link(nc.vector.tensor_tensor(lg, src, gbias[:, l, 0:E].unsqueeze(1).broadcast_to([P, NT, E]), ALU.add))
                if l == 0:
                    link(nc.vector.tensor_tensor(lg, lg, gbias[:, 2, 0:E].unsqueeze(1).broadcast_to([P, NT, E]), ALU.add))
                for t in range(NT):
                    link(nc.vector.max(top8[:, t, :], logit[:, t, 0:E]))
                    link(nc.vector.max_index(idx8[:, t, :], top8[:, t, :], logit[:, t, 0:E]))
                link(nc.vector.tensor_copy(idf[:, :, 0:K], idx8[:, :, 0:K]))
                oh = onehot[:, 0:NT * K * E].rearrange("p (t k e) -> p t k e", t=NT, k=K)
                link(nc.vector.tensor_tensor(
                    oh, idf[:, :, 0:K].unsqueeze(3).broadcast_to([P, NT, K, E]),
                    iota_e[:, 0:E].unsqueeze(1).unsqueeze(1).broadcast_to([P, NT, K, E]), ALU.is_equal))
                ch = chosen[:, 0:NT * E].rearrange("p (t e) -> p t e", t=NT)
                with nc.allow_low_precision(reason="zeros and ones"):
                    nc.vector.tensor_reduce(ch, oh.rearrange("p t k e -> p t e k"), AX.X, ALU.add).then_inc(chosen_ready[l], 1)
                gk = gexp[:, :, 0:K]
                nc.vector.tensor_tensor(gk, top8[:, :, 0:K], top8[:, :, 0:1].broadcast_to([P, NT, K]),
                                        ALU.subtract).then_inc(gexp_in[l], 1)
                dve.wait_ge(gexp_done[l], 1)
                link(nc.vector.tensor_reduce(gsum[:, :], gk, AX.X, ALU.add))
                link(nc.vector.reciprocal(grec[:, :], gsum[:, :]))
                link(nc.vector.tensor_tensor(gate[:, :, 0:K], gk, grec[:, :].unsqueeze(2).broadcast_to([P, NT, K]), ALU.mult))
                dve.wait_ge(rank_ps[l], 1)
                pk = picked[:, 0:E * 8].rearrange("p (e c) -> p e c", e=E)
                link(nc.vector.tensor_tensor(pk, ps[5][:, 0:E].unsqueeze(2).broadcast_to([P, E, 8]),
                                             c128.unsqueeze(1).broadcast_to([P, E, 8]), ALU.is_gt))
                link(nc.vector.tensor_reduce(ntile[:, 0:E], pk, AX.X, ALU.add))
                pk = picked[:, 0:E * E].rearrange("p (a b) -> p a b", a=E)
                link(nc.vector.tensor_tensor(pk, ntile[:, 0:E].unsqueeze(1).broadcast_to([P, E, E]), lower[:, 0:E, 0:E], ALU.mult))
                link(nc.vector.tensor_reduce(excl[:, 0:E], pk, AX.X, ALU.add))
                link(nc.vector.tensor_tensor(incl[:, 0:E], excl[:, 0:E], ntile[:, 0:E], ALU.add))
                sl = slot[:, 0:NT * E].rearrange("p (t e) -> p t e", t=NT)
                link(nc.vector.scalar_tensor_tensor(
                    sl, excl[:, 0:E].unsqueeze(1).broadcast_to([P, NT, E]), float(P),
                    ps[7][:, 0:NT * E].rearrange("p (t e) -> p t e", t=NT), ALU.mult, ALU.add))
                pk = picked[:, 0:NT * K * E].rearrange("p (t k e) -> p t k e", t=NT, k=K)
                link(nc.vector.tensor_tensor(pk, oh, sl.unsqueeze(2).broadcast_to([P, NT, K, E]), ALU.mult))
                link(nc.vector.tensor_reduce(slotf[:, 0:NT * K], pk.rearrange("p t k e -> p (t k) e"), AX.X, ALU.add))
                link(nc.vector.tensor_copy(slotk[:, 0:NT * K], slotf[:, 0:NT * K]))
                n = SLOTS_T[l]
                pk = picked[0:1, 0:n * E].rearrange("p (t e) -> p t e", t=n) 
                link(nc.vector.tensor_tensor(pk, iota_t[:, 0:n].unsqueeze(2).broadcast_to([1, n, E]),
                                             incl[0:1, 0:E].unsqueeze(1).broadcast_to([1, n, E]), ALU.is_ge))
                link(nc.vector.tensor_reduce(tef[:, 0:n], pk, AX.X, ALU.add))
                link(nc.vector.tensor_scalar(tef[:, 0:n], tef[:, 0:n], float(E - 1), None, ALU.min))
                nc.vector.tensor_copy(te[:, 0:n], tef[:, 0:n]).then_inc(slots_ready[l], 1)

                def dve_x(ii, off):
                    i, _, _ = tile_at(ii, off)
                    dve.wait_ge(xT_ps[l], i + 1)
                    if not (isinstance(i, int) and i < 2):
                        dve.wait_ge(h_ps[l], i - 1)
                    nc.vector.tensor_copy(xtT[:, off % 2, :, :].rearrange("p k c -> p (k c)"),
                                          ps[off % 2][:, 0:D]).then_inc(xT_sb[l], 1)

                def dve_hT(ii, off):
                    i, _, _ = tile_at(ii, off)
                    dve.wait_ge(hT_ps[l], i + 1)
                    if not (isinstance(i, int) and i < 2):
                        dve.wait_ge(y_ps[l], i - 1)
                    nc.vector.tensor_copy(hidT[0:HK[0], off % 2, :, :].rearrange("p k c -> p (k c)"),
                                          ps[4 + off % 2][0:HK[0], 0:D]).then_inc(hT_sb[l], 1)

                def dve_gate(ii, off):
                    i, _, _ = tile_at(ii, off)
                    r = off % 2
                    early = isinstance(i, int) and i < 2
                    dve.wait_ge(h_ps[l], i + 1)
                    if not early:
                        dve.wait_ge(hid_ready[l], i - 1)
                        dve.wait_ge(hT_ps[l], i - 1)
                    nc.vector.tensor_scalar(ga_[:, r, :], ps[2 + r][:, 0:HALF], LIMIT, None, ALU.min).then_inc(sig_in, 1)
                    nc.vector.tensor_scalar(gb_[:, r, :], ps[2 + r][:, HALF:2 * HALF], LIMIT, -LIMIT, ALU.min,
                                            ALU.max).then_inc(h_read, 1)
                    dve.wait_ge(h_read, i + 1)
                    nc.vector.scalar_tensor_tensor(gu_[:, r, :], gb_[:, r, :], 1.0, ga_[:, r, :], ALU.add,
                                                   ALU.mult).then_inc(gu_done, 1)
                    dve.wait_ge(gu_done, i + 1)
                    dve.wait_ge(sig_done, i + 1)
                    nc.vector.tensor_tensor(hid[:, r, :], gu_[:, r, :], gs_[:, r, :], ALU.mult).then_inc(hid_ready[l], 1)

                def dve_step(ii, off):
                    n = SLOTS_T[l]
                    known = isinstance(ii, int)
                    if l == 0:
                        if not known or off < n:
                            dve_x(ii, off)
                        if not known or 0 <= off - 2 < n:
                            dve_hT(ii, off - 2)
                    elif not known or 0 <= off - 1 < n:
                        dve_gate(ii, off - 1)

                for s in range(STEADY):
                    dve_step(0, s)
                with dve.Fori(0, (SLOTS_T[l] - STEADY) // UNROLL) as ii:
                    for q in range(UNROLL):
                        dve_step(ii, STEADY + q)
                for s in range(SLOTS_T[l], SLOTS_T[l] + 3):
                    dve_step(0, s)

                if l == 0:
                    spread_silu(1)
                for t in range(NT):
                    for k in range(K):
                        n = t * K + k
                        dve.wait_ge(gathered[n % 4], 16 * (l * NT * TOPK[0] // 4 + n // 4 + 1))
                        if n:
                            dve.wait_ge(y_added[l], n)
                        if k == 0:
                            ins = nc.vector.tensor_scalar(tmp[:, 0, :], yg[:, n % 4, :], gate[:, t, 0:1], None, ALU.mult)
                        else:
                            ins = nc.vector.scalar_tensor_tensor(tmp[:, 0, :], yg[:, n % 4, :], gate[:, t, k:k + 1],
                                                                 tmp[:, 0, :], ALU.mult, ALU.add)
                        ins.then_inc(y_added[l], 1)
                    dve.wait_ge(y_added[l], (t + 1) * K)
                    link(nc.vector.tensor_tensor(tmp[:, 0, :], tmp[:, 0, :], modbc[:, t // TB, 3, :], ALU.mult))
                    nc.vector.tensor_tensor(x[:, t, :], x[:, t, :], tmp[:, 0, :], ALU.add).then_inc(x_new[l], 1)
                    dve.wait_ge(x_new[l], t + 1)

        @block.tensor
        def _(pe):
            def modulation(l):
                pe.wait_ge(ld_mod[l], 16)
                pe.wait_ge(silb_done[l], 1)
                for c in range(4):
                    for k in range(KD):
                        nc.tensor.matmul(ps[7][:, 2 * c:2 * c + 2], wmod[:, k, c * P:(c + 1) * P], silc[:, l, k, :],
                                         start=(k == 0), stop=(k == KD - 1))
                for b in range(B):
                    for h in range(2):
                        for k in range(KD):
                            last = nc.tensor.matmul(ps[2 * b + h], silb[:, k, b, :],
                                                    wmod[:, k, (h + 1) * 512:(h + 2) * 512],
                                                    start=(k == 0), stop=(k == KD - 1))
                last.then_inc(mod_ps[l], 1)

            def turn(l, which, ready, count):
                for b in range(B):
                    pe.wait_ge(ready, count * (b + 1))
                    for k in range(KD):
                        n = KD * b + k
                        if n >= 2:
                            pe.wait_ge(feat_ready[l][which], n - 1)
                        for i in range(TB):
                            last = nc.tensor.transpose(ps[4 + n % 2][:, i * P:(i + 1) * P],
                                                       tok[:, b * TB + i, k * P:(k + 1) * P], ident)
                        last.then_inc(tr_ps[l][which], 1)

            pe.wait_ge(ld_const, 48)
            for l in range(2):
                modulation(l)
                turn(l, 0, xhat_ready[l][0], TB)
                pe.wait_ge(ld_wqkv[l], 16)
                pe.wait_ge(mod_sb[l], 1 + B)
                for n, (kind, b, u) in enumerate(FILLS):
                    if n >= 4:
                        wait_fill_read(pe, l, n - 4)
                    pe.wait_ge(feat_ready[l][0], KD * (b + 1))
                    if kind == "v":
                        for half_t in range(2):
                            t = b * TB + 2 * u + half_t
                            for k in range(KD):
                                last = nc.tensor.matmul(ps[n % 4][:, half_t * D:(half_t + 1) * D],
                                                        feat[:, k, t * P:(t + 1) * P], wqkv[:, k, 2 * D:3 * D],
                                                        start=(k == 0), stop=(k == KD - 1))
                    else:
                        lo = (0 if kind == "q" else D) + u * P
                        for k in range(KD):
                            last = nc.tensor.matmul(ps[n % 4], wqkv[:, k, lo:lo + P], feat[:, k, b * S:(b + 1) * S],
                                                    start=(k == 0), stop=(k == KD - 1))
                    last.then_inc(qkv_ps[l], 1)
                for n in range(8, len(FILLS)):
                    wait_fill_read(pe, l, n)

                def scores_by_query(g, c):
                    i, j0, heads = A_CHUNKS[c]
                    u = g // 2
                    pe.wait_ge(spread[u], 16 * 2 * TERMS * (l + 1))
                    if NA * g + c >= 2:
                        pe.wait_ge(a_max[l], NA * g + c - 1)
                    w = (i + 1) * P
                    dst = a_view(c)
                    for j in range(heads):
                        hl = (g % 2) * HG + j0 + j
                        nc.tensor.matmul(dst[:, j, :], qr[0:SROWS, u % 2, hl, i * P:(i + 1) * P],
                                         kr[0:SROWS, u % 2, hl, 0:w], start=True, stop=False)
                        last = nc.tensor.matmul(dst[:, j, w - P:w], ident_b, causal_b, start=False, stop=True)
                    last.then_inc(a_ps[l], 1)

                def scores_by_key(g, c):
                    u = g // 2
                    n = NB * g + c
                    if c == 0:
                        pe.wait_ge(m_rows[l][g % 2], 32 * (g // 2 + 1))
                    if n >= 2:
                        pe.wait_ge(b_exp[l], n - 1)
                    for j, k, col in B_CHUNKS[c]:
                        hl = (g % 2) * HG + j
                        nc.tensor.matmul(ps[4 + c % 2][:, col:col + S - k * P],
                                         kr[0:MROWS, u % 2, hl, k * P:(k + 1) * P],
                                         qr[0:MROWS, u % 2, hl, k * P:S], start=True, stop=False)
                        last = nc.tensor.matmul(ps[4 + c % 2][:, col:col + P], causal_b, ident_b,
                                                start=False, stop=True)
                    last.then_inc(b_ps[l], 1)

                def turn_maxima(g):
                    pe.wait_ge(m_ready[l], g + 1)
                    if g >= 2:
                        pe.wait_ge(ctx_ready[l], g - 1)
                    nc.tensor.transpose(ps[7][0:32, 0:P // 2].bitcast(BF16), mneg[:, g % 2, :], ident_b).then_inc(m_tr[l], 1)

                def weigh_values(g):
                    b, hg = g // 4, g % 4
                    pe.wait_ge(b_exp[l], NB * (g + 1))
                    if g >= 1:
                        pe.wait_ge(ctxden_ready[l], g)
                    for k in range(TB):
                        for j in range(HG):
                            last = nc.tensor.matmul(ps[6][32 * j:32 * j + 32, k * P:S],
                                                    vaug[:, b * TB + k, hg * HG + j, :],
                                                    pt[:, g % 2, j, PK[k]:PK[k] + S - k * P],
                                                    start=(k == 0), stop=(k == TB - 1))
                    last.then_inc(pv_ps[l], 1)

                def turn_context(g):
                    pe.wait_ge(ctxden_ready[l], g + 1)
                    if g + 1 < NG:
                        pe.wait_ge(mT_ready[l], g + 2)
                    else:
                        pe.wait_ge(ctx_ready[l], g)
                    for i in range(TB):
                        last = nc.tensor.transpose(ps[7][:, i * P:(i + 1) * P], ctxden[:, g % 2, i * P:(i + 1) * P], ident)
                    last.then_inc(c_tr[l], 1)

                for s in range(NG + 2):
                    if s < NG:
                        scores_by_query(s, 0)
                        scores_by_query(s, 1)
                    if 0 <= s - 1 < NG:
                        turn_maxima(s - 1)
                    if 0 <= s - 2 < NG:
                        weigh_values(s - 2)
                    if s < NG:
                        scores_by_query(s, 2)
                    if 0 <= s - 2 < NG:
                        turn_context(s - 2)
                    for c in range(NB):
                        if 0 <= s - 1 < NG:
                            scores_by_key(s - 1, c)
                        if s < NG and c in (1, 4, 7):
                            scores_by_query(s, 3 + c // 3)

                turn(l, 1, ctx_ready[l], NG // B)
                pe.wait_ge(ld_wo[l], 16)
                for m in range(NT // 2):
                    pe.wait_ge(feat_ready[l][1], KD * (m // 2 + 1))
                    for half_t in range(2):
                        t = 2 * m + half_t
                        for k in range(KD):
                            last = nc.tensor.matmul(ps[m][:, half_t * D:(half_t + 1) * D], feat[:, k, t * P:(t + 1) * P],
                                                    wo[:, k, :], start=(k == 0), stop=(k == KD - 1))
                    last.then_inc(wo_ps[l], 1)

                E, K = EXPERTS[l], TOPK[l]
                turn(l, 2, tok_ready[l], 1)
                pe.wait_ge(ld_small, 64)
                for t in range(NT):
                    pe.wait_ge(feat_ready[l][2], KD * (t // TB + 1))
                    for k in range(KD):
                        last = nc.tensor.matmul(ps[6][:, t * 16:t * 16 + E], feat[:, k, t * P:(t + 1) * P],
                                                gw[:, l, k, 0:E], start=(k == 0), stop=(k == KD - 1))
                last.then_inc(gate_ps[l], 1)
                pe.wait_ge(chosen_ready[l], 1)
                nc.tensor.matmul(ps[7][:, 0:NT * E], before_b, chosen[:, 0:NT * E], start=True, stop=False)
                for t in range(NT - 1):
                    m = NT - 1 - t
                    nc.tensor.matmul(ps[7][:, (t + 1) * E:NT * E].rearrange("p (m e) -> p m e", m=m), ones_b[:, :],
                                     chosen[:, t * E:(t + 1) * E].unsqueeze(1).broadcast_to([P, m, E]),
                                     start=False, stop=(t == NT - 2))
                for t in range(NT):
                    last = nc.tensor.matmul(ps[5][:, 0:E], ones_b[:, :], chosen[:, t * E:(t + 1) * E],
                                            start=(t == 0), stop=(t == NT - 1))
                last.then_inc(rank_ps[l], 1)

                h_free = hid_ready[l] if l == 0 else h_read

                def pe_x(ii, off):
                    i, r, rnd = tile_at(ii, off)
                    pe.wait_ge(xt_loaded[r], LOADS_BEFORE[l][r] + 16 * rnd + 16)
                    if not (isinstance(i, int) and i < 2):
                        pe.wait_ge(xT_sb[l], i - 1)
                    for k in range(KD):
                        last = nc.tensor.transpose(ps[off % 2][:, k * P:(k + 1) * P], xt[:, r, k * P:(k + 1) * P], ident)
                    last.then_inc(xT_ps[l], 1)

                def expert_of(i):
                    return pe.value_load(te[0:1, bass.ds(i, 1)], min_val=0, max_val=E - 1)

                def pe_h(ii, off):
                    i, _, _ = tile_at(ii, off)
                    e = expert_of(i)
                    dst = ps[2 + off % 2][:, 0:HB[l]]
                    if not (isinstance(i, int) and i < 2):
                        pe.wait_ge(h_free, i - 1)
                    nc.tensor.matmul(dst, ones_b[0:3, :], moe_bias(l, 0, HB[l], e), start=True, stop=False)
                    pe.wait_ge(xT_sb[l], i + 1)
                    for k in range(KD):
                        last = nc.tensor.matmul(dst, xtT[:, off % 2, k, :], moe_w1(l, k, e), start=False, stop=(k == KD - 1))
                    last.then_inc(h_ps[l], 1)

                def pe_hT(ii, off):
                    i, _, _ = tile_at(ii, off)
                    pe.wait_ge(hid_ready[l], i + 1)
                    if not (isinstance(i, int) and i < 2):
                        pe.wait_ge(hT_sb[l], i - 1)
                    for k in range(2):
                        last = nc.tensor.transpose(ps[4 + off % 2][0:HK[l], k * P:(k + 1) * P],
                                                   hid[:, off % 2, k * HK[l]:(k + 1) * HK[l]], ident)
                    last.then_inc(hT_ps[l], 1)

                def pe_y(ii, off):
                    i, _, _ = tile_at(ii, off)
                    e = expert_of(i)
                    dst = ps[6 + off % 2][:, 0:D]
                    if not (isinstance(i, int) and i < 2):
                        pe.wait_ge(y_sb[l], i - 1)
                    nc.tensor.matmul(dst, ones_b[0:3, :], moe_bias(l, HB[l], BROW[l], e), start=True, stop=False)
                    pe.wait_ge(hT_sb[l], i + 1)
                    for k in range(2):
                        last = nc.tensor.matmul(dst, hidT[0:HK[l], off % 2, k, :], moe_w2(l, k, e), start=False, stop=(k == 1))
                    last.then_inc(y_ps[l], 1)

                def pe_step(ii, off):
                    n = SLOTS_T[l]
                    known = isinstance(ii, int)
                    if not known or off < n:
                        pe_x(ii, off)
                    if not known or 0 <= off - 1 < n:
                        pe_h(ii, off - 1)
                    if not known or 0 <= off - 2 < n:
                        pe_hT(ii, off - 2)
                    if not known or 0 <= off - 3 < n:
                        pe_y(ii, off - 3)

                pe.wait_ge(slots_ready[l], 1)
                pe.wait_ge(brows_ready[l], 48)
                pe.wait_ge(ld_w_lo[l], 16)
                if l == 1:
                    pe.wait_ge(ld_w_hi, 16)
                for s in range(STEADY):
                    pe_step(0, s)
                with pe.Fori(0, (SLOTS_T[l] - STEADY) // UNROLL) as ii:
                    for q in range(UNROLL):
                        pe_step(ii, STEADY + q)
                for s in range(SLOTS_T[l], SLOTS_T[l] + 3):
                    pe_step(0, s)


def _by_k(w, np):
    n, k = w.shape
    return np.ascontiguousarray(w.T.reshape(k // P, P, n).transpose(1, 0, 2))


def _mixture(w1, w2, l, np):
    e, h, d = w1.shape
    if l == 1:
        w1 = np.concatenate([w1[:, 0::2], w1[:, 1::2]], 1)
    a = np.zeros((e, HB[l], d), w1.dtype)
    a[:, :h] = w1
    a = a.transpose(2, 0, 1).reshape(KD, P, e, HB[l]).transpose(1, 2, 0, 3).reshape(P, e, KD * HB[l])
    rows = np.zeros((e, 2 * HK[l], d), w2.dtype)
    rows[:, :w2.shape[2]] = w2.transpose(0, 2, 1)
    rows = rows.reshape(e, 2, HK[l], d).transpose(2, 0, 1, 3).reshape(HK[l], e, 2 * d)
    b = np.zeros((P, e, 2 * d), w2.dtype)
    b[:HK[l]] = rows
    return np.ascontiguousarray(np.concatenate([a, b], 2).reshape(P, -1))


def _biases(b1, b2, l, np):
    e, h = b1.shape
    if l == 1:
        b1 = np.concatenate([b1[:, 0::2], b1[:, 1::2]], 1)
    out = np.zeros((e, BROW[l]), b1.dtype)
    out[:, :h] = b1
    out[:, HB[l]:] = b2
    return out


def kernel(**inputs):
    import numpy as np
    import concourse.bacc as bacc
    from concourse.bass_utils import run_bass_kernel_spmd

    a = {k: np.asarray(v) for k, v in inputs.items()}

    def spread_rows(v):
        return np.broadcast_to(v, (P,) + v.shape)

    consts = np.zeros((P, CONST_W), np.float32)
    consts[:, 0:P] = np.eye(P)
    consts[:, P:P + 16] = np.arange(16)
    consts[:, P + 16:P + 24] = np.arange(8) * P
    consts[:, P + 24:P + 280] = np.tril(np.ones((16, 16)), -1).reshape(-1)
    consts[:, P + 280:P + 328] = np.arange(48)
    row, col = np.arange(P)[:, None], np.arange(P)[None, :]
    constb = np.concatenate([np.eye(P), np.where(col > row, BIG_NEG, 0.0), row < col], 1).astype(np.float32)

    def pad16(v):
        return np.concatenate([v, np.zeros(16 - len(v), v.dtype)])

    gws = []
    for name in ("L0_ffn_gate_w", "L1_ffn_gate_w"):
        w = a[name]
        w = np.concatenate([w, np.zeros((16 - len(w), D), w.dtype)], 0)
        gws.append(_by_k(w, np))
    def by_dim(w):
        return w.reshape(2, 8, HD, -1).transpose(0, 2, 1, 3).reshape(w.shape)

    arrays = {
        "x": a["L0_attn_x"].reshape(T, D),
        "consts": consts,
        "constb": constb,
        "cT": np.stack([a[f"L{l}_c"].T.reshape(KD, P, B).transpose(1, 0, 2) for l in range(2)], 1).reshape(P, 2 * KD * B),
        "wmod": np.stack([a[f"L{l}_wmod"].reshape(KD, P, 6 * D).transpose(1, 0, 2) for l in range(2)]),
        "wqkv": np.stack([
            _by_k(np.concatenate([by_dim(a["L0_attn_Wq"]), by_dim(a["L0_attn_Wk"]), a["L0_attn_Wv"]], 0), np),
            _by_k(np.concatenate([by_dim(a["L1_attn_wq"]), by_dim(a["L1_attn_wk"]), a["L1_attn_wv"]], 0), np)]),
        "wo": np.stack([_by_k(a["L0_attn_Wo"], np), _by_k(a["L1_attn_wo"], np)]),
        "rows": spread_rows(np.stack([a["L1_attn_bv"], a["L1_attn_bo"], a["L1_ffn_norm_w"]])),
        "qkb": np.concatenate([by_dim(a["L1_attn_bq"]).reshape(KD, P).T, by_dim(a["L1_attn_bk"]).reshape(KD, P).T], 1),
        "gbias": spread_rows(np.stack([pad16(a["L0_ffn_gate_b"]), pad16(a["L1_ffn_gate_b"]), pad16(a["L0_ffn_bias"])])),
        "gw": np.stack(gws, 1),
        "moe0": _mixture(a["L0_ffn_w1"], a["L0_ffn_w2"], 0, np),
        "moe1": _mixture(a["L1_ffn_w1"], a["L1_ffn_w2"], 1, np),
        "bias0": _biases(a["L0_ffn_b1"], a["L0_ffn_b2"], 0, np),
        "bias1": _biases(a["L1_ffn_b1"], a["L1_ffn_b2"], 1, np),
    }
    nc = bacc.Bacc("TRN2", target_bir_lowering=False, num_devices=1)
    arrays = {f"in_{k}_dram": np.ascontiguousarray(v) for k, v in arrays.items()}
    dram = {k[3:-5]: nc.dram_tensor(k, v.shape, mybir.dt.from_np(v.dtype), kind="ExternalInput").ap()
            for k, v in arrays.items()}
    out = nc.dram_tensor("out_dram", (T, D), F32, kind="ExternalOutput").ap()
    build_kernel(nc, dram, out)
    r = run_bass_kernel_spmd(nc, [arrays], core_ids=[0])
    return r.results[0]["out_dram"].reshape(B, S, D)
```

```python
from contextlib import ExitStack

import concourse.bass as bass
from concourse import mybir

P = 128
D = 256
KD = D // P
B = 2
S = 512
T = B * S
NT = T // P
TB = S // P
H = 16
HD = D // H
HG = 4
NG = B * H // HG
TERMS = 6
QSIDE = [0, 0, 1, 0, 2, 1]
KSIDE = [0, 1, 0, 2, 0, 1]
SROWS = TERMS * HD
MROWS = SROWS + 2
EPS = 1e-5
LN_CLAMP = 0.25
PK = [0, 512, 1024, 896]
PTW = 1280
BIG_NEG = -1e30

F32 = mybir.dt.float32
BF16 = mybir.dt.bfloat16
I32 = mybir.dt.int32
U32 = mybir.dt.uint32
ALU = mybir.AluOpType
ACT = mybir.ActivationFunctionType
AX = mybir.AxisListType

EXPERTS = [8, 16]
TOPK = [2, 4]
HB = [192, 512]
HK = [96, 128]
HALF = 256
ALPHA = 1.702
LIMIT = 7.0
SLOTS_T = [(T * k - e) // P + e for e, k in zip(EXPERTS, TOPK)]
WROW = [2 * HB[l] + 2 * D for l in range(2)]
BROW = [HB[l] + D for l in range(2)]
UNROLL = 4
STEADY = 7
LAG = 7
POOL_STEADY = 11
TILES_BEFORE = [[16 * sum(len(range(r, n, 4)) for n in SLOTS_T[:l]) for r in range(4)] for l in range(3)]
TILES_TO = [0, SLOTS_T[0]]
CONST_W = P + 16 + 8 + 256 + 48 + P + NT + 1
MT = 48
BIG_W = 16 * WROW[1]


def build_kernel(nc, dram, out):
    with ExitStack() as ctx:
        def sb(name, shape, dt=F32):
            return ctx.enter_context(nc.sbuf_tensor(name, shape, dt))

        def sem(name):
            return ctx.enter_context(nc.semaphore(name))

        def sems(name, n=2):
            return [sem(f"{name}{i}") for i in range(n)]

        x = sb("x", [P, NT, D])
        big = sb("big", [P, BIG_W])
        ptm = sb("ptm", [P, 2 * HG * PTW])
        tok = sb("tok", [P, NT, D])
        feat = sb("feat", [P, KD, T])
        modbc = sb("modbc", [P, B, 4, D])
        parts = sb("parts", [P, 2, 2, 3, S], BF16)
        tok_flat = tok[:, :, :].rearrange("p t c -> p (t c)")
        qkf = tok_flat[:, 0:2 * S].rearrange("p (n t) -> p n t", n=2)
        rest = tok_flat[:, 2 * S:3 * S]
        wqkv = sb("wqkv", [P, KD, 3 * D])
        wo = sb("wo", [P, KD, D])
        ctxden = sb("ctxden", [P, 2, S])
        consts = sb("consts", [P, CONST_W])
        constb_f = ptm[:, 0:3 * P]
        constb = sb("constb", [P, 3, P], BF16)
        cT = sb("cT", [P, 2, KD, B])
        silc = sb("silc", [P, 2, KD, B])
        silb = ptm[:, 4096:4096 + KD * B * P].rearrange("p (k b n) -> p k b n", k=KD, b=B)
        modcol = sb("modcol", [P, 2, 4, B])
        rows = sb("rows", [P, 3, D])
        qkb = sb("qkb", [P, 4])
        qkb4 = sb("qkb4", [P, 4])
        gbias = sb("gbias", [P, 3, 16])
        gw = sb("gw", [P, 2, KD, 16])
        stats = sb("stats", [P, NT, 6])
        mv = sb("mv", [P, NT, 2])
        rstd = sb("rstd", [P, NT])
        vareps = sb("vareps", [P, NT])
        neghalf = sb("neghalf", [P, NT])
        sumsq = sb("sumsq", [P, NT])
        mx = sb("mx", [P, 2, 16])
        mneg = sb("mneg", [P, 2, 32], BF16)
        mT = sb("mT", [32, 2, P], BF16)
        rden = sb("rden", [P, 2, 16])
        tmp = sb("tmp", [P, 2, D])
        parts_flat = parts[:, :, :, :, :].rearrange("p a b c d -> p (a b c d)")
        bfull = parts_flat[0:16, 0:2 * BROW[1]].bitcast(F32)
        bparts = parts_flat[0:16, 2 * BROW[1]:5 * BROW[1]].rearrange("p (r c) -> p r c", r=3)
        logit = sb("logit", [P, NT, 16])
        top8 = sb("top8", [P, NT, 8])
        idx8 = sb("idx8", [P, NT, 8], U32)
        idf = sb("idf", [P, NT, 4])
        feat_flat = feat[:, :, :].rearrange("p k t -> p (k t)")
        onehot = feat_flat[:, 0:NT * 4 * 16]
        picked = feat_flat[:, NT * 4 * 16:NT * 4 * 16 + 48 * 16]
        chosen = sb("chosen", [P, NT * 16], BF16)
        gate = sb("gate", [P, NT, 4])
        gexp = sb("gexp", [P, NT, 4])
        gsum = sb("gsum", [P, NT])
        grec = sb("grec", [P, NT])
        ntile = sb("ntile", [P, 16])
        excl = sb("excl", [P, 16])
        incl = sb("incl", [P, 16])
        slot = sb("slot", [P, NT * 16])
        slotf = sb("slotf", [P, NT * 4])
        place = sb("place", [P, NT * 4])
        first = sb("first", [P, NT * 4])
        slot_i = sb("slot_i", [P, NT * 4], I32)
        token_f = sb("token_f", [P, MT])
        token = sb("token", [P, MT], U32)
        weight = sb("weight", [P, MT])
        token_in = sb("token_in", [P, 4], U32)
        token_out = sb("token_out", [P, 4], U32)
        tef = sb("tef", [1, 48])
        te = sb("te", [1, 48], I32)

        half = BIG_W // 2
        qr = big[:, half:half + 4096].bitcast(BF16).rearrange("p (r h t) -> p r h t", r=2, h=8)
        kr = big[:, half + 4096:half + 8192].bitcast(BF16).rearrange("p (r h t) -> p r h t", r=2, h=8)
        vaug = big[:, half + 8192:half + 12288].rearrange("p (t h c) -> p t h c", t=NT, h=H)
        pt = ptm[:, :].rearrange("p (r j c) -> p r j c", r=2, j=HG)
        wmods = [ptm[:, 512:512 + KD * 6 * D].rearrange("p (k n) -> p k n", k=KD),
                 big[:, half:half + KD * 6 * D].rearrange("p (k n) -> p k n", k=KD)]
        zeros = sb("zeros", [P, D])
        brows = ptm[:, 0:16 * BROW[1] // 2].bitcast(BF16)
        o = 16 * BROW[1] // 2
        xt = ptm[:, o:o + 4 * D].rearrange("p (r c) -> p r c", r=4)
        o += 4 * D
        xtT = ptm[:, o:o + 2 * D].rearrange("p (r k c) -> p r k c", r=2, k=KD)
        o += 2 * D
        hid = ptm[:, o:o + 2 * D].rearrange("p (r c) -> p r c", r=2)
        o += 2 * D
        hidT = ptm[:, o:o + 2 * D].rearrange("p (r k c) -> p r k c", r=2, k=KD)
        o += 2 * D
        yt = ptm[:, o:o + 4 * D].rearrange("p (r c) -> p r c", r=4)
        o += 4 * D
        assert o <= 2 * HG * PTW
        ga_ = qkf[:, :, 0:D]
        gb_ = qkf[:, :, D:2 * D]
        gs_ = ctxden[:, :, 0:D]
        gu_ = ctxden[:, :, D:2 * D]
        at_place = ptm[:, 6144:6144 + 4096]
        at_tile = parts[:, :, :, :, :].rearrange("p a b c d -> p (a b c d)").bitcast(F32)
        acc_in = ptm[:, 0:2 * NT * D].rearrange("p (a t c) -> p a t c", a=2, t=NT)
        gb_next = ctxden[:, :, 0:D]

        ident = consts[:, 0:P]
        iota_e = consts[:, P:P + 16]
        c128 = consts[:, P + 16:P + 24]
        lower = consts[:, P + 24:P + 280].rearrange("p (a b) -> p a b", a=16)
        iota_t = consts[:, P + 280:P + 328]
        iota_p = consts[:, P + 328:2 * P + 328]
        left = consts[:, 2 * P + 328:2 * P + 328 + NT]
        lane = consts[:, 2 * P + 328 + NT:2 * P + 329 + NT]
        ident_b = constb[:, 0, :]
        causal_b = constb[:, 1, :]
        before_b = constb[:, 2, :]
        ones_b = sb("ones_b", [P, P], BF16)

        bank = [ctx.enter_context(nc.psum_tensor(f"bank{i}", [P, 1024], F32)) for i in range(2)]
        bank += [ctx.enter_context(nc.psum_tensor(f"bank{i}", [P, 512], F32)) for i in range(2, 6)]
        ps = [bank[0][:, 0:512], bank[0][:, 512:1024], bank[1][:, 0:512], bank[1][:, 512:1024]]
        ps += [bank[i][:, :] for i in range(2, 6)]

        xs = [nc.dram_tensor(f"token_rows{l}", [T + P, D], F32, kind="Internal") for l in range(2)]
        acc = [[nc.dram_tensor(f"sums{l}_{a}", [T + P, D], F32, kind="Internal") for a in range(2)] for l in range(2)]

        ld_const = sem("ld_const")
        ld_x = sems("ld_x")
        ld_mod = sems("ld_mod")
        ld_wqkv = sems("ld_wqkv")
        ld_wo = sems("ld_wo")
        ld_small = sem("ld_small")
        ld_bias = sems("ld_bias")
        ld_w_lo = sems("ld_w_lo")
        ld_w_hi = sem("ld_w_hi")
        zeroed = sem("zeroed")
        set_up = sem("set_up")
        silu_done = sem("silu_done")
        silb_done = sems("silb_done")
        mod_ps = sems("mod_ps")
        mod_sb = sems("mod_sb")
        qkb_done = sem("qkb_done")
        dve_own = sem("dve_own")
        pool_own = sem("pool_own")
        act_own = sem("act_own")
        var_ready = [sems(f"var_ready{l}_") for l in range(2)]
        rstd_ready = [sems(f"rstd_ready{l}_") for l in range(2)]
        xhat_ready = [sems(f"xhat_ready{l}_") for l in range(2)]
        tr_ps = [sems(f"tr_ps{l}_", 3) for l in range(2)]
        feat_ready = [sems(f"feat_ready{l}_", 3) for l in range(2)]
        qkv_ps = sems("qkv_ps")
        qkf_ready = sems("qkf_ready")
        v_ready = sems("v_ready")
        parts_ready = sems("parts_ready")
        spread = sems("spread", 4)
        a_ps = sems("a_ps")
        a_max = sems("a_max")
        m_ready = sems("m_ready")
        m_tr = sems("m_tr")
        mT_ready = sems("mT_ready")
        m_rows = [sems(f"m_rows{l}_") for l in range(2)]
        b_ps = sems("b_ps")
        b_exp = sems("b_exp")
        pv_ps = sems("pv_ps")
        ctxden_ready = sems("ctxden_ready")
        c_tr = sems("c_tr")
        ctx_ready = sems("ctx_ready")
        wo_ps = sems("wo_ps")
        wo_added = sems("wo_added")
        gate_ps = sems("gate_ps")
        chosen_ready = sems("chosen_ready")
        gexp_in = sems("gexp_in")
        gexp_done = sems("gexp_done")
        rank_ps = sems("rank_ps")
        slots_ready = sems("slots_ready")
        bparts_ready = sems("bparts_ready")
        brows_ready = sems("brows_ready")
        rows_stored = sems("rows_stored")
        tile_of = sems("tile_of")
        token_picked = sem("token_picked")
        sum_picked = sem("sum_picked")
        placed_ps = sems("placed_ps")
        acc_loaded = sems("acc_loaded")
        rms_in = sem("rms_in")
        rms_out = sem("rms_out")
        tok_ready = sems("tok_ready")
        xt_loaded = sems("xt_loaded", 4)
        xT_ps = sems("xT_ps")
        xT_sb = sems("xT_sb")
        h_ps = sems("h_ps")
        h_read = sem("h_read")
        sig_in = sem("sig_in")
        sig_done = sem("sig_done")
        gu_done = sem("gu_done")
        hid_ready = sems("hid_ready")
        hT_ps = sems("hT_ps")
        hT_sb = sems("hT_sb")
        y_ps = sems("y_ps")
        y_sb = sems("y_sb")
        y_summed = sems("y_summed", 4)
        x_new = sems("x_new")
        stored = sem("stored")

        def moe_w1(l, k, e):
            v = big[:, 0:EXPERTS[l] * WROW[l]].rearrange("p (e c) -> p e c", e=EXPERTS[l])
            return v[:, bass.ds(e, 1), k * HB[l]:(k + 1) * HB[l]].rearrange("p a b -> p (a b)")

        def moe_w2(l, k, e):
            v = big[:, 0:EXPERTS[l] * WROW[l]].rearrange("p (e c) -> p e c", e=EXPERTS[l])
            lo = 2 * HB[l] + k * D
            return v[0:HK[l], bass.ds(e, 1), lo:lo + D].rearrange("p a b -> p (a b)")

        def moe_bias(l, lo, hi, e):
            v = brows[0:3, 0:EXPERTS[l] * BROW[l]].rearrange("p (e c) -> p e c", e=EXPERTS[l])
            return v[:, bass.ds(e, 1), lo:hi].rearrange("p a b -> p (a b)")

        A_CHUNKS = [(0, 0, 4), (1, 0, 4), (2, 0, 2), (2, 2, 2), (3, 0, 2), (3, 2, 2)]
        NA = len(A_CHUNKS)
        B_CHUNKS = []
        for j0 in (0, 2):
            B_CHUNKS += [[(j0, 0, 0)], [(j0, 1, 0), (j0, 3, 384)], [(j0 + 1, 0, 0)],
                         [(j0 + 1, 1, 0), (j0 + 1, 3, 384)], [(j0, 2, 0), (j0 + 1, 2, 256)]]
        NB = len(B_CHUNKS)

        def a_view(c):
            i, _, n = A_CHUNKS[c]
            w = (i + 1) * P
            full = bank[c % 2][:, :]
            if n == 4:
                return full[:, 0:4 * w].rearrange("p (j w) -> p j w", j=4)
            return full.rearrange("p (j w) -> p j w", j=2)[:, :, 0:w]


        def tile_at(ii, off):
            return 4 * ii + off, off % 4, ii + off // 4

        def qkv_fills():
            for b in range(B):
                yield from (("q", b, 0), ("k", b, 0), ("v", b, 0), ("v", b, 1), ("q", b, 1), ("k", b, 1))

        FILLS = list(qkv_fills())

        def wait_fill_read(eng, l, n):
            kind = FILLS[n][0]
            before = [f[0] == "v" for f in FILLS[:n + 1]]
            if kind == "v":
                eng.wait_ge(v_ready[l], sum(before))
            else:
                eng.wait_ge(qkf_ready[l], len(before) - sum(before))

        def spread_unit(eng, issue, l, u):
            eng.wait_ge(parts_ready[l], 2 * (u + 1))
            if u >= 2:
                eng.wait_ge(b_ps[l], NB * 2 * (u - 1))
            elif l == 1:
                eng.wait_ge(b_ps[0], NB * NG)
                eng.wait_ge(mod_ps[1], 1)
            for n, (dst, side) in enumerate(((qr, QSIDE), (kr, KSIDE))):
                for r in range(TERMS):
                    issue.dma_start(dst[r * HD:(r + 1) * HD, u % 2, :, :],
                                    parts[:, n, u % 2, side[r], :]).then_inc(spread[u], 16)

        block = ctx.enter_context(nc.Block())

        @block.sync
        def _(sp):
            nc.sync.dma_start(x[:, 0:TB, :], dram["x"][0:S, :].rearrange("(t p) c -> p t c", p=P)).then_inc(ld_x[0], 16)
            nc.sync.dma_start(consts[:, :], dram["consts"]).then_inc(ld_const, 16)
            nc.sync.dma_start(constb_f, dram["constb"]).then_inc(ld_const, 16)
            nc.sync.dma_start(cT[:, :, :, :].rearrange("p l k b -> p (l k b)"), dram["cT"]).then_inc(ld_const, 16)
            nc.sync.dma_start(wmods[0], dram["wmod"][0]).then_inc(ld_mod[0], 16)
            nc.sync.dma_start(x[:, TB:NT, :], dram["x"][S:T, :].rearrange("(t p) c -> p t c", p=P)).then_inc(ld_x[1], 16)
            nc.sync.dma_start(wqkv[:, :, :], dram["wqkv"][0]).then_inc(ld_wqkv[0], 16)
            nc.sync.dma_start(wo[:, :, :], dram["wo"][0]).then_inc(ld_wo[0], 16)
            nc.sync.dma_start(rows[:, :, :], dram["rows"]).then_inc(ld_small, 16)
            nc.sync.dma_start(qkb[:, :], dram["qkb"]).then_inc(ld_small, 16)
            nc.sync.dma_start(gbias[:, :, :], dram["gbias"]).then_inc(ld_small, 16)
            nc.sync.dma_start(gw[:, :, :, :], dram["gw"]).then_inc(ld_small, 16)
            nc.sync.dma_start(big[:, 0:EXPERTS[0] * WROW[0]], dram["moe0"]).then_inc(ld_w_lo[0], 16)
            sp.wait_ge(set_up, 1)
            for l in range(2):
                for a in range(2):
                    nc.sync.dma_start(acc[l][a][:, :].rearrange("(t p) c -> p t c", p=P),
                                      zeros[:, :].unsqueeze(1).broadcast_to([P, NT + 1, D])).then_inc(zeroed, 16)
                nc.sync.dma_start(xs[l][T:T + P, :], zeros[:, :]).then_inc(zeroed, 16)

            def send_maxima(l, g):
                sp.wait_ge(mT_ready[l], g + 1)
                hl = (g % 2) * HG
                for r in range(2):
                    nc.sync.dma_start(
                        qr[SROWS + r:SROWS + r + 1, (g // 2) % 2, hl:hl + HG, :],
                        mT[r * 16:(r + 1) * 16, g % 2, :]).then_inc(m_rows[l][g % 2], 16)

            for l in range(2):
                spread_unit(sp, nc.sync, l, 0)
                spread_unit(sp, nc.sync, l, 1)
                if l == 1:
                    nc.sync.dma_start(big[:, 0:half], dram["moe1"][:, 0:half]).then_inc(ld_w_lo[1], 16)
                for g in range(NG):
                    send_maxima(l, g)
                for u in range(4):
                    sp.wait_ge(spread[u], 16 * 2 * TERMS * (l + 1))
                nc.sync.dma_start(bfull[0:EXPERTS[l], 0:BROW[l]], dram[f"bias{l}"]).then_inc(ld_bias[l], 16)
                if l == 1:
                    sp.wait_ge(pv_ps[1], NG)
                    nc.sync.dma_start(big[:, half:BIG_W], dram["moe1"][:, half:BIG_W]).then_inc(ld_w_hi, 16)
                else:
                    sp.wait_ge(qkv_ps[0], len(FILLS))
                    nc.sync.dma_start(wqkv[:, :, :], dram["wqkv"][1]).then_inc(ld_wqkv[1], 16)
                    sp.wait_ge(b_ps[0], NB * NG)
                    nc.sync.dma_start(wmods[1], dram["wmod"][1]).then_inc(ld_mod[1], 16)
                sp.wait_ge(bparts_ready[l], 1)
                sp.wait_ge(pv_ps[l], NG)
                for r in range(3):
                    nc.sync.dma_start(
                        brows[r:r + 1, 0:EXPERTS[l] * BROW[l]].rearrange("p (e c) -> p e c", e=EXPERTS[l]),
                        bparts[0:EXPERTS[l], r, 0:BROW[l]]).then_inc(brows_ready[l], 16)
                for b in range(B):
                    sp.wait_ge(tok_ready[l], b + 1)
                    nc.sync.dma_start(xs[l][b * S:(b + 1) * S, :].rearrange("(t p) c -> p t c", p=P),
                                      tok[:, b * TB:(b + 1) * TB, :]).then_inc(rows_stored[l], 16)
                if l == 0:
                    sp.wait_ge(wo_ps[0], NT // 2)
                    nc.sync.dma_start(wo[:, :, :], dram["wo"][1]).then_inc(ld_wo[1], 16)
                for r in range(4):
                    sp.wait_ge(y_summed[r], TILES_BEFORE[l + 1][r])
                for b in range(B):
                    for a in range(2):
                        nc.sync.dma_start(acc_in[:, a, b * TB:(b + 1) * TB, :],
                                          acc[l][a][b * S:(b + 1) * S, :].rearrange("(t p) c -> p t c", p=P)
                                          ).then_inc(acc_loaded[b], 16)
            for b in range(B):
                sp.wait_ge(x_new[1], b + 1)
                nc.sync.dma_start(out[b * S:(b + 1) * S, :].rearrange("(t p) c -> p t c", p=P),
                                  x[:, b * TB:(b + 1) * TB, :]).then_inc(stored, 16)
            sp.wait_ge(stored, 16 * B)

        @block.gpsimd
        def _(pool):
            nc.gpsimd.memset(zeros[:, :], 0.0).then_inc(set_up, 1)
            nc.gpsimd.memset(neghalf[:, :], -0.5).then_inc(pool_own, 1)
            pool.wait_ge(pool_own, 1)

            def inverse_root(l, which, b):
                pool.wait_ge(var_ready[l][which], b + 1)
                c = slice(b * TB, (b + 1) * TB)
                nc.gpsimd.tensor_tensor(rstd[:, c], vareps[:, c], neghalf[:, c], ALU.pow).then_inc(rstd_ready[l][which], 1)

            for l in range(2):
                inverse_root(l, 0, 0)
                inverse_root(l, 0, 1)
                spread_unit(pool, nc.gpsimd, l, 2)
                spread_unit(pool, nc.gpsimd, l, 3)
                for b in range(B):
                    inverse_root(l, 1, b)
                    if l == 1:
                        c = slice(b * TB, (b + 1) * TB)
                        pool.wait_ge(rms_in, b + 1)
                        nc.gpsimd.tensor_tensor(rstd[:, c], vareps[:, c], neghalf[:, c], ALU.pow).then_inc(rms_out, 1)
                def pick_in(ii, off):
                    i, r, _ = tile_at(ii, off)
                    if not (isinstance(i, int) and i < 4):
                        pool.wait_ge(xT_ps[l], i - 3)
                    nc.gpsimd.tensor_copy(token_in[:, r:r + 1], token[:, bass.ds(i, 1)]).then_inc(token_picked, 1)

                def pick_out(ii, off):
                    i, r, _ = tile_at(ii, off)
                    pool.wait_ge(y_sb[l], i + 1)
                    if not (isinstance(i, int) and i < 2):
                        _, r2, rnd2 = tile_at(ii, off - 2)
                        pool.wait_ge(y_summed[r2], TILES_BEFORE[l][r2] + 16 * rnd2 + 16)
                    nc.gpsimd.tensor_copy(token_out[:, r:r + 1], token[:, bass.ds(i, 1)]).then_inc(sum_picked, 1)

                def gather(off):
                    r = off % 4
                    nc.gpsimd.indirect_dma_start(
                        out=xt[:, r, :], out_offset=None, in_=xs[l][:, :],
                        in_offset=bass.IndirectOffsetOnAxis(ap=token_in[:, r:r + 1], axis=0)).then_inc(xt_loaded[r], 16)

                def add_rows(off):
                    r = off % 4
                    nc.gpsimd.indirect_dma_start(
                        out=acc[l][off % 2][:, :],
                        out_offset=bass.IndirectOffsetOnAxis(ap=token_out[:, r:r + 1], axis=0),
                        in_=yt[:, r, :], in_offset=None, compute_op=ALU.add).then_inc(y_summed[r], 16)

                def pool_step(ii, off):
                    n = SLOTS_T[l]
                    known = isinstance(ii, int)
                    gathers = not known or off < n
                    adds = not known or 0 <= off - LAG < n
                    i, _, _ = tile_at(ii, off)
                    if gathers:
                        pool.wait_ge(token_picked, TILES_TO[l] + l + i + 1)
                    if adds:
                        pick_out(ii, off - LAG)
                        pool.wait_ge(sum_picked, TILES_TO[l] + i - LAG + 1)
                    if not known or off + 1 < n:
                        pick_in(ii, off + 1)
                    if gathers:
                        gather(off)
                    if adds:
                        add_rows(off - LAG)

                pool.wait_ge(zeroed, 16 * 6)
                pool.wait_ge(rows_stored[l], 16 * B)
                pool.wait_ge(slots_ready[l], 1)
                pick_in(0, 0)
                for s in range(POOL_STEADY):
                    pool_step(0, s)
                with pool.Fori(0, (SLOTS_T[l] - POOL_STEADY) // UNROLL) as ii:
                    for q in range(UNROLL):
                        pool_step(ii, POOL_STEADY + q)
                for s in range(SLOTS_T[l], SLOTS_T[l] + LAG):
                    pool_step(0, s)

        @block.scalar
        def _(act):
            act.wait_ge(ld_const, 48)
            nc.scalar.activation(silc[:, :, :, :].rearrange("p l k b -> p (l k b)"),
                                 cT[:, :, :, :].rearrange("p l k b -> p (l k b)"), ACT.Silu).then_inc(silu_done, 1)

            def move_transposed(l, which):
                for b in range(B):
                    for k in range(KD):
                        n = KD * b + k
                        if which == 0:
                            act.wait_ge(mod_sb[l], 1)
                        act.wait_ge(tr_ps[l][which], n + 1)
                        dst, src = feat[:, k, b * S:(b + 1) * S], ps[4 + n % 2]
                        if which == 0:
                            nc.scalar.activation(dst, src, ACT.Identity, scale=modcol[:, l, 2 + k, b:b + 1],
                                                 bias=modcol[:, l, k, b:b + 1]).then_inc(feat_ready[l][which], 1)
                        else:
                            nc.scalar.activation(dst, src, ACT.Copy).then_inc(feat_ready[l][which], 1)

            for l in range(2):
                move_transposed(l, 0)
                m = 0
                if l == 1:
                    act.wait_ge(qkb_done, 1)
                for n, (kind, b, u) in enumerate(FILLS):
                    if kind == "v" and l == 1:
                        continue
                    act.wait_ge(qkv_ps[l], n + 1)
                    src = ps[n % 4]
                    if kind == "v":
                        t = b * TB + 2 * u
                        nc.scalar.activation(vaug[:, t:t + 2, :, 0:HD],
                                             src.rearrange("p (t h d) -> p t h d", t=2, h=H), ACT.Copy).then_inc(v_ready[l], 1)
                        continue
                    side = 0 if kind == "q" else 1
                    unit = 2 * b + u
                    scale = HD ** -0.5 if side == 0 else 1.0
                    bias = 0.0 if l == 0 else qkb4[:, 2 * side + u:2 * side + u + 1]
                    if m >= 2:
                        act.wait_ge(parts_ready[l], m - 1)
                    if unit >= 2:
                        act.wait_ge(spread[unit - 2], 16 * 2 * TERMS * (l + 1))
                    nc.scalar.activation(qkf[:, side, :], src, ACT.Identity, scale=scale, bias=bias).then_inc(act_own, 1)
                    nc.scalar.activation(parts[:, side, unit % 2, 0, :], src, ACT.Identity, scale=scale,
                                         bias=bias).then_inc(qkf_ready[l], 1)
                    m += 1

                def move_context(g):
                    act.wait_ge(pv_ps[l], g + 1)
                    if g >= 2:
                        act.wait_ge(c_tr[l], g - 1)
                    nc.scalar.activation(ctxden[:, g % 2, :], ps[6], ACT.Copy).then_inc(ctxden_ready[l], 1)

                for s in range(NG + 2):
                    if 0 <= s - 2 < NG:
                        move_context(s - 2)
                    g = s - 1
                    if not 0 <= g < NG:
                        continue
                    for c, pieces in enumerate(B_CHUNKS):
                        n = NB * g + c
                        if c == 0 and g >= 2:
                            act.wait_ge(pv_ps[l], g - 1)
                        act.wait_ge(b_ps[l], n + 1)
                        src = ps[4 + c % 2]
                        j, k, _ = pieces[0]
                        if k == 2:
                            dst = pt[:, g % 2, j:j + 2, PK[2]:PK[2] + 256]
                            src = src.rearrange("p (j q) -> p j q", j=2)
                        else:
                            dst = pt[:, g % 2, j, PK[k]:PK[k] + 512]
                        nc.scalar.activation(dst, src, ACT.Exp).then_inc(b_exp[l], 1)
                move_transposed(l, 1)
                move_transposed(l, 2)
                act.wait_ge(gexp_in[l], 1)
                nc.scalar.activation(gexp[:, :, 0:TOPK[l]], gexp[:, :, 0:TOPK[l]], ACT.Exp).then_inc(gexp_done[l], 1)

                def act_x(ii, off):
                    i, _, _ = tile_at(ii, off)
                    act.wait_ge(xT_ps[l], i + 1)
                    if not (isinstance(i, int) and i < 2):
                        act.wait_ge(h_ps[l], i - 1)
                    nc.scalar.activation(xtT[:, off % 2, :, :].rearrange("p k c -> p (k c)"),
                                         ps[off % 2][:, 0:D], ACT.Copy).then_inc(xT_sb[l], 1)

                def act_hid(ii, off):
                    i, _, _ = tile_at(ii, off)
                    if l == 0:
                        act.wait_ge(h_ps[l], i + 1)
                        if not (isinstance(i, int) and i < 2):
                            act.wait_ge(hT_ps[l], i - 1)
                        nc.scalar.activation(hid[:, off % 2, 0:HB[0]], ps[2 + off % 2][:, 0:HB[0]],
                                             ACT.Silu).then_inc(hid_ready[l], 1)
                    else:
                        act.wait_ge(sig_in, i + 1)
                        nc.scalar.activation(gs_[:, off % 2, :], ga_[:, off % 2, :], ACT.Sigmoid,
                                             scale=ALPHA).then_inc(sig_done, 1)

                def act_hT(ii, off):
                    i, _, _ = tile_at(ii, off)
                    act.wait_ge(hT_ps[l], i + 1)
                    if not (isinstance(i, int) and i < 2):
                        act.wait_ge(y_ps[l], i - 1)
                    nc.scalar.activation(hidT[:, off % 2, :, :].rearrange("p k c -> p (k c)"),
                                         ps[4 + off % 2][:, 0:D], ACT.Copy).then_inc(hT_sb[l], 1)

                def act_y(ii, off):
                    i, r, rnd = tile_at(ii, off)
                    act.wait_ge(y_ps[l], i + 1)
                    if not (isinstance(i, int) and i < 4):
                        act.wait_ge(y_summed[r], TILES_BEFORE[l][r] + 16 * rnd)
                    nc.scalar.activation(yt[:, r, :], ps[6 + off % 2][:, 0:D], ACT.Copy,
                                         scale=weight[:, bass.ds(i, 1)]).then_inc(y_sb[l], 1)

                def act_step(ii, off):
                    n = SLOTS_T[l]
                    known = isinstance(ii, int)
                    if l == 1 and (not known or off < n):
                        act_x(ii, off)
                    if not known or 0 <= off - 1 < n:
                        act_hid(ii, off - 1)
                    if l == 1 and (not known or 0 <= off - 2 < n):
                        act_hT(ii, off - 2)
                    if not known or 0 <= off - 3 < n:
                        act_y(ii, off - 3)

                for s in range(STEADY):
                    act_step(0, s)
                with act.Fori(0, (SLOTS_T[l] - STEADY) // UNROLL) as ii:
                    for q in range(UNROLL):
                        act_step(ii, STEADY + q)
                for s in range(SLOTS_T[l], SLOTS_T[l] + 3):
                    act_step(0, s)

        @block.vector
        def _(dve):
            links = [0]

            def count(ins):
                links[0] += 1
                ins.then_inc(dve_own, 1)

            def settle():
                dve.wait_ge(dve_own, links[0])

            def link(ins):
                count(ins)
                settle()

            link(nc.vector.memset(ones_b[:, :], 1.0))
            link(nc.vector.memset(vaug[:, :, :, :], 1.0))
            link(nc.vector.memset(kr[SROWS:MROWS, :, :, :], 1.0))
            dve.wait_ge(ld_const, 48)
            link(nc.vector.tensor_copy(constb[:, :, :].rearrange("p a c -> p (a c)"), constb_f))

            def spread_silu(l):
                dve.wait_ge(silu_done, 1)
                nc.vector.tensor_copy(
                    silb.rearrange("p k b n -> p (k b) n"),
                    silc[:, l, :, :].rearrange("p k b -> p (k b)").unsqueeze(2).broadcast_to([P, KD * B, P]),
                ).then_inc(silb_done[l], 1)

            def modulation(l):
                dve.wait_ge(mod_ps[l], 1)
                link(nc.vector.tensor_copy(modcol[:, l, 0:2, :].rearrange("p c b -> p (c b)"), ps[7][:, 0:4]))
                nc.vector.tensor_scalar(modcol[:, l, 2:4, :].rearrange("p c b -> p (c b)"), ps[7][:, 4:8], 1.0,
                                        None, ALU.add).then_inc(mod_sb[l], 1)
                for b in range(B):
                    gb = modbc[:, b, 3, :] if l == 0 else gb_next[:, b, :]
                    gates = ((ps[2 * b][:, 0:D], modbc[:, b, 0, :]), (ps[2 * b + 1][:, D:2 * D], gb))
                    for r, (src, _) in enumerate(gates):
                        count(nc.vector.tensor_scalar(tmp[:, r, :], src, 0.0, 2.0, ALU.is_ge, ALU.mult))
                    settle()
                    link(nc.vector.tensor_scalar(tmp[:, :, :], tmp[:, :, :], 1.0, None, ALU.subtract))
                    for r, (src, dst) in enumerate(gates):
                        count(nc.vector.tensor_tensor(dst, src, tmp[:, r, :], ALU.mult))
                    settle()
                    for r, (_, dst) in enumerate(gates):
                        count(nc.vector.scalar_tensor_tensor(dst, dst, LN_CLAMP, tmp[:, r, :], ALU.max, ALU.mult))
                    count(nc.vector.tensor_copy(modbc[:, b, 1, :], ps[2 * b][:, D:2 * D]))
                    count(nc.vector.tensor_scalar(modbc[:, b, 2, :], ps[2 * b + 1][:, 0:D], 1.0, None, ALU.add))
                    settle()
                    dve.sem_inc(mod_sb[l], 1)

            def normalise(l, which, b):
                for t in range(b * TB, (b + 1) * TB):
                    count(nc.vector.bn_stats(stats[:, t, :], x[:, t, :]))
                settle()
                for t in range(b * TB, (b + 1) * TB):
                    count(nc.vector.bn_aggr(mv[:, t, :], stats[:, t, :]))
                settle()
                c = slice(b * TB, (b + 1) * TB)
                nc.vector.tensor_scalar(vareps[:, c], mv[:, c, 1], EPS, None, ALU.add).then_inc(var_ready[l][which], 1)
                dve.wait_ge(rstd_ready[l][which], b + 1)
                for t in range(b * TB, (b + 1) * TB):
                    nc.vector.tensor_scalar(tok[:, t, :], x[:, t, :], mv[:, t, 0:1], rstd[:, t:t + 1],
                                            ALU.subtract, ALU.mult).then_inc(xhat_ready[l][which], 1)
                dve.wait_ge(xhat_ready[l][which], (b + 1) * TB)

            spread_silu(0)
            for l in range(2):
                if l == 1:
                    dve.wait_ge(ld_small, 64)
                    link(nc.vector.tensor_scalar(qkb4[:, 0:2], qkb[:, 0:2], HD ** -0.5, None, ALU.mult))
                    nc.vector.tensor_copy(qkb4[:, 2:4], qkb[:, 2:4]).then_inc(qkb_done, 1)
                for b in range(B):
                    if l == 0:
                        dve.wait_ge(ld_x[b], 16)
                    normalise(l, 0, b)
                if l == 0:
                    modulation(0)
                m = 0
                for n, (kind, b, u) in enumerate(FILLS):
                    if kind == "v":
                        if l == 1:
                            dve.wait_ge(qkv_ps[l], n + 1)
                            t = b * TB + 2 * u
                            for half_t in range(2):
                                ins = nc.vector.tensor_tensor(
                                    vaug[:, t + half_t, :, 0:HD],
                                    ps[n % 4][:, half_t * D:(half_t + 1) * D].rearrange("p (h d) -> p h d", h=H),
                                    rows[:, 0, :].rearrange("p (h d) -> p h d", h=H), ALU.add)
                            ins.then_inc(v_ready[l], 1)
                        continue
                    side, r = (0 if kind == "q" else 1), (2 * b + u) % 2
                    dve.wait_ge(qkf_ready[l], m + 1)
                    link(nc.vector.tensor_tensor(rest, qkf[:, side, :], parts[:, side, r, 0, :], ALU.subtract))
                    link(nc.vector.tensor_copy(parts[:, side, r, 1, :], rest))
                    nc.vector.tensor_tensor(parts[:, side, r, 2, :], rest, parts[:, side, r, 1, :],
                                            ALU.subtract).then_inc(parts_ready[l], 1)
                    dve.wait_ge(parts_ready[l], m + 1)
                    m += 1

                def maxima(g, c):
                    dve.wait_ge(a_ps[l], NA * g + c + 1)
                    i, j0, n = A_CHUNKS[c]
                    if c == 0 and g >= 2:
                        dve.wait_ge(m_ready[l], g - 1)
                    nc.vector.tensor_reduce(mx[:, g % 2, :].rearrange("p (j i) -> p j i", j=HG)[:, j0:j0 + n, i], a_view(c), AX.X,
                                            ALU.max).then_inc(a_max[l], 1)

                def split_maxima(g):
                    dve.wait_ge(a_max[l], NA * (g + 1))
                    link(nc.vector.tensor_scalar(mneg[:, g % 2, 0:16], mx[:, g % 2, :], -1.0, None, ALU.mult))
                    nc.vector.scalar_tensor_tensor(mneg[:, g % 2, 16:32], mx[:, g % 2, :], -1.0, mneg[:, g % 2, 0:16],
                                                   ALU.mult, ALU.subtract).then_inc(m_ready[l], 1)

                def move_maxima(g):
                    dve.wait_ge(m_tr[l], g + 1)
                    if g >= 2:
                        dve.wait_ge(m_rows[l][g % 2], 32 * (g // 2))
                    nc.vector.tensor_copy(mT[:, g % 2, :], ps[7][0:32, 0:P // 2].bitcast(BF16)).then_inc(mT_ready[l], 1)

                def context(g):
                    dve.wait_ge(c_tr[l], g + 1)
                    view = ps[7].rearrange("p (t j c) -> p t j c", t=TB, j=HG)
                    rd = rden[:, g % 2, :].rearrange("p (t j) -> p t j", t=TB)
                    link(nc.vector.reciprocal(rd, view[:, :, :, HD]))
                    b, hg = g // 4, g % 4
                    nc.vector.tensor_tensor(
                        tok[:, b * TB:(b + 1) * TB, hg * 64:(hg + 1) * 64].rearrange("p t (j d) -> p t j d", j=HG),
                        view[:, :, :, 0:HD], rd.unsqueeze(3).broadcast_to([P, TB, HG, HD]),
                        ALU.mult).then_inc(ctx_ready[l], 1)

                for s in range(NG + 2):
                    if s < NG:
                        maxima(s, 0)
                        maxima(s, 1)
                    if 0 <= s - 1 < NG:
                        move_maxima(s - 1)
                    if s < NG:
                        maxima(s, 2)
                    if 0 <= s - 2 < NG:
                        context(s - 2)
                    if s < NG:
                        for c in range(3, NA):
                            maxima(s, c)
                        split_maxima(s)

                dve.wait_ge(ld_bias[l], 16)
                bf = bfull[0:EXPERTS[l], 0:BROW[l]]
                bp = [bparts[0:EXPERTS[l], r, 0:BROW[l]] for r in range(3)]
                link(nc.vector.tensor_copy(bp[0], bf))
                link(nc.vector.tensor_tensor(bf, bf, bp[0], ALU.subtract))
                link(nc.vector.tensor_copy(bp[1], bf))
                nc.vector.tensor_tensor(bp[2], bf, bp[1], ALU.subtract).then_inc(bparts_ready[l], 1)

                for m in range(NT // 2):
                    b = m // 2
                    dve.wait_ge(wo_ps[l], m + 1)
                    src = ps[m].rearrange("p (t c) -> p t c", t=2)
                    ga = modbc[:, b, 0, :].unsqueeze(1).broadcast_to([P, 2, D])
                    if l == 1:
                        link(nc.vector.tensor_tensor(tmp[:, :, :], src, rows[:, 1, :].unsqueeze(1).broadcast_to([P, 2, D]), ALU.add))
                        src = tmp[:, :, :]
                    link(nc.vector.tensor_tensor(tmp[:, :, :], src, ga, ALU.mult))
                    link(nc.vector.tensor_tensor(x[:, 2 * m:2 * m + 2, :], x[:, 2 * m:2 * m + 2, :], tmp[:, :, :], ALU.add))

                for b in range(B):
                    dve.wait_ge(tr_ps[l][1], KD * (b + 1))
                    normalise(l, 1, b)
                    rng = slice(b * TB, (b + 1) * TB)
                    wide = [P, TB, D]
                    link(nc.vector.tensor_tensor(tok[:, rng, :], tok[:, rng, :],
                                                 modbc[:, b, 2, :].unsqueeze(1).broadcast_to(wide), ALU.mult))
                    link(nc.vector.tensor_tensor(tok[:, rng, :], tok[:, rng, :],
                                                 modbc[:, b, 1, :].unsqueeze(1).broadcast_to(wide), ALU.add))
                    if l == 1:
                        t4 = xt
                        link(nc.vector.tensor_tensor(t4, tok[:, rng, :],
                                                     modbc[:, b, 3, :].unsqueeze(1).broadcast_to(wide), ALU.mult))
                        link(nc.vector.tensor_tensor(x[:, rng, :], x[:, rng, :], t4, ALU.add))
                        for t in range(b * TB, (b + 1) * TB):
                            count(nc.vector.tensor_tensor_reduce(t4[:, t % TB, :], tok[:, t, :], tok[:, t, :], 1.0, 0.0,
                                                                 ALU.mult, ALU.add, sumsq[:, t:t + 1]))
                        settle()
                        nc.vector.tensor_scalar(vareps[:, rng], sumsq[:, rng], 1.0 / D, EPS, ALU.mult,
                                                ALU.add).then_inc(rms_in, 1)
                        dve.wait_ge(rms_out, b + 1)
                        for t in range(b * TB, (b + 1) * TB):
                            count(nc.vector.scalar_tensor_tensor(tok[:, t, :], tok[:, t, :], rstd[:, t:t + 1],
                                                                 rows[:, 2, :], ALU.mult, ALU.mult))
                        settle()
                    dve.sem_inc(tok_ready[l], 1)

                E, K = EXPERTS[l], TOPK[l]
                dve.wait_ge(gate_ps[l], 1)
                lg = logit[:, :, 0:E]
                if l == 0:
                    dve.wait_ge(ld_small, 64)
                src = ps[6][:, 0:NT * 16].rearrange("p (t e) -> p t e", t=NT)[:, :, 0:E]
                link(nc.vector.tensor_tensor(lg, src, gbias[:, l, 0:E].unsqueeze(1).broadcast_to([P, NT, E]), ALU.add))
                if l == 0:
                    link(nc.vector.tensor_tensor(lg, lg, gbias[:, 2, 0:E].unsqueeze(1).broadcast_to([P, NT, E]), ALU.add))
                for t in range(NT):
                    count(nc.vector.max(top8[:, t, :], logit[:, t, 0:E]))
                settle()
                for t in range(NT):
                    count(nc.vector.max_index(idx8[:, t, :], top8[:, t, :], logit[:, t, 0:E]))
                settle()
                link(nc.vector.tensor_copy(idf[:, :, 0:K], idx8[:, :, 0:K]))
                oh = onehot[:, 0:NT * K * E].rearrange("p (t k e) -> p t k e", t=NT, k=K)
                link(nc.vector.tensor_tensor(
                    oh, idf[:, :, 0:K].unsqueeze(3).broadcast_to([P, NT, K, E]),
                    iota_e[:, 0:E].unsqueeze(1).unsqueeze(1).broadcast_to([P, NT, K, E]), ALU.is_equal))
                ch = chosen[:, 0:NT * E].rearrange("p (t e) -> p t e", t=NT)
                with nc.allow_low_precision(reason="zeros and ones"):
                    nc.vector.tensor_reduce(ch, oh.rearrange("p t k e -> p t e k"), AX.X, ALU.add).then_inc(chosen_ready[l], 1)
                gk = gexp[:, :, 0:K]
                nc.vector.tensor_tensor(gk, top8[:, :, 0:K], top8[:, :, 0:1].broadcast_to([P, NT, K]),
                                        ALU.subtract).then_inc(gexp_in[l], 1)
                dve.wait_ge(gexp_done[l], 1)
                link(nc.vector.tensor_reduce(gsum[:, :], gk, AX.X, ALU.add))
                link(nc.vector.reciprocal(grec[:, :], gsum[:, :]))
                link(nc.vector.tensor_tensor(gate[:, :, 0:K], gk, grec[:, :].unsqueeze(2).broadcast_to([P, NT, K]), ALU.mult))
                dve.wait_ge(rank_ps[l], 1)
                pk = picked[:, 0:E * 8].rearrange("p (e c) -> p e c", e=E)
                link(nc.vector.tensor_tensor(pk, ps[5][:, 0:E].unsqueeze(2).broadcast_to([P, E, 8]),
                                             c128.unsqueeze(1).broadcast_to([P, E, 8]), ALU.is_gt))
                link(nc.vector.tensor_reduce(ntile[:, 0:E], pk, AX.X, ALU.add))
                pk = picked[:, 0:E * E].rearrange("p (a b) -> p a b", a=E)
                link(nc.vector.tensor_tensor(pk, ntile[:, 0:E].unsqueeze(1).broadcast_to([P, E, E]), lower[:, 0:E, 0:E], ALU.mult))
                link(nc.vector.tensor_reduce(excl[:, 0:E], pk, AX.X, ALU.add))
                link(nc.vector.tensor_tensor(incl[:, 0:E], excl[:, 0:E], ntile[:, 0:E], ALU.add))
                sl = slot[:, 0:NT * E].rearrange("p (t e) -> p t e", t=NT)
                link(nc.vector.scalar_tensor_tensor(
                    sl, excl[:, 0:E].unsqueeze(1).broadcast_to([P, NT, E]), float(P),
                    ps[7][:, 0:NT * E].rearrange("p (t e) -> p t e", t=NT), ALU.mult, ALU.add))
                pk = picked[:, 0:NT * K * E].rearrange("p (t k e) -> p t k e", t=NT, k=K)
                link(nc.vector.tensor_tensor(pk, oh, sl.unsqueeze(2).broadcast_to([P, NT, K, E]), ALU.mult))
                link(nc.vector.tensor_reduce(slotf[:, 0:NT * K], pk.rearrange("p t k e -> p (t k) e"), AX.X, ALU.add))
                link(nc.vector.tensor_copy(slot_i[:, 0:NT * K], slotf[:, 0:NT * K]))
                link(nc.vector.tensor_scalar(slot_i[:, 0:NT * K], slot_i[:, 0:NT * K], P - 1, None, ALU.bitwise_and))
                link(nc.vector.tensor_copy(place[:, 0:NT * K], slot_i[:, 0:NT * K]))
                link(nc.vector.tensor_tensor(first[:, 0:NT * K], slotf[:, 0:NT * K], place[:, 0:NT * K], ALU.subtract))
                link(nc.vector.tensor_scalar(first[:, 0:NT * K], first[:, 0:NT * K], 1.0 / P, None, ALU.mult))
                n = SLOTS_T[l]
                dve.wait_ge(brows_ready[l], 48)
                at_p = at_place[:, 0:NT * K * P].rearrange("p (n c) -> p n c", n=NT * K)
                at_t = at_tile[:, 0:NT * K * 2 * MT].rearrange("p (n a c) -> p n a c", n=NT * K, a=2)
                for t in range(NT):
                    c = slice(t * K, (t + 1) * K)
                    count(nc.vector.tensor_tensor(
                        at_t[:, c, 1, :], first[:, c].unsqueeze(2).broadcast_to([P, K, MT]),
                        iota_t.unsqueeze(1).broadcast_to([P, K, MT]), ALU.is_equal))
                    count(nc.vector.tensor_tensor(
                        at_p[:, c, :], place[:, c].unsqueeze(2).broadcast_to([P, K, P]),
                        iota_p.unsqueeze(1).broadcast_to([P, K, P]), ALU.is_equal))
                    settle()
                    link(nc.vector.tensor_scalar(at_t[:, c, 0, :], at_t[:, c, 1, :], left[:, t:t + 1], None, ALU.mult))
                    nc.vector.tensor_tensor(at_t[:, c, 1, :], at_t[:, c, 1, :],
                                            gate[:, t, 0:K].unsqueeze(2).broadcast_to([P, K, MT]),
                                            ALU.mult).then_inc(tile_of[l], 1)
                pk = picked[0:1, 0:n * E].rearrange("p (t e) -> p t e", t=n) 
                link(nc.vector.tensor_tensor(pk, iota_t[0:1, 0:n].unsqueeze(2).broadcast_to([1, n, E]),
                                             incl[0:1, 0:E].unsqueeze(1).broadcast_to([1, n, E]), ALU.is_ge))
                link(nc.vector.tensor_reduce(tef[:, 0:n], pk, AX.X, ALU.add))
                link(nc.vector.tensor_scalar(tef[:, 0:n], tef[:, 0:n], float(E - 1), None, ALU.min))
                link(nc.vector.tensor_copy(te[:, 0:n], tef[:, 0:n]))
                dve.wait_ge(placed_ps[l], 1)
                sums = ps[4][:, 0:2 * MT].rearrange("p (a c) -> p a c", a=2)
                link(nc.vector.tensor_copy(weight[:, :], sums[:, 1, :]))
                link(nc.vector.tensor_scalar(token_f[:, :], sums[:, 0, :], 0.0, lane[:, 0:1], ALU.is_equal, ALU.mult))
                link(nc.vector.tensor_tensor(token_f[:, :], token_f[:, :], sums[:, 0, :], ALU.subtract))
                nc.vector.tensor_scalar(token[:, :], token_f[:, :], float(T), None, ALU.add).then_inc(slots_ready[l], 1)

                if l == 0:
                    spread_silu(1)

                def dve_x(ii, off):
                    i, _, _ = tile_at(ii, off)
                    dve.wait_ge(xT_ps[l], i + 1)
                    if not (isinstance(i, int) and i < 2):
                        dve.wait_ge(h_ps[l], i - 1)
                    nc.vector.tensor_copy(xtT[:, off % 2, :, :].rearrange("p k c -> p (k c)"),
                                          ps[off % 2][:, 0:D]).then_inc(xT_sb[l], 1)

                def dve_hT(ii, off):
                    i, _, _ = tile_at(ii, off)
                    dve.wait_ge(hT_ps[l], i + 1)
                    if not (isinstance(i, int) and i < 2):
                        dve.wait_ge(y_ps[l], i - 1)
                    nc.vector.tensor_copy(hidT[0:HK[0], off % 2, :, :].rearrange("p k c -> p (k c)"),
                                          ps[4 + off % 2][0:HK[0], 0:D]).then_inc(hT_sb[l], 1)

                def dve_gate(ii, off):
                    i, _, _ = tile_at(ii, off)
                    r = off % 2
                    early = isinstance(i, int) and i < 2
                    dve.wait_ge(h_ps[l], i + 1)
                    if not early:
                        dve.wait_ge(hid_ready[l], i - 1)
                        dve.wait_ge(hT_ps[l], i - 1)
                    nc.vector.tensor_scalar(ga_[:, r, :], ps[2 + r][:, 0:HALF], LIMIT, None, ALU.min).then_inc(sig_in, 1)
                    nc.vector.tensor_scalar(gb_[:, r, :], ps[2 + r][:, HALF:2 * HALF], LIMIT, -LIMIT, ALU.min,
                                            ALU.max).then_inc(h_read, 1)
                    dve.wait_ge(h_read, i + 1)
                    nc.vector.scalar_tensor_tensor(gu_[:, r, :], gb_[:, r, :], 1.0, ga_[:, r, :], ALU.add,
                                                   ALU.mult).then_inc(gu_done, 1)
                    dve.wait_ge(gu_done, i + 1)
                    dve.wait_ge(sig_done, i + 1)
                    nc.vector.tensor_tensor(hid[:, r, :], gu_[:, r, :], gs_[:, r, :], ALU.mult).then_inc(hid_ready[l], 1)

                def dve_step(ii, off):
                    n = SLOTS_T[l]
                    known = isinstance(ii, int)
                    if l == 0:
                        if not known or off < n:
                            dve_x(ii, off)
                        if not known or 0 <= off - 2 < n:
                            dve_hT(ii, off - 2)
                    elif not known or 0 <= off - 1 < n:
                        dve_gate(ii, off - 1)

                for s in range(STEADY):
                    dve_step(0, s)
                with dve.Fori(0, (SLOTS_T[l] - STEADY) // UNROLL) as ii:
                    for q in range(UNROLL):
                        dve_step(ii, STEADY + q)
                for s in range(SLOTS_T[l], SLOTS_T[l] + 3):
                    dve_step(0, s)

                if l == 0:
                    modulation(1)
                for b in range(B):
                    rng = slice(b * TB, (b + 1) * TB)
                    dve.wait_ge(acc_loaded[b], 32 * (l + 1))
                    link(nc.vector.tensor_tensor(acc_in[:, 0, rng, :], acc_in[:, 0, rng, :], acc_in[:, 1, rng, :], ALU.add))
                    link(nc.vector.tensor_tensor(acc_in[:, 0, rng, :], acc_in[:, 0, rng, :],
                                                 modbc[:, b, 3, :].unsqueeze(1).broadcast_to([P, TB, D]), ALU.mult))
                    nc.vector.tensor_tensor(x[:, rng, :], x[:, rng, :], acc_in[:, 0, rng, :], ALU.add).then_inc(x_new[l], 1)
                    dve.wait_ge(x_new[l], b + 1)
                if l == 0:
                    link(nc.vector.tensor_copy(modbc[:, :, 3, :], gb_next[:, :, :]))

        @block.tensor
        def _(pe):
            def modulation(l):
                pe.wait_ge(ld_mod[l], 16)
                pe.wait_ge(silb_done[l], 1)
                wmod = wmods[l]
                if l == 1:
                    pe.wait_ge(y_sb[0], SLOTS_T[0])
                    pe.wait_ge(xT_sb[0], SLOTS_T[0])
                    pe.wait_ge(hid_ready[0], SLOTS_T[0])
                for c in range(4):
                    for k in range(KD):
                        nc.tensor.matmul(ps[7][:, 2 * c:2 * c + 2], wmod[:, k, c * P:(c + 1) * P], silc[:, l, k, :],
                                         start=(k == 0), stop=(k == KD - 1))
                for b in range(B):
                    for h in range(2):
                        for k in range(KD):
                            last = nc.tensor.matmul(ps[2 * b + h], silb[:, k, b, :],
                                                    wmod[:, k, (h + 1) * 512:(h + 2) * 512],
                                                    start=(k == 0), stop=(k == KD - 1))
                last.then_inc(mod_ps[l], 1)

            def turn(l, which, ready, count):
                for b in range(B):
                    pe.wait_ge(ready, count * (b + 1))
                    for k in range(KD):
                        n = KD * b + k
                        if n >= 2:
                            pe.wait_ge(feat_ready[l][which], n - 1)
                        for i in range(TB):
                            last = nc.tensor.transpose(ps[4 + n % 2][:, i * P:(i + 1) * P],
                                                       tok[:, b * TB + i, k * P:(k + 1) * P], ident)
                        last.then_inc(tr_ps[l][which], 1)

            pe.wait_ge(ld_const, 48)
            for l in range(2):
                modulation(l)
                turn(l, 0, xhat_ready[l][0], TB)
                pe.wait_ge(ld_wqkv[l], 16)
                pe.wait_ge(mod_sb[l], 1 + B)
                for n, (kind, b, u) in enumerate(FILLS):
                    if n >= 4:
                        wait_fill_read(pe, l, n - 4)
                    pe.wait_ge(feat_ready[l][0], KD * (b + 1))
                    if kind == "v":
                        for half_t in range(2):
                            t = b * TB + 2 * u + half_t
                            for k in range(KD):
                                last = nc.tensor.matmul(ps[n % 4][:, half_t * D:(half_t + 1) * D],
                                                        feat[:, k, t * P:(t + 1) * P], wqkv[:, k, 2 * D:3 * D],
                                                        start=(k == 0), stop=(k == KD - 1))
                    else:
                        lo = (0 if kind == "q" else D) + u * P
                        for k in range(KD):
                            last = nc.tensor.matmul(ps[n % 4], wqkv[:, k, lo:lo + P], feat[:, k, b * S:(b + 1) * S],
                                                    start=(k == 0), stop=(k == KD - 1))
                    last.then_inc(qkv_ps[l], 1)
                for n in range(8, len(FILLS)):
                    wait_fill_read(pe, l, n)

                def scores_by_query(g, c):
                    i, j0, heads = A_CHUNKS[c]
                    u = g // 2
                    pe.wait_ge(spread[u], 16 * 2 * TERMS * (l + 1))
                    if NA * g + c >= 2:
                        pe.wait_ge(a_max[l], NA * g + c - 1)
                    w = (i + 1) * P
                    dst = a_view(c)
                    for j in range(heads):
                        hl = (g % 2) * HG + j0 + j
                        nc.tensor.matmul(dst[:, j, :], qr[0:SROWS, u % 2, hl, i * P:(i + 1) * P],
                                         kr[0:SROWS, u % 2, hl, 0:w], start=True, stop=False)
                        last = nc.tensor.matmul(dst[:, j, w - P:w], ident_b, causal_b, start=False, stop=True)
                    last.then_inc(a_ps[l], 1)

                def scores_by_key(g, c):
                    u = g // 2
                    n = NB * g + c
                    if c == 0:
                        pe.wait_ge(m_rows[l][g % 2], 32 * (g // 2 + 1))
                    if n >= 2:
                        pe.wait_ge(b_exp[l], n - 1)
                    for j, k, col in B_CHUNKS[c]:
                        hl = (g % 2) * HG + j
                        nc.tensor.matmul(ps[4 + c % 2][:, col:col + S - k * P],
                                         kr[0:MROWS, u % 2, hl, k * P:(k + 1) * P],
                                         qr[0:MROWS, u % 2, hl, k * P:S], start=True, stop=False)
                        last = nc.tensor.matmul(ps[4 + c % 2][:, col:col + P], causal_b, ident_b,
                                                start=False, stop=True)
                    last.then_inc(b_ps[l], 1)

                def turn_maxima(g):
                    pe.wait_ge(m_ready[l], g + 1)
                    if g >= 2:
                        pe.wait_ge(ctx_ready[l], g - 1)
                    nc.tensor.transpose(ps[7][0:32, 0:P // 2].bitcast(BF16), mneg[:, g % 2, :], ident_b).then_inc(m_tr[l], 1)

                def weigh_values(g):
                    b, hg = g // 4, g % 4
                    pe.wait_ge(b_exp[l], NB * (g + 1))
                    if g >= 1:
                        pe.wait_ge(ctxden_ready[l], g)
                    for k in range(TB):
                        for j in range(HG):
                            last = nc.tensor.matmul(ps[6][32 * j:32 * j + 32, k * P:S],
                                                    vaug[:, b * TB + k, hg * HG + j, :],
                                                    pt[:, g % 2, j, PK[k]:PK[k] + S - k * P],
                                                    start=(k == 0), stop=(k == TB - 1))
                    last.then_inc(pv_ps[l], 1)

                def turn_context(g):
                    pe.wait_ge(ctxden_ready[l], g + 1)
                    if g + 1 < NG:
                        pe.wait_ge(mT_ready[l], g + 2)
                    else:
                        pe.wait_ge(ctx_ready[l], g)
                    for i in range(TB):
                        last = nc.tensor.transpose(ps[7][:, i * P:(i + 1) * P], ctxden[:, g % 2, i * P:(i + 1) * P], ident)
                    last.then_inc(c_tr[l], 1)

                for s in range(NG + 2):
                    if s < NG:
                        scores_by_query(s, 0)
                        scores_by_query(s, 1)
                    if 0 <= s - 1 < NG:
                        turn_maxima(s - 1)
                    if 0 <= s - 2 < NG:
                        weigh_values(s - 2)
                    if s < NG:
                        scores_by_query(s, 2)
                    if 0 <= s - 2 < NG:
                        turn_context(s - 2)
                    for c in range(NB):
                        if 0 <= s - 1 < NG:
                            scores_by_key(s - 1, c)
                        if s < NG and c in (1, 4, 7):
                            scores_by_query(s, 3 + c // 3)

                turn(l, 1, ctx_ready[l], NG // B)
                pe.wait_ge(ld_wo[l], 16)
                for m in range(NT // 2):
                    pe.wait_ge(feat_ready[l][1], KD * (m // 2 + 1))
                    for half_t in range(2):
                        t = 2 * m + half_t
                        for k in range(KD):
                            last = nc.tensor.matmul(ps[m][:, half_t * D:(half_t + 1) * D], feat[:, k, t * P:(t + 1) * P],
                                                    wo[:, k, :], start=(k == 0), stop=(k == KD - 1))
                    last.then_inc(wo_ps[l], 1)

                E, K = EXPERTS[l], TOPK[l]
                turn(l, 2, tok_ready[l], 1)
                pe.wait_ge(ld_small, 64)
                for t in range(NT):
                    pe.wait_ge(feat_ready[l][2], KD * (t // TB + 1))
                    for k in range(KD):
                        last = nc.tensor.matmul(ps[6][:, t * 16:t * 16 + E], feat[:, k, t * P:(t + 1) * P],
                                                gw[:, l, k, 0:E], start=(k == 0), stop=(k == KD - 1))
                last.then_inc(gate_ps[l], 1)
                pe.wait_ge(chosen_ready[l], 1)
                nc.tensor.matmul(ps[7][:, 0:NT * E], before_b, chosen[:, 0:NT * E], start=True, stop=False)
                for t in range(NT - 1):
                    m = NT - 1 - t
                    nc.tensor.matmul(ps[7][:, (t + 1) * E:NT * E].rearrange("p (m e) -> p m e", m=m), ones_b[:, :],
                                     chosen[:, t * E:(t + 1) * E].unsqueeze(1).broadcast_to([P, m, E]),
                                     start=False, stop=(t == NT - 2))
                for t in range(NT):
                    last = nc.tensor.matmul(ps[5][:, 0:E], ones_b[:, :], chosen[:, t * E:(t + 1) * E],
                                            start=(t == 0), stop=(t == NT - 1))
                last.then_inc(rank_ps[l], 1)
                for t in range(NT):
                    pe.wait_ge(tile_of[l], t + 1)
                    for n in range(t * K, (t + 1) * K):
                        last = nc.tensor.matmul(ps[4][:, 0:2 * MT], at_place[:, n * P:(n + 1) * P],
                                                at_tile[:, n * 2 * MT:(n + 1) * 2 * MT],
                                                start=(n == 0), stop=(n == NT * K - 1))
                last.then_inc(placed_ps[l], 1)

                h_free = hid_ready[l] if l == 0 else h_read

                def pe_x(ii, off):
                    i, r, rnd = tile_at(ii, off)
                    pe.wait_ge(xt_loaded[r], TILES_BEFORE[l][r] + 16 * rnd + 16)
                    if not (isinstance(i, int) and i < 2):
                        pe.wait_ge(xT_sb[l], i - 1)
                    for k in range(KD):
                        last = nc.tensor.transpose(ps[off % 2][:, k * P:(k + 1) * P], xt[:, r, k * P:(k + 1) * P], ident)
                    last.then_inc(xT_ps[l], 1)

                def expert_of(i):
                    return pe.value_load(te[0:1, bass.ds(i, 1)], min_val=0, max_val=E - 1)

                def pe_h(ii, off):
                    i, _, _ = tile_at(ii, off)
                    e = expert_of(i)
                    dst = ps[2 + off % 2][:, 0:HB[l]]
                    if not (isinstance(i, int) and i < 2):
                        pe.wait_ge(h_free, i - 1)
                    nc.tensor.matmul(dst, ones_b[0:3, :], moe_bias(l, 0, HB[l], e), start=True, stop=False)
                    pe.wait_ge(xT_sb[l], i + 1)
                    for k in range(KD):
                        last = nc.tensor.matmul(dst, xtT[:, off % 2, k, :], moe_w1(l, k, e), start=False, stop=(k == KD - 1))
                    last.then_inc(h_ps[l], 1)

                def pe_hT(ii, off):
                    i, _, _ = tile_at(ii, off)
                    pe.wait_ge(hid_ready[l], i + 1)
                    if not (isinstance(i, int) and i < 2):
                        pe.wait_ge(hT_sb[l], i - 1)
                    for k in range(2):
                        last = nc.tensor.transpose(ps[4 + off % 2][0:HK[l], k * P:(k + 1) * P],
                                                   hid[:, off % 2, k * HK[l]:(k + 1) * HK[l]], ident)
                    last.then_inc(hT_ps[l], 1)

                def pe_y(ii, off):
                    i, _, _ = tile_at(ii, off)
                    e = expert_of(i)
                    dst = ps[6 + off % 2][:, 0:D]
                    if not (isinstance(i, int) and i < 2):
                        pe.wait_ge(y_sb[l], i - 1)
                    nc.tensor.matmul(dst, ones_b[0:3, :], moe_bias(l, HB[l], BROW[l], e), start=True, stop=False)
                    pe.wait_ge(hT_sb[l], i + 1)
                    for k in range(2):
                        last = nc.tensor.matmul(dst, hidT[0:HK[l], off % 2, k, :], moe_w2(l, k, e), start=False, stop=(k == 1))
                    last.then_inc(y_ps[l], 1)

                def pe_step(ii, off):
                    n = SLOTS_T[l]
                    known = isinstance(ii, int)
                    if not known or off < n:
                        pe_x(ii, off)
                    if not known or 0 <= off - 1 < n:
                        pe_h(ii, off - 1)
                    if not known or 0 <= off - 2 < n:
                        pe_hT(ii, off - 2)
                    if not known or 0 <= off - 3 < n:
                        pe_y(ii, off - 3)

                pe.wait_ge(slots_ready[l], 1)
                pe.wait_ge(brows_ready[l], 48)
                pe.wait_ge(ld_w_lo[l], 16)
                if l == 1:
                    pe.wait_ge(ld_w_hi, 16)
                for s in range(STEADY):
                    pe_step(0, s)
                with pe.Fori(0, (SLOTS_T[l] - STEADY) // UNROLL) as ii:
                    for q in range(UNROLL):
                        pe_step(ii, STEADY + q)
                for s in range(SLOTS_T[l], SLOTS_T[l] + 3):
                    pe_step(0, s)


def _by_k(w, np):
    n, k = w.shape
    return np.ascontiguousarray(w.T.reshape(k // P, P, n).transpose(1, 0, 2))


def _mixture(w1, w2, l, np):
    e, h, d = w1.shape
    if l == 1:
        w1 = np.concatenate([w1[:, 0::2], w1[:, 1::2]], 1)
    a = np.zeros((e, HB[l], d), w1.dtype)
    a[:, :h] = w1
    a = a.transpose(2, 0, 1).reshape(KD, P, e, HB[l]).transpose(1, 2, 0, 3).reshape(P, e, KD * HB[l])
    rows = np.zeros((e, 2 * HK[l], d), w2.dtype)
    rows[:, :w2.shape[2]] = w2.transpose(0, 2, 1)
    rows = rows.reshape(e, 2, HK[l], d).transpose(2, 0, 1, 3).reshape(HK[l], e, 2 * d)
    b = np.zeros((P, e, 2 * d), w2.dtype)
    b[:HK[l]] = rows
    return np.ascontiguousarray(np.concatenate([a, b], 2).reshape(P, -1))


def _biases(b1, b2, l, np):
    e, h = b1.shape
    if l == 1:
        b1 = np.concatenate([b1[:, 0::2], b1[:, 1::2]], 1)
    out = np.zeros((e, BROW[l]), b1.dtype)
    out[:, :h] = b1
    out[:, HB[l]:] = b2
    return out


def kernel(**inputs):
    import numpy as np
    import concourse.bacc as bacc
    from concourse.bass_utils import run_bass_kernel_spmd

    a = {k: np.asarray(v) for k, v in inputs.items()}

    def spread_rows(v):
        return np.broadcast_to(v, (P,) + v.shape)

    consts = np.zeros((P, CONST_W), np.float32)
    consts[:, 0:P] = np.eye(P)
    consts[:, P:P + 16] = np.arange(16)
    consts[:, P + 16:P + 24] = np.arange(8) * P
    consts[:, P + 24:P + 280] = np.tril(np.ones((16, 16)), -1).reshape(-1)
    consts[:, P + 280:P + 328] = np.arange(MT)
    consts[:, P + 328:2 * P + 328] = np.arange(P)
    consts[:, 2 * P + 328:2 * P + 328 + NT] = T - np.arange(T).reshape(NT, P).T
    consts[:, 2 * P + 328 + NT] = np.arange(P)
    row, col = np.arange(P)[:, None], np.arange(P)[None, :]
    constb = np.concatenate([np.eye(P), np.where(col > row, BIG_NEG, 0.0), row < col], 1).astype(np.float32)

    def pad16(v):
        return np.concatenate([v, np.zeros(16 - len(v), v.dtype)])

    gws = []
    for name in ("L0_ffn_gate_w", "L1_ffn_gate_w"):
        w = a[name]
        w = np.concatenate([w, np.zeros((16 - len(w), D), w.dtype)], 0)
        gws.append(_by_k(w, np))
    def by_dim(w):
        return w.reshape(2, 8, HD, -1).transpose(0, 2, 1, 3).reshape(w.shape)

    arrays = {
        "x": a["L0_attn_x"].reshape(T, D),
        "consts": consts,
        "constb": constb,
        "cT": np.stack([a[f"L{l}_c"].T.reshape(KD, P, B).transpose(1, 0, 2) for l in range(2)], 1).reshape(P, 2 * KD * B),
        "wmod": np.stack([a[f"L{l}_wmod"].reshape(KD, P, 6 * D).transpose(1, 0, 2) for l in range(2)]),
        "wqkv": np.stack([
            _by_k(np.concatenate([by_dim(a["L0_attn_Wq"]), by_dim(a["L0_attn_Wk"]), a["L0_attn_Wv"]], 0), np),
            _by_k(np.concatenate([by_dim(a["L1_attn_wq"]), by_dim(a["L1_attn_wk"]), a["L1_attn_wv"]], 0), np)]),
        "wo": np.stack([_by_k(a["L0_attn_Wo"], np), _by_k(a["L1_attn_wo"], np)]),
        "rows": spread_rows(np.stack([a["L1_attn_bv"], a["L1_attn_bo"], a["L1_ffn_norm_w"]])),
        "qkb": np.concatenate([by_dim(a["L1_attn_bq"]).reshape(KD, P).T, by_dim(a["L1_attn_bk"]).reshape(KD, P).T], 1),
        "gbias": spread_rows(np.stack([pad16(a["L0_ffn_gate_b"]), pad16(a["L1_ffn_gate_b"]), pad16(a["L0_ffn_bias"])])),
        "gw": np.stack(gws, 1),
        "moe0": _mixture(a["L0_ffn_w1"], a["L0_ffn_w2"], 0, np),
        "moe1": _mixture(a["L1_ffn_w1"], a["L1_ffn_w2"], 1, np),
        "bias0": _biases(a["L0_ffn_b1"], a["L0_ffn_b2"], 0, np),
        "bias1": _biases(a["L1_ffn_b1"], a["L1_ffn_b2"], 1, np),
    }
    nc = bacc.Bacc("TRN2", target_bir_lowering=False, num_devices=1)
    arrays = {f"in_{k}_dram": np.ascontiguousarray(v) for k, v in arrays.items()}
    dram = {k[3:-5]: nc.dram_tensor(k, v.shape, mybir.dt.from_np(v.dtype), kind="ExternalInput").ap()
            for k, v in arrays.items()}
    out = nc.dram_tensor("out_dram", (T, D), F32, kind="ExternalOutput").ap()
    build_kernel(nc, dram, out)
    r = run_bass_kernel_spmd(nc, [arrays], core_ids=[0])
    return r.results[0]["out_dram"].reshape(B, S, D)
```

```python
from contextlib import ExitStack

import concourse.bass as bass
from concourse import mybir

P = 128
D = 256
KD = D // P
B = 2
S = 512
T = B * S
NT = T // P
TB = S // P
H = 16
HD = D // H
HG = 4
NG = B * H // HG
TERMS = 6
QSIDE = [0, 0, 1, 0, 2, 1]
KSIDE = [0, 1, 0, 2, 0, 1]
SROWS = TERMS * HD
MROWS = SROWS + 2
EPS = 1e-5
LN_CLAMP = 0.25
PK = [0, 512, 1024, 896]
PTW = 1280
BIG_NEG = -1e30

F32 = mybir.dt.float32
BF16 = mybir.dt.bfloat16
I32 = mybir.dt.int32
U32 = mybir.dt.uint32
ALU = mybir.AluOpType
ACT = mybir.ActivationFunctionType
AX = mybir.AxisListType

EXPERTS = [8, 16]
TOPK = [2, 4]
HB = [176, 512]
HK = [88, 128]
BIAS_ROWS = 96
HALF = 256
ALPHA = 1.702
LIMIT = 7.0
SLOTS_T = [(T * k - e) // P + e for e, k in zip(EXPERTS, TOPK)]
WROW = [2 * HB[l] + 2 * D for l in range(2)]
BROW = [HB[l] + D for l in range(2)]
TURNS = KD * B
UNROLL = 4
STEADY = 7
LAG = 7
PICKS_BEFORE = [0, SLOTS_T[0] + LAG]
POOL_STEADY = 11
TILES_BEFORE = [[16 * sum(len(range(r, n, 4)) for n in SLOTS_T[:l]) for r in range(4)] for l in range(3)]
CONST_W = P + 16 + 8 + 256 + 48 + P + NT + 1 + 48
MT = [24, 48]
BIG_W = 16 * WROW[1]


def build_kernel(nc, dram, out):
    with ExitStack() as ctx:
        def sb(name, shape, dt=F32):
            return ctx.enter_context(nc.sbuf_tensor(name, shape, dt))

        def sem(name):
            return ctx.enter_context(nc.semaphore(name))

        def sems(name, n=2):
            return [sem(f"{name}{i}") for i in range(n)]

        x = sb("x", [P, NT, D])
        big = sb("big", [P, BIG_W])
        ptm = sb("ptm", [P, 2 * HG * PTW])
        tok = sb("tok", [P, NT, D])
        feat = sb("feat", [P, KD, T])
        modbc = sb("modbc", [P, B, 4, D])
        parts = sb("parts", [P, 2, 2, 3, S], BF16)
        tok_flat = tok[:, :, :].rearrange("p t c -> p (t c)")
        qkf = tok_flat[:, 0:4 * S].rearrange("p (n t) -> p n t", n=4)
        wqkv = sb("wqkv", [P, KD, 3 * D])
        wo = sb("wo", [P, KD, D])
        ctxden = sb("ctxden", [P, 2, S])
        consts = sb("consts", [P, CONST_W])
        constb_f = ptm[:, 0:3 * P]
        constb = sb("constb", [P, 3, P], BF16)
        cT = sb("cT", [P, 2, KD, B])
        silc = sb("silc", [P, 2, KD, B])
        silb = ptm[:, 4096:4096 + KD * B * P].rearrange("p (k b n) -> p k b n", k=KD, b=B)
        modcol = sb("modcol", [P, 2, 4, B])
        rows = sb("rows", [P, 3, D])
        qkb = sb("qkb", [P, 4])
        qkb4 = sb("qkb4", [P, 4])
        gbias = sb("gbias", [P, 3, 16])
        gw = sb("gw", [P, 2, KD, 16])
        stats = sb("stats", [P, NT, 6])
        mv = sb("mv", [P, NT, 2])
        rstd = sb("rstd", [P, NT])
        vareps = sb("vareps", [P, NT])
        neghalf = sb("neghalf", [P, NT])
        sumsq = sb("sumsq", [P, NT])
        mx = sb("mx", [P, 2, 16])
        mneg = sb("mneg", [P, 2, 32], BF16)
        mT = sb("mT", [32, 2, P], BF16)
        rden = sb("rden", [P, 2, 16])
        tmp = sb("tmp", [P, 2, D])
        rest = tmp[:, :, :].rearrange("p a c -> p (a c)")
        parts_flat = parts[:, :, :, :, :].rearrange("p a b c d -> p (a b c d)")
        bfull = parts_flat[0:16, 0:2 * BROW[1]].bitcast(F32)
        bparts = parts_flat[0:16, 2 * BROW[1]:5 * BROW[1]].rearrange("p (r c) -> p r c", r=3)
        logit = sb("logit", [P, NT, 16])
        top8 = sb("top8", [P, NT, 8])
        idx8 = sb("idx8", [P, NT, 8], U32)
        idf = sb("idf", [P, NT, 4])
        feat_flat = feat[:, :, :].rearrange("p k t -> p (k t)")
        onehot = feat_flat[:, 0:NT * 4 * 16]
        picked = feat_flat[:, NT * 4 * 16:NT * 4 * 16 + 48 * 16]
        chosen = sb("chosen", [P, NT * 16], BF16)
        gate = sb("gate", [P, NT, 4])
        gexp = sb("gexp", [P, NT, 4])
        gsum = sb("gsum", [P, NT])
        grec = sb("grec", [P, NT])
        ntile = sb("ntile", [P, 16])
        excl = sb("excl", [P, 16])
        incl = sb("incl", [P, 16])
        slot = sb("slot", [P, NT * 16])
        slotf = sb("slotf", [P, NT * 4])
        place = sb("place", [P, NT * 4])
        first = sb("first", [P, NT * 4])
        slot_i = sb("slot_i", [P, NT * 4], I32)
        token_f = sb("token_f", [P, MT[1]])
        token = sb("token", [P, MT[1]], U32)
        weight = sb("weight", [P, MT[1]])
        indices = sb("indices", [P, 4, 2], U32)
        tef = sb("tef", [1, 48])
        te = sb("te", [1, MT[1] + 4, 2], I32)

        half = BIG_W // 2
        qr = big[:, half:half + 4096].bitcast(BF16).rearrange("p (r h t) -> p r h t", r=2, h=8)
        kr = big[:, half + 4096:half + 8192].bitcast(BF16).rearrange("p (r h t) -> p r h t", r=2, h=8)
        vaug = big[:, half + 8192:half + 12288].rearrange("p (t h c) -> p t h c", t=NT, h=H)
        pt = ptm[:, :].rearrange("p (r j c) -> p r j c", r=2, j=HG)
        moe0_w = EXPERTS[0] * WROW[0]
        assert moe0_w + KD * 6 * D <= half
        wmods = [ptm[:, 512:512 + KD * 6 * D].rearrange("p (k n) -> p k n", k=KD),
                 big[:, moe0_w:moe0_w + KD * 6 * D].rearrange("p (k n) -> p k n", k=KD)]
        zeros = sb("zeros", [P, D])
        brows_f = ptm[0:BIAS_ROWS, 0:16 * BROW[1] // 2]
        brows = ptm[:, 0:16 * BROW[1] // 2].bitcast(BF16)
        o = 16 * BROW[1] // 2
        xt = ptm[:, o:o + 4 * D].rearrange("p (r c) -> p r c", r=4)
        o += 4 * D
        xtT = ptm[:, o:o + 2 * D].rearrange("p (r k c) -> p r k c", r=2, k=KD)
        o += 2 * D
        hid = ptm[:, o:o + 2 * D].rearrange("p (r c) -> p r c", r=2)
        o += 2 * D
        hidT = ptm[:, o:o + 2 * D].rearrange("p (r k c) -> p r k c", r=2, k=KD)
        o += 2 * D
        yt = ptm[:, o:o + 4 * D].rearrange("p (r c) -> p r c", r=4)
        o += 4 * D
        assert o <= 2 * HG * PTW
        ga_ = qkf[:, 0:2, 0:D]
        gb_ = qkf[:, 0:2, D:2 * D]
        gs_ = ctxden[:, :, 0:D]
        gu_ = ctxden[:, :, D:2 * D]
        at_place = ptm[:, 6144:6144 + 4096]
        at_tile = parts[:, :, :, :, :].rearrange("p a b c d -> p (a b c d)").bitcast(F32)
        wo_gated = [wqkv[:, :, :].rearrange("p k c -> p (k c)")[:, TB * D:TB * D + KD * D].rearrange("p (k c) -> p k c", k=KD),
                    wo[:, :, :]]
        gb_next = ctxden[:, :, 0:D]
        normed = [wqkv[:, :, :].rearrange("p k c -> p (k c)")[:, 0:TB * D].rearrange("p (t c) -> p t c", t=TB),
                  ptm[:, 6144:6144 + TB * D].rearrange("p (t c) -> p t c", t=TB)]

        def mixture_input(l, b):
            return tok[:, b * TB:(b + 1) * TB, :] if l == 0 else normed[b]

        def in_tile(l, t):
            n = TOPK[l] * MT[l]
            room = ctxden[:, 0:2, :].rearrange("p a c -> p (a c)") if t < TB else feat_flat[:, 1280:2048]
            return room[:, t % TB * n:(t % TB + 1) * n].rearrange("p (n c) -> p n c", n=TOPK[l])

        def weighed_tile(l):
            n = NT * TOPK[l]
            return at_tile[:, 0:n * 2 * MT[l]].rearrange("p (n a c) -> p n a c", n=n, a=2)

        acc_in = ptm[:, 0:2 * NT * D].rearrange("p (a t c) -> p a t c", a=2, t=NT)

        ident = consts[:, 0:P]
        iota_e = consts[:, P:P + 16]
        c128 = consts[:, P + 16:P + 24]
        lower = consts[:, P + 24:P + 280].rearrange("p (a b) -> p a b", a=16)
        iota_t = consts[:, P + 280:P + 328]
        iota_t128 = consts[:, 2 * P + 329 + NT:2 * P + 377 + NT]
        iota_p = consts[:, P + 328:2 * P + 328]
        left = consts[:, 2 * P + 328:2 * P + 328 + NT]
        lane = consts[:, 2 * P + 328 + NT:2 * P + 329 + NT]
        ident_b = constb[:, 0, :]
        causal_b = constb[:, 1, :]
        before_b = constb[:, 2, :]
        ones_b = sb("ones_b", [P, P], BF16)

        bank = [ctx.enter_context(nc.psum_tensor(f"bank{i}", [P, 1024], F32)) for i in range(2)]
        bank += [ctx.enter_context(nc.psum_tensor(f"bank{i}", [P, 512], F32)) for i in range(2, 6)]
        ps = [bank[0][:, 0:512], bank[0][:, 512:1024], bank[1][:, 0:512], bank[1][:, 512:1024]]
        ps += [bank[i][:, :] for i in range(2, 6)]

        xs = [nc.dram_tensor(f"token_rows{l}", [T + P, D], F32, kind="Internal") for l in range(2)]
        acc = [[nc.dram_tensor(f"sums{l}_{a}", [T + P, D], F32, kind="Internal") for a in range(2)] for l in range(2)]

        ld_const = sem("ld_const")
        ld_constb = sem("ld_constb")
        ld_c = sem("ld_c")
        ones_set = sem("ones_set")
        rows_ps = sems("rows_ps")
        ld_x = sems("ld_x")
        ld_mod = sems("ld_mod")
        ld_mod_rows = sem("ld_mod_rows")
        ld_wqkv = sems("ld_wqkv")
        ld_wo = sems("ld_wo")
        ld_small = sem("ld_small")
        ld_bias = sems("ld_bias")
        ld_w_lo = sems("ld_w_lo")
        ld_w_hi = sem("ld_w_hi")
        zeroed = sem("zeroed")
        set_up = sem("set_up")
        silu_done = sem("silu_done")
        silb_done = sem("silb_done")
        mod_ps = sems("mod_ps")
        mod_sb = sems("mod_sb")
        qkb_done = sem("qkb_done")
        dve_own = sem("dve_own")
        pool_own = sem("pool_own")
        act_own = sem("act_own")
        var_ready = sems("var_ready")
        rstd_ready = sems("rstd_ready")
        xhat_ready = sems("xhat_ready")
        tr_ps = sems("tr_ps")
        feat_ready = sems("feat_ready")
        qkv_ps = sems("qkv_ps")
        qkf_ready = sems("qkf_ready")
        v_ready = sems("v_ready")
        parts_ready = sems("parts_ready")
        spread = sems("spread", 4)
        spread_by_pool = sems("spread_by_pool")
        a_ps = sems("a_ps")
        a_max = sems("a_max")
        m_ready = sems("m_ready")
        m_tr = sems("m_tr")
        mT_ready = sems("mT_ready")
        m_rows = [sems(f"m_rows{l}_") for l in range(2)]
        b_ps = sems("b_ps")
        b_exp = sems("b_exp")
        pv_ps = sems("pv_ps")
        ctxden_ready = sems("ctxden_ready")
        c_tr = sems("c_tr")
        ctx_ready = sems("ctx_ready")
        wo_ps = sems("wo_ps")
        wo_read = sems("wo_read")
        wo_scaled = sem("wo_scaled")
        bo_added = sem("bo_added")
        h_added = sem("h_added")
        gate_ps = sems("gate_ps")
        chosen_ready = sem("chosen_ready")
        gexp_in = sem("gexp_in")
        gexp_done = sem("gexp_done")
        rank_ps = sem("rank_ps")
        tokens_ready = sem("tokens_ready")
        slots_ready = sems("slots_ready")
        bparts_ready = sem("bparts_ready")
        brows_ready = sems("brows_ready")
        brows_zero = sem("brows_zero")
        rows_stored = sems("rows_stored")
        gate_ready = sem("gate_ready")
        tile_of = sems("tile_of")
        place_of = sems("place_of")
        tile_weighed = sems("tile_weighed")
        token_picked = sem("token_picked")
        placed_ps = sem("placed_ps")
        acc_loaded = sems("acc_loaded", 4)
        h_rows = sem("h_rows")
        combined = sem("combined")
        squared = sem("squared")
        rms_in = sem("rms_in")
        rms_out = sem("rms_out")
        tok_ready = sems("tok_ready")
        xt_loaded = sems("xt_loaded", 4)
        xT_ps = sems("xT_ps")
        xT_sb = sems("xT_sb")
        h_ps = sems("h_ps")
        h_read = sem("h_read")
        sig_in = sem("sig_in")
        sig_done = sem("sig_done")
        gu_done = sem("gu_done")
        hid_ready = sems("hid_ready")
        hT_ps = sems("hT_ps")
        hT_sb = sems("hT_sb")
        y_ps = sems("y_ps")
        y_sb = sems("y_sb")
        y_summed = sems("y_summed", 4)
        x_new = sems("x_new")
        stored = sem("stored")

        def moe_w1(l, k, e):
            v = big[:, 0:EXPERTS[l] * WROW[l]].rearrange("p (e c) -> p e c", e=EXPERTS[l])
            return v[:, bass.ds(e, 1), k * HB[l]:(k + 1) * HB[l]].rearrange("p a b -> p (a b)")

        def moe_w2(l, k, e):
            v = big[:, 0:EXPERTS[l] * WROW[l]].rearrange("p (e c) -> p e c", e=EXPERTS[l])
            lo = 2 * HB[l] + k * D
            return v[0:HK[l], bass.ds(e, 1), lo:lo + D].rearrange("p a b -> p (a b)")

        def moe_bias(l, lo, hi, e):
            v = brows[0:BIAS_ROWS, 0:EXPERTS[l] * BROW[l]].rearrange("p (e c) -> p e c", e=EXPERTS[l])
            return v[:, bass.ds(e, 1), lo:hi].rearrange("p a b -> p (a b)")

        A_CHUNKS = [(0, 0, 4), (1, 0, 4), (2, 0, 2), (2, 2, 2), (3, 0, 2), (3, 2, 2)]
        NA = len(A_CHUNKS)
        B_CHUNKS = []
        for j0 in (0, 2):
            B_CHUNKS += [[(j0, 0, 0)], [(j0, 1, 0), (j0, 3, 384)], [(j0 + 1, 0, 0)],
                         [(j0 + 1, 1, 0), (j0 + 1, 3, 384)], [(j0, 2, 0), (j0 + 1, 2, 256)]]
        NB = len(B_CHUNKS)

        def a_view(c):
            i, _, n = A_CHUNKS[c]
            w = (i + 1) * P
            full = bank[c % 2][:, :]
            if n == 4:
                return full[:, 0:4 * w].rearrange("p (j w) -> p j w", j=4)
            return full.rearrange("p (j w) -> p j w", j=2)[:, :, 0:w]


        rows_bank = [[ps[6], ps[7]], [ps[4], ps[5]]]
        gate_bank = [ps[6], ps[0]]

        def turned(l, which, n):
            if which == 1:
                return ps[n % 2]
            if (l, which) == (1, 0):
                return ps[(0, 1, 6, 7)[n]]
            return ps[4 + n % 2]

        def tile_at(ii, off):
            return 4 * ii + off, off % 4, ii + off // 4

        def qkv_fills():
            yield from (("q", 0, 0), ("k", 0, 0), ("v", 0, 0), ("v", 0, 1), ("q", 0, 1), ("k", 0, 1))
            yield from (("v", 1, 0), ("v", 1, 1), ("q", 1, 0), ("k", 1, 0), ("q", 1, 1), ("k", 1, 1))

        FILLS = list(qkv_fills())
        EARLY = 8

        TURN1 = 4
        FIRST_TURNED = [[0, 1], [0]]

        def fill_bank(n):
            return ps[n % 4] if n < EARLY else ps[4 + n % 2]

        def wait_fill_read(eng, l, n):
            kind = FILLS[n][0]
            before = [f[0] == "v" for f in FILLS[:n + 1]]
            if kind == "v":
                eng.wait_ge(v_ready[l], sum(before))
            else:
                eng.wait_ge(qkf_ready[l], len(before) - sum(before))

        def spread_unit(eng, issue, l, u, sides, done):
            if u >= 2:
                eng.wait_ge(b_ps[l], NB * 2 * (u - 1))
            elif l == 1:
                eng.wait_ge(b_ps[0], NB * NG)
            for n in sides:
                dst, side = ((qr, QSIDE), (kr, KSIDE))[n]
                eng.wait_ge(parts_ready[l], 2 * u + n + 1)
                for r in range(TERMS):
                    issue.dma_start(dst[r * HD:(r + 1) * HD, u % 2, :, :],
                                    parts[:, n, u % 2, side[r], :]).then_inc(done, 16)

        def wait_spread(eng, l, u):
            eng.wait_ge(spread[u], 16 * (2 if u < 2 else 1) * TERMS * (l + 1))
            if u >= 2:
                eng.wait_ge(spread_by_pool[u - 2], 16 * TERMS * (l + 1))

        block = ctx.enter_context(nc.Block())

        @block.sync
        def _(sp):
            nc.sync.dma_start(x[:, 0:TB, :], dram["x"][0:S, :].rearrange("(t p) c -> p t c", p=P)).then_inc(ld_x[0], 16)
            nc.sync.dma_start(cT[:, :, :, :].rearrange("p l k b -> p (l k b)"), dram["cT"]).then_inc(ld_c, 16)
            nc.sync.dma_start(wmods[0][:, :, 0:2 * D], dram["wmod"][0][:, :, 0:2 * D]).then_inc(ld_mod[0], 16)
            nc.sync.dma_start(wmods[0][:, :, 2 * D:6 * D], dram["wmod"][0][:, :, 2 * D:6 * D]).then_inc(ld_mod_rows, 16)
            nc.sync.dma_start(consts[:, :], dram["consts"]).then_inc(ld_const, 16)
            nc.sync.dma_start(x[:, TB:NT, :], dram["x"][S:T, :].rearrange("(t p) c -> p t c", p=P)).then_inc(ld_x[1], 16)
            nc.sync.dma_start(wqkv[:, :, :], dram["wqkv"][0]).then_inc(ld_wqkv[0], 16)
            nc.sync.dma_start(constb_f, dram["constb"]).then_inc(ld_constb, 16)
            nc.sync.dma_start(wo[:, :, :], dram["wo"][0]).then_inc(ld_wo[0], 16)
            nc.sync.dma_start(rows[:, :, :], dram["rows"]).then_inc(ld_small, 16)
            nc.sync.dma_start(qkb[:, :], dram["qkb"]).then_inc(ld_small, 16)
            nc.sync.dma_start(gbias[:, :, :], dram["gbias"]).then_inc(ld_small, 16)
            nc.sync.dma_start(gw[:, :, :, :], dram["gw"]).then_inc(ld_small, 16)
            def send_maxima(l, g):
                sp.wait_ge(mT_ready[l], g + 1)
                hl = (g % 2) * HG
                for r in range(2):
                    nc.sync.dma_start(
                        qr[SROWS + r:SROWS + r + 1, (g // 2) % 2, hl:hl + HG, :],
                        mT[r * 16:(r + 1) * 16, g % 2, :]).then_inc(m_rows[l][g % 2], 16)

            ZERO_AT = [0, 1, 5, 6]

            for l in range(2):
                spread_unit(sp, nc.sync, l, 0, (0, 1), spread[0])
                spread_unit(sp, nc.sync, l, 1, (0, 1), spread[1])
                if l == 0:
                    sp.wait_ge(set_up, 1)
                else:
                    sp.wait_ge(rows_ps[1], B)
                for g in range(NG):
                    if g in (3, 5):
                        u = (g + 1) // 2
                        spread_unit(sp, nc.sync, l, u, (1,), spread[u])
                    send_maxima(l, g)
                    piece = slice(g * WROW[l], (g + 1) * WROW[l])
                    nc.sync.dma_start(big[:, piece], dram[f"moe{l}"][:, piece]).then_inc(ld_w_lo[l], 16)
                    if l == 0 and g in ZERO_AT:
                        z = ZERO_AT.index(g)
                        nc.sync.dma_start(acc[z // 2][z % 2][:, :].rearrange("(t p) c -> p t c", p=P),
                                          zeros[:, :].unsqueeze(1).broadcast_to([P, NT + 1, D])).then_inc(zeroed, 16)
                    if l == 0 and g in (2, 7):
                        nc.sync.dma_start(xs[g // 4][T:T + P, :], zeros[:, :]).then_inc(zeroed, 16)
                for u in range(4):
                    wait_spread(sp, l, u)
                nc.sync.dma_start(bfull[0:EXPERTS[l], 0:BROW[l]], dram[f"bias{l}"]).then_inc(ld_bias[l], 16)
                if l == 1:
                    sp.wait_ge(pv_ps[1], NG)
                    nc.sync.dma_start(big[:, half:BIG_W], dram["moe1"][:, half:BIG_W]).then_inc(ld_w_hi, 16)
                else:
                    sp.wait_ge(wo_ps[0], NT // 4)
                    nc.sync.dma_start(wqkv[:, :, :], dram["wqkv"][1]).then_inc(ld_wqkv[1], 16)
                    nc.sync.dma_start(wmods[1], dram["wmod"][1]).then_inc(ld_mod[1], 16)
                sp.wait_ge(bparts_ready, l + 1)
                sp.wait_ge(brows_zero, l + 1)
                for r in range(3):
                    nc.sync.dma_start(
                        brows[r:r + 1, 0:EXPERTS[l] * BROW[l]].rearrange("p (e c) -> p e c", e=EXPERTS[l]),
                        bparts[0:EXPERTS[l], r, 0:BROW[l]]).then_inc(brows_ready[l], 16)
                for b in range(B):
                    sp.wait_ge(tok_ready[l], b + 1)
                    nc.sync.dma_start(xs[l][b * S:(b + 1) * S, :].rearrange("(t p) c -> p t c", p=P),
                                      mixture_input(l, b)).then_inc(rows_stored[l], 16)
                n = SLOTS_T[l]
                if l == 0:
                    sp.wait_ge(wo_ps[0], NT // 2)
                    nc.sync.dma_start(wo[:, :, :], dram["wo"][1]).then_inc(ld_wo[1], 16)
                sp.wait_ge(y_ps[l], n)
                for a in ((n - 2) % 2, (n - 1) % 2):
                    for r in (a, a + 2):
                        sp.wait_ge(y_summed[r], TILES_BEFORE[l + 1][r])
                    for m in (3, 0, 1, 2):
                        nc.sync.dma_start(acc_in[:, a, 2 * m:2 * m + 2, :],
                                          acc[l][a][2 * m * P:(2 * m + 2) * P, :].rearrange("(t p) c -> p t c", p=P)
                                          ).then_inc(acc_loaded[m], 16)
            for m in (0, 3, 1, 2):
                if m < NT // 2 - 1:
                    sp.wait_ge(x_new[1], m + 1)
                else:
                    sp.wait_ge(combined, 6)
                nc.sync.dma_start(out[2 * m * P:(2 * m + 2) * P, :].rearrange("(t p) c -> p t c", p=P),
                                  x[:, 2 * m:2 * m + 2, :]).then_inc(stored, 16)
            sp.wait_ge(stored, 16 * (NT // 2))

        @block.gpsimd
        def _(pool):
            nc.gpsimd.memset(zeros[:, :], 0.0).then_inc(set_up, 1)
            nc.gpsimd.memset(neghalf[:, :], -0.5).then_inc(pool_own, 1)
            pool.wait_ge(pool_own, 1)

            def inverse_root(l, which, b):
                pool.wait_ge(var_ready[l], B * which + b + 1)
                c = slice(b * TB, (b + 1) * TB)
                nc.gpsimd.tensor_tensor(rstd[:, c], vareps[:, c], neghalf[:, c], ALU.pow).then_inc(rstd_ready[l], 1)

            for l in range(2):
                inverse_root(l, 0, 0)
                inverse_root(l, 0, 1)
                if l == 0:
                    pool.wait_ge(rstd_ready[0], B)
                    nc.gpsimd.memset(kr[SROWS:MROWS, :, :, :], 1.0).then_inc(ones_set, 1)
                    pool.wait_ge(ones_set, 1)
                    nc.gpsimd.memset(vaug[:, :, :, HD:2 * HD], 1.0).then_inc(ones_set, 1)
                spread_unit(pool, nc.gpsimd, l, 2, (0,), spread_by_pool[0])
                spread_unit(pool, nc.gpsimd, l, 3, (0,), spread_by_pool[1])
                pool.wait_ge(ld_wo[l], 16)
                pool.wait_ge(qkv_ps[l], len(FILLS))
                pool.wait_ge(mod_sb[l], 1 + B)
                for b in range(B):
                    nc.gpsimd.tensor_tensor(wo_gated[b], wo[:, :, :],
                                            modbc[:, b, 0, :].unsqueeze(1).broadcast_to([P, KD, D]),
                                            ALU.mult).then_inc(wo_scaled, 1)
                    pool.wait_ge(wo_scaled, B * l + b + 1)
                if l == 1:
                    pool.wait_ge(ld_small, 64)
                    pool.wait_ge(mod_sb[1], 1 + B)
                    pool.wait_ge(xhat_ready[1], NT)
                    nc.gpsimd.tensor_tensor(tmp[:, :, :], modbc[:, :, 0, :], rows[:, 1, :].unsqueeze(1).broadcast_to([P, B, D]),
                                            ALU.mult).then_inc(pool_own, 1)
                    pool.wait_ge(pool_own, 2)
                    for b in range(B):
                        ins = nc.gpsimd.tensor_tensor(x[:, b * TB:(b + 1) * TB, :], x[:, b * TB:(b + 1) * TB, :],
                                                      tmp[:, b, :].unsqueeze(1).broadcast_to([P, TB, D]), ALU.add)
                    ins.then_inc(bo_added, 1)
                for b in range(B):
                    inverse_root(l, 1, b)
                    if l == 1:
                        c = slice(b * TB, (b + 1) * TB)
                        pool.wait_ge(rms_in, b + 1)
                        nc.gpsimd.tensor_tensor(rstd[:, c], vareps[:, c], neghalf[:, c], ALU.pow).then_inc(rms_out, 1)
                    if b == 0:
                        pool.wait_ge(pv_ps[l], NG)
                        if l == 0:
                            pool.wait_ge(rstd_ready[0], B + 1)
                        else:
                            pool.wait_ge(rms_out, 1)
                        nc.gpsimd.memset(brows_f[:, 0:EXPERTS[l] * BROW[l] // 2], 0.0).then_inc(brows_zero, 1)
                        pool.wait_ge(brows_zero, l + 1)
                if l == 1:
                    pool.wait_ge(tok_ready[1], B)
                    for b in range(B):
                        rng = slice(b * TB, (b + 1) * TB)
                        nc.gpsimd.tensor_tensor(tok[:, rng, :], tok[:, rng, :],
                                                modbc[:, b, 3, :].unsqueeze(1).broadcast_to([P, TB, D]),
                                                ALU.mult).then_inc(pool_own, 1)
                        pool.wait_ge(pool_own, 3 + b)
                        nc.gpsimd.tensor_tensor(x[:, rng, :], x[:, rng, :], tok[:, rng, :], ALU.add).then_inc(h_added, 1)
                def pick(ii, off):
                    i, r, _ = tile_at(ii, off)
                    n = SLOTS_T[l]
                    gathers, adds = takes_part(ii, off)
                    if gathers and adds:
                        src, dst = token[:, bass.ds(i - LAG, LAG + 1)][:, ::LAG], indices[:, r, :]
                    elif gathers:
                        src, dst = token[:, i:i + 1], indices[:, r, 1:2]
                    else:
                        src, dst = token[:, i - LAG:i - LAG + 1], indices[:, r, 0:1]
                    nc.gpsimd.tensor_copy(dst, src).then_inc(token_picked, 1)

                def takes_part(ii, off):
                    known, n = isinstance(ii, int), SLOTS_T[l]
                    return not known or off < n, not known or 0 <= off - LAG < n

                def gather(off):
                    r = off % 4
                    nc.gpsimd.indirect_dma_start(
                        out=xt[:, r, :], out_offset=None, in_=xs[l][:, :],
                        in_offset=bass.IndirectOffsetOnAxis(ap=indices[:, r, 1:2], axis=0)).then_inc(xt_loaded[r], 16)

                def add_rows(off):
                    r = off % 4
                    place_r = (off + LAG) % 4
                    nc.gpsimd.indirect_dma_start(
                        out=acc[l][off % 2][:, :],
                        out_offset=bass.IndirectOffsetOnAxis(ap=indices[:, place_r, 0:1], axis=0),
                        in_=yt[:, r, :], in_offset=None, compute_op=ALU.add).then_inc(y_summed[r], 16)

                def pool_step(ii, off):
                    gathers, adds = takes_part(ii, off)
                    i, _, _ = tile_at(ii, off)
                    pool.wait_ge(token_picked, PICKS_BEFORE[l] + i + 1)
                    if adds:
                        pool.wait_ge(y_sb[l], i - LAG + 1)
                        if not (isinstance(i, int) and i < LAG + 2):
                            _, r2, rnd2 = tile_at(ii, off - LAG - 2)
                            pool.wait_ge(y_summed[r2], TILES_BEFORE[l][r2] + 16 * rnd2 + 16)
                    if gathers and not (isinstance(i, int) and i < 3):
                        pool.wait_ge(xT_ps[l], i - 2)
                    if not isinstance(ii, int) or off + 1 < SLOTS_T[l] + LAG:
                        pick(ii, off + 1)
                    if gathers:
                        gather(off)
                    if adds:
                        add_rows(off - LAG)

                pool.wait_ge(zeroed, 16 * 6)
                pool.wait_ge(rows_stored[l], 16 * B)
                pool.wait_ge(tokens_ready, l + 1)
                pick(0, 0)
                for s in range(POOL_STEADY):
                    pool_step(0, s)
                with pool.Fori(0, (SLOTS_T[l] - POOL_STEADY) // UNROLL) as ii:
                    for q in range(UNROLL):
                        pool_step(ii, POOL_STEADY + q)
                for s in range(SLOTS_T[l], SLOTS_T[l] + LAG):
                    pool_step(0, s)
                m = NT // 2 - 1
                rng = slice(2 * m, 2 * m + 2)
                pool.wait_ge(acc_loaded[m], 32 * (l + 1))
                nc.gpsimd.tensor_tensor(acc_in[:, 0, rng, :], acc_in[:, 0, rng, :], acc_in[:, 1, rng, :],
                                        ALU.add).then_inc(combined, 1)
                pool.wait_ge(combined, 3 * l + 1)
                nc.gpsimd.tensor_tensor(acc_in[:, 0, rng, :], acc_in[:, 0, rng, :],
                                        modbc[:, 1, 3, :].unsqueeze(1).broadcast_to([P, 2, D]),
                                        ALU.mult).then_inc(combined, 1)
                pool.wait_ge(combined, 3 * l + 2)
                nc.gpsimd.tensor_tensor(x[:, rng, :], x[:, rng, :], acc_in[:, 0, rng, :], ALU.add).then_inc(combined, 1)

        @block.scalar
        def _(act):
            act.wait_ge(ld_c, 16)
            nc.scalar.activation(silc[:, :, :, :].rearrange("p l k b -> p (l k b)"),
                                 cT[:, :, :, :].rearrange("p l k b -> p (l k b)"), ACT.Silu).then_inc(silu_done, 1)

            def move_transposed(l, which, batches=range(B)):
                for b in batches:
                    for k in range(KD):
                        n = KD * b + k
                        if which == 0:
                            act.wait_ge(mod_sb[l], 1)
                        act.wait_ge(tr_ps[l], TURNS * which + n + 1)
                        dst, src = feat[:, k, b * S:(b + 1) * S], turned(l, which, n)
                        if which == 0:
                            nc.scalar.activation(dst, src, ACT.Identity, scale=modcol[:, l, 2 + k, b:b + 1],
                                                 bias=modcol[:, l, k, b:b + 1]).then_inc(feat_ready[l], 1)
                        else:
                            nc.scalar.activation(dst, src, ACT.Copy).then_inc(feat_ready[l], 1)

            for l in range(2):
                move_transposed(l, 0, FIRST_TURNED[l])
                if l == 1:
                    act.wait_ge(qkb_done, 1)

                def move_fill(n):
                    kind, b, u = FILLS[n]
                    if kind == "v" and l == 1:
                        return
                    act.wait_ge(qkv_ps[l], n + 1)
                    src = fill_bank(n)
                    if kind == "v":
                        t = b * TB + 2 * u
                        nc.scalar.activation(vaug[:, t:t + 2, :, 0:HD],
                                             src.rearrange("p (t h d) -> p t h d", t=2, h=H), ACT.Copy).then_inc(v_ready[l], 1)
                        return
                    m = sum(f[0] != "v" for f in FILLS[:n])
                    side = 0 if kind == "q" else 1
                    unit = 2 * b + u
                    scale = HD ** -0.5 if side == 0 else 1.0
                    bias = 0.0 if l == 0 else qkb4[:, 2 * side + u:2 * side + u + 1]
                    if m >= 4:
                        act.wait_ge(parts_ready[l], m - 3)
                    if unit >= 2:
                        wait_spread(act, l, unit - 2)
                    nc.scalar.activation(qkf[:, m % 4, :], src, ACT.Identity, scale=scale, bias=bias).then_inc(act_own, 1)
                    nc.scalar.activation(parts[:, side, unit % 2, 0, :], src, ACT.Identity, scale=scale,
                                         bias=bias).then_inc(qkf_ready[l], 1)

                for n in range(EARLY):
                    if n == TURN1 and l == 1:
                        move_transposed(1, 0, [1])
                    move_fill(n)

                def move_context(g):
                    act.wait_ge(pv_ps[l], g + 1)
                    if g >= 2:
                        act.wait_ge(c_tr[l], g - 1)
                    nc.scalar.activation(ctxden[:, g % 2, :], ps[6], ACT.Copy).then_inc(ctxden_ready[l], 1)

                for s in range(NG + 2):
                    if s == NG:
                        move_transposed(l, 1, [0])
                    if 0 <= s - 2 < NG:
                        move_context(s - 2)
                    if s == 0:
                        for n in range(EARLY, len(FILLS)):
                            move_fill(n)
                    g = s - 1
                    if not 0 <= g < NG:
                        continue
                    for c, pieces in enumerate(B_CHUNKS):
                        n = NB * g + c
                        if c == 0 and g >= 2:
                            act.wait_ge(pv_ps[l], g - 1)
                        act.wait_ge(b_ps[l], n + 1)
                        src = ps[4 + c % 2]
                        j, k, _ = pieces[0]
                        if k == 2:
                            dst = pt[:, g % 2, j:j + 2, PK[2]:PK[2] + 256]
                            src = src.rearrange("p (j q) -> p j q", j=2)
                        else:
                            dst = pt[:, g % 2, j, PK[k]:PK[k] + 512]
                        nc.scalar.activation(dst, src, ACT.Exp).then_inc(b_exp[l], 1)
                def sum_squares(b):
                    for t in range(b * TB, (b + 1) * TB):
                        act.wait_ge(h_rows, NT + t + 1)
                        nc.scalar.activation(normed[b][:, t % TB, :], tok[:, t, :], ACT.Square,
                                             accum_out=sumsq[:, t:t + 1]).then_inc(squared, 1)

                move_transposed(l, 1, [1])
                for b in range(B):
                    if l == 1:
                        sum_squares(b)
                    move_transposed(l, 2, [b])
                act.wait_ge(gexp_in, l + 1)
                nc.scalar.activation(gexp[:, :, 0:TOPK[l]], gexp[:, :, 0:TOPK[l]], ACT.Exp).then_inc(gexp_done, 1)

                K = TOPK[l]
                act.wait_ge(gate_ready, l + 1)
                act.wait_ge(brows_ready[l], 48)
                for t in range(NT):
                    act.wait_ge(tile_of[l], t + 1)
                    v = weighed_tile(l)
                    for k in range(K):
                        n = t * K + k
                        ins = nc.scalar.activation(v[:, n, 1, :], in_tile(l, t)[:, k, :], ACT.Copy, scale=gate[:, t, k:k + 1])
                    ins.then_inc(tile_weighed[l], 1)

                def act_x(ii, off):
                    i, _, _ = tile_at(ii, off)
                    act.wait_ge(xT_ps[l], i + 1)
                    if not (isinstance(i, int) and i < 2):
                        act.wait_ge(h_ps[l], i - 1)
                    nc.scalar.activation(xtT[:, off % 2, :, :].rearrange("p k c -> p (k c)"),
                                         ps[off % 2][:, 0:D], ACT.Copy).then_inc(xT_sb[l], 1)

                def act_hid(ii, off):
                    i, _, _ = tile_at(ii, off)
                    if l == 0:
                        act.wait_ge(h_ps[l], i + 1)
                        if not (isinstance(i, int) and i < 2):
                            act.wait_ge(hT_ps[l], i - 1)
                        nc.scalar.activation(hid[:, off % 2, 0:HB[0]], ps[2 + off % 2][:, 0:HB[0]],
                                             ACT.Silu).then_inc(hid_ready[l], 1)
                    else:
                        act.wait_ge(sig_in, i + 1)
                        nc.scalar.activation(gs_[:, off % 2, :], ga_[:, off % 2, :], ACT.Sigmoid,
                                             scale=ALPHA).then_inc(sig_done, 1)

                def act_hT(ii, off):
                    i, _, _ = tile_at(ii, off)
                    act.wait_ge(hT_ps[l], i + 1)
                    if not (isinstance(i, int) and i < 2):
                        act.wait_ge(y_ps[l], i - 1)
                    nc.scalar.activation(hidT[:, off % 2, :, :].rearrange("p k c -> p (k c)"),
                                         ps[4 + off % 2][:, 0:D], ACT.Copy).then_inc(hT_sb[l], 1)

                def act_y(ii, off):
                    i, r, rnd = tile_at(ii, off)
                    act.wait_ge(y_ps[l], i + 1)
                    if not (isinstance(i, int) and i < 4):
                        act.wait_ge(y_summed[r], TILES_BEFORE[l][r] + 16 * rnd)
                    nc.scalar.activation(yt[:, r, :], ps[6 + off % 2][:, 0:D], ACT.Copy,
                                         scale=weight[:, bass.ds(i, 1)]).then_inc(y_sb[l], 1)

                def act_step(ii, off):
                    n = SLOTS_T[l]
                    known = isinstance(ii, int)
                    if l == 1 and (not known or off < n):
                        act_x(ii, off)
                    if not known or 0 <= off - 1 < n:
                        act_hid(ii, off - 1)
                    if l == 1 and (not known or 0 <= off - 2 < n):
                        act_hT(ii, off - 2)
                    if not known or 0 <= off - 3 < n:
                        act_y(ii, off - 3)

                for s in range(STEADY):
                    act_step(0, s)
                with act.Fori(0, (SLOTS_T[l] - STEADY) // UNROLL) as ii:
                    for q in range(UNROLL):
                        act_step(ii, STEADY + q)
                for s in range(SLOTS_T[l], SLOTS_T[l] + 3):
                    act_step(0, s)

        @block.vector
        def _(dve):
            links = [0]

            def count(ins):
                links[0] += 1
                ins.then_inc(dve_own, 1)

            def settle():
                dve.wait_ge(dve_own, links[0])

            def link(ins):
                count(ins)
                settle()

            link(nc.vector.memset(ones_b[:, :], 1.0))
            link(nc.vector.memset(te[:, :, :], 0))

            def spread_silu(l):
                dve.wait_ge(silu_done, 1)
                nc.vector.tensor_copy(
                    silb.rearrange("p k b n -> p (k b) n"),
                    silc[:, l, :, :].rearrange("p k b -> p (k b)").unsqueeze(2).broadcast_to([P, KD * B, P]),
                ).then_inc(silb_done, 1)

            def modulation_columns(l):
                dve.wait_ge(mod_ps[l], 1)
                link(nc.vector.tensor_copy(modcol[:, l, 0:2, :].rearrange("p c b -> p (c b)"), ps[7][:, 0:4]))
                nc.vector.tensor_scalar(modcol[:, l, 2:4, :].rearrange("p c b -> p (c b)"), ps[7][:, 4:8], 1.0,
                                        None, ALU.add).then_inc(mod_sb[l], 1)

            def modulation_rows(l, b):
                dve.wait_ge(rows_ps[l], b + 1)
                lo, hi = rows_bank[b]
                gates = ((lo[:, 0:D], modbc[:, b, 0, :]), (hi[:, D:2 * D], modbc[:, b, 3, :] if l == 0 else gb_next[:, b, :]))
                for r, (src, _) in enumerate(gates):
                    count(nc.vector.tensor_scalar(tmp[:, r, :], src, 0.0, 2.0, ALU.is_ge, ALU.mult))
                settle()
                link(nc.vector.tensor_scalar(tmp[:, :, :], tmp[:, :, :], 1.0, None, ALU.subtract))
                for r, (src, dst) in enumerate(gates):
                    count(nc.vector.tensor_tensor(dst, src, tmp[:, r, :], ALU.mult))
                settle()
                for r, (_, dst) in enumerate(gates):
                    count(nc.vector.scalar_tensor_tensor(dst, dst, LN_CLAMP, tmp[:, r, :], ALU.max, ALU.mult))
                count(nc.vector.tensor_copy(modbc[:, b, 1, :], lo[:, D:2 * D]))
                count(nc.vector.tensor_scalar(modbc[:, b, 2, :], hi[:, 0:D], 1.0, None, ALU.add))
                settle()
                dve.sem_inc(mod_sb[l], 1)

            def statistics(l, which, b):
                for t in range(b * TB, (b + 1) * TB):
                    count(nc.vector.bn_stats(stats[:, t, :], x[:, t, :]))
                settle()
                for t in range(b * TB, (b + 1) * TB):
                    count(nc.vector.bn_aggr(mv[:, t, :], stats[:, t, :]))
                settle()
                c = slice(b * TB, (b + 1) * TB)
                nc.vector.tensor_scalar(vareps[:, c], mv[:, c, 1], EPS, None, ALU.add).then_inc(var_ready[l], 1)

            def normalise(l, which, b):
                statistics(l, which, b)
                if (l, b) == (0, 0):
                    modulation_columns(0)
                dve.wait_ge(rstd_ready[l], B * which + b + 1)
                for t in range(b * TB, (b + 1) * TB):
                    nc.vector.tensor_scalar(tok[:, t, :], x[:, t, :], mv[:, t, 0:1], rstd[:, t:t + 1],
                                            ALU.subtract, ALU.mult).then_inc(xhat_ready[l], 1)
                dve.wait_ge(xhat_ready[l], (b + 1) * TB)

            spread_silu(0)
            for l in range(2):
                if l == 1:
                    dve.wait_ge(ld_small, 64)
                    link(nc.vector.tensor_scalar(qkb4[:, 0:2], qkb[:, 0:2], HD ** -0.5, None, ALU.mult))
                    nc.vector.tensor_copy(qkb4[:, 2:4], qkb[:, 2:4]).then_inc(qkb_done, 1)
                if l == 0:
                    for b in range(B):
                        dve.wait_ge(ld_x[b], 16)
                        normalise(0, 0, b)
                    modulation_rows(0, 0)
                    dve.wait_ge(ld_constb, 16)
                    link(nc.vector.tensor_copy(constb[:, :, :].rearrange("p a c -> p (a c)"), constb_f))
                def split_fill(n):
                    kind, b, u = FILLS[n]
                    if kind == "v":
                        if l == 1:
                            dve.wait_ge(qkv_ps[l], n + 1)
                            t = b * TB + 2 * u
                            for half_t in range(2):
                                ins = nc.vector.tensor_tensor(
                                    vaug[:, t + half_t, :, 0:HD],
                                    fill_bank(n)[:, half_t * D:(half_t + 1) * D].rearrange("p (h d) -> p h d", h=H),
                                    rows[:, 0, :].rearrange("p (h d) -> p h d", h=H), ALU.add)
                            ins.then_inc(v_ready[l], 1)
                        return
                    m = sum(f[0] != "v" for f in FILLS[:n])
                    side, r = (0 if kind == "q" else 1), (2 * b + u) % 2
                    dve.wait_ge(qkf_ready[l], m + 1)
                    link(nc.vector.tensor_tensor(rest, qkf[:, m % 4, :], parts[:, side, r, 0, :], ALU.subtract))
                    link(nc.vector.tensor_copy(parts[:, side, r, 1, :], rest))
                    nc.vector.tensor_tensor(parts[:, side, r, 2, :], rest, parts[:, side, r, 1, :],
                                            ALU.subtract).then_inc(parts_ready[l], 1)
                    dve.wait_ge(parts_ready[l], m + 1)

                for n in range(EARLY):
                    split_fill(n)
                    if n == 3:
                        modulation_rows(l, 1)
                        if l == 1:
                            link(nc.vector.tensor_copy(modbc[:, :, 3, :], gb_next[:, :, :]))

                def split_biases():
                    dve.wait_ge(ld_bias[l], 16)
                    bf = bfull[0:EXPERTS[l], 0:BROW[l]]
                    bp = [bparts[0:EXPERTS[l], r, 0:BROW[l]] for r in range(3)]
                    link(nc.vector.tensor_copy(bp[0], bf))
                    link(nc.vector.tensor_tensor(bf, bf, bp[0], ALU.subtract))
                    link(nc.vector.tensor_copy(bp[1], bf))
                    nc.vector.tensor_tensor(bp[2], bf, bp[1], ALU.subtract).then_inc(bparts_ready, 1)

                def residual(b):
                    if l == 1:
                        dve.wait_ge(bo_added, 1)
                    for m in range(2):
                        dve.wait_ge(wo_ps[l], 2 * b + m + 1)
                        src = ps[2 + m].rearrange("p (t c) -> p t c", t=2)
                        t = b * TB + 2 * m
                        nc.vector.tensor_tensor(x[:, t:t + 2, :], x[:, t:t + 2, :], src, ALU.add).then_inc(wo_read[l], 1)
                    dve.wait_ge(wo_read[l], 2 * b + 2)

                def centre(b):
                    dve.wait_ge(tr_ps[l], TURNS * 1 + KD * (b + 1))
                    statistics(l, 1, b)
                    for t in range(b * TB, (b + 1) * TB):
                        count(nc.vector.scalar_tensor_tensor(tok[:, t, :], x[:, t, :], mv[:, t, 0:1], modbc[:, b, 2, :],
                                                             ALU.subtract, ALU.mult))

                def second_norm(b):
                    batch = range(b * TB, (b + 1) * TB)
                    rng = slice(b * TB, (b + 1) * TB)
                    dve.wait_ge(rstd_ready[l], B + b + 1)
                    settle()
                    for t in batch:
                        nc.vector.scalar_tensor_tensor(tok[:, t, :], tok[:, t, :], rstd[:, t:t + 1], modbc[:, b, 1, :],
                                                       ALU.mult, ALU.add).then_inc(h_rows, 1)
                    dve.wait_ge(h_rows, NT * l + (b + 1) * TB)
                    if l == 1:
                        dve.wait_ge(squared, (b + 1) * TB)
                        nc.vector.tensor_scalar(vareps[:, rng], sumsq[:, rng], 1.0 / D, EPS, ALU.mult,
                                                ALU.add).then_inc(rms_in, 1)
                        dve.wait_ge(rms_out, b + 1)
                        for t in batch:
                            count(nc.vector.scalar_tensor_tensor(normed[b][:, t % TB, :], tok[:, t, :], rstd[:, t:t + 1],
                                                                 rows[:, 2, :], ALU.mult, ALU.mult))
                        settle()
                    dve.sem_inc(tok_ready[l], 1)

                def maxima(g, c):
                    dve.wait_ge(a_ps[l], NA * g + c + 1)
                    i, j0, n = A_CHUNKS[c]
                    if c == 0 and g >= 2:
                        dve.wait_ge(m_ready[l], g - 1)
                    nc.vector.tensor_reduce(mx[:, g % 2, :].rearrange("p (j i) -> p j i", j=HG)[:, j0:j0 + n, i], a_view(c), AX.X,
                                            ALU.max).then_inc(a_max[l], 1)

                def split_maxima(g):
                    dve.wait_ge(a_max[l], NA * (g + 1))
                    link(nc.vector.tensor_scalar(mneg[:, g % 2, 0:16], mx[:, g % 2, :], -1.0, None, ALU.mult))
                    nc.vector.scalar_tensor_tensor(mneg[:, g % 2, 16:32], mx[:, g % 2, :], -1.0, mneg[:, g % 2, 0:16],
                                                   ALU.mult, ALU.subtract).then_inc(m_ready[l], 1)

                def move_maxima(g):
                    dve.wait_ge(m_tr[l], g + 1)
                    if g >= 2:
                        dve.wait_ge(m_rows[l][g % 2], 32 * (g // 2))
                    nc.vector.tensor_copy(mT[:, g % 2, :], ps[7][0:32, 0:P // 2].bitcast(BF16)).then_inc(mT_ready[l], 1)

                def context(g):
                    dve.wait_ge(c_tr[l], g + 1)
                    view = ps[7].rearrange("p (t j c) -> p t j c", t=TB, j=HG)
                    rd = rden[:, g % 2, :].rearrange("p (t j) -> p t j", t=TB)
                    link(nc.vector.reciprocal(rd, view[:, :, :, HD]))
                    b, hg = g // 4, g % 4
                    nc.vector.tensor_tensor(
                        tok[:, b * TB:(b + 1) * TB, hg * 64:(hg + 1) * 64].rearrange("p t (j d) -> p t j d", j=HG),
                        view[:, :, :, 0:HD], rd.unsqueeze(3).broadcast_to([P, TB, HG, HD]),
                        ALU.mult).then_inc(ctx_ready[l], 1)

                for s in range(NG + 2):
                    if s < NG:
                        maxima(s, 0)
                    if 1 <= s - 1 < NG:
                        move_maxima(s - 1)
                    if s < NG:
                        maxima(s, 1)
                        maxima(s, 2)
                    if 1 <= s <= len(FILLS) - EARLY:
                        split_fill(EARLY + s - 1)
                    if 0 <= s - 2 < NG:
                        context(s - 2)
                    if s < NG:
                        for c in range(3, NA):
                            maxima(s, c)
                        split_maxima(s)
                    if s == 0:
                        move_maxima(0)
                    if s == NG:
                        split_biases()
                        residual(0)
                        centre(0)

                second_norm(0)
                residual(1)
                centre(1)
                second_norm(1)

                E, K = EXPERTS[l], TOPK[l]
                if l == 0:
                    dve.wait_ge(ld_small, 64)
                oh = onehot[:, 0:NT * K * E].rearrange("p (t k e) -> p t k e", t=NT, k=K)
                ch = chosen[:, 0:NT * E].rearrange("p (t e) -> p t e", t=NT)
                for b in range(B):
                    dve.wait_ge(gate_ps[l], b + 1)
                    rng = slice(b * TB, (b + 1) * TB)
                    src = gate_bank[b][:, 0:NT * 16].rearrange("p (t e) -> p t e", t=NT)[:, rng, 0:E]
                    link(nc.vector.tensor_tensor(logit[:, rng, 0:E], src,
                                                 gbias[:, l, 0:E].unsqueeze(1).broadcast_to([P, TB, E]), ALU.add))
                    if l == 0:
                        link(nc.vector.tensor_tensor(logit[:, rng, 0:E], logit[:, rng, 0:E],
                                                     gbias[:, 2, 0:E].unsqueeze(1).broadcast_to([P, TB, E]), ALU.add))
                    for t in range(b * TB, (b + 1) * TB):
                        count(nc.vector.max(top8[:, t, :], logit[:, t, 0:E]))
                    settle()
                    for t in range(b * TB, (b + 1) * TB):
                        count(nc.vector.max_index(idx8[:, t, :], top8[:, t, :], logit[:, t, 0:E]))
                    settle()
                    link(nc.vector.tensor_copy(idf[:, rng, 0:K], idx8[:, rng, 0:K]))
                    link(nc.vector.tensor_tensor(
                        oh[:, rng], idf[:, rng, 0:K].unsqueeze(3).broadcast_to([P, TB, K, E]),
                        iota_e[:, 0:E].unsqueeze(1).unsqueeze(1).broadcast_to([P, TB, K, E]), ALU.is_equal))
                    with nc.allow_low_precision(reason="zeros and ones"):
                        nc.vector.tensor_reduce(ch[:, rng], oh[:, rng].rearrange("p t k e -> p t e k"), AX.X,
                                                ALU.add).then_inc(chosen_ready, 1)
                gk = gexp[:, :, 0:K]
                nc.vector.tensor_tensor(gk, top8[:, :, 0:K], top8[:, :, 0:1].broadcast_to([P, NT, K]),
                                        ALU.subtract).then_inc(gexp_in, 1)
                dve.wait_ge(gexp_done, l + 1)
                link(nc.vector.tensor_reduce(gsum[:, :], gk, AX.X, ALU.add))
                link(nc.vector.reciprocal(grec[:, :], gsum[:, :]))
                nc.vector.tensor_tensor(gate[:, :, 0:K], gk, grec[:, :].unsqueeze(2).broadcast_to([P, NT, K]),
                                        ALU.mult).then_inc(gate_ready, 1)
                dve.wait_ge(rank_ps, l + 1)
                pk = picked[:, 0:E * 8].rearrange("p (e c) -> p e c", e=E)
                link(nc.vector.tensor_tensor(pk, ps[5][:, 0:E].unsqueeze(2).broadcast_to([P, E, 8]),
                                             c128.unsqueeze(1).broadcast_to([P, E, 8]), ALU.is_gt))
                link(nc.vector.tensor_reduce(ntile[:, 0:E], pk, AX.X, ALU.add))
                pk = picked[:, 0:E * E].rearrange("p (a b) -> p a b", a=E)
                link(nc.vector.tensor_tensor(pk, ntile[:, 0:E].unsqueeze(1).broadcast_to([P, E, E]), lower[:, 0:E, 0:E], ALU.mult))
                link(nc.vector.tensor_reduce(excl[:, 0:E], pk, AX.X, ALU.add))
                sl = slot[:, 0:NT * E].rearrange("p (t e) -> p t e", t=NT)
                link(nc.vector.scalar_tensor_tensor(
                    sl, excl[:, 0:E].unsqueeze(1).broadcast_to([P, NT, E]), float(P),
                    ps[7][:, 0:NT * E].rearrange("p (t e) -> p t e", t=NT), ALU.mult, ALU.add))
                pk = picked[:, 0:NT * K * E].rearrange("p (t k e) -> p t k e", t=NT, k=K)
                at_p = at_place[:, 0:NT * K * P].rearrange("p (n c) -> p n c", n=NT * K)
                n = SLOTS_T[l]
                for b in range(B):
                    rng, c = slice(b * TB, (b + 1) * TB), slice(b * TB * K, (b + 1) * TB * K)
                    link(nc.vector.tensor_tensor(pk[:, rng], oh[:, rng], sl[:, rng].unsqueeze(2).broadcast_to([P, TB, K, E]),
                                                 ALU.mult))
                    link(nc.vector.tensor_reduce(slotf[:, c], pk[:, rng].rearrange("p t k e -> p (t k) e"), AX.X, ALU.add))
                    link(nc.vector.tensor_copy(slot_i[:, c], slotf[:, c]))
                    link(nc.vector.tensor_scalar(slot_i[:, c], slot_i[:, c], P - 1, None, ALU.bitwise_and))
                    link(nc.vector.tensor_copy(place[:, c], slot_i[:, c]))
                    link(nc.vector.tensor_tensor(first[:, c], slotf[:, c], place[:, c], ALU.subtract))
                    if b == 0:
                        dve.wait_ge(brows_ready[l], 48)
                    if l == 1 and b == 0:
                        dve.wait_ge(rows_stored[1], 16 * B)
                        dve.wait_ge(tr_ps[1], TURNS * 2 + KD * B)
                    for t in range(b * TB, (b + 1) * TB):
                        c = slice(t * K, (t + 1) * K)
                        nc.vector.tensor_tensor(
                            in_tile(l, t), first[:, c].unsqueeze(2).broadcast_to([P, K, MT[l]]),
                            iota_t128[:, 0:MT[l]].unsqueeze(1).broadcast_to([P, K, MT[l]]),
                            ALU.is_equal).then_inc(tile_of[l], 1)
                        nc.vector.tensor_tensor(
                            at_p[:, c, :], place[:, c].unsqueeze(2).broadcast_to([P, K, P]),
                            iota_p.unsqueeze(1).broadcast_to([P, K, P]), ALU.is_equal)
                        dve.wait_ge(tile_of[l], t + 1)
                        nc.vector.tensor_scalar(weighed_tile(l)[:, c, 0, :], in_tile(l, t), left[:, t:t + 1], None,
                                                ALU.mult).then_inc(place_of[l], 1)
                pk = picked[0:1, 0:n * E].rearrange("p (t e) -> p t e", t=n)
                link(nc.vector.tensor_tensor(incl[:, 0:E], excl[:, 0:E], ntile[:, 0:E], ALU.add))
                link(nc.vector.tensor_tensor(pk, iota_t[0:1, 0:n].unsqueeze(2).broadcast_to([1, n, E]),
                                             incl[0:1, 0:E].unsqueeze(1).broadcast_to([1, n, E]), ALU.is_ge))
                dve.wait_ge(placed_ps, l + 1)
                sums = ps[4][:, 0:2 * MT[l]].rearrange("p (a c) -> p a c", a=2)
                w = slice(0, MT[l])
                count(nc.vector.tensor_copy(weight[:, w], sums[:, 1, :]))
                link(nc.vector.tensor_scalar(token_f[:, w], sums[:, 0, :], 0.0, lane[:, 0:1], ALU.is_equal, ALU.mult))
                link(nc.vector.tensor_tensor(token_f[:, w], token_f[:, w], sums[:, 0, :], ALU.subtract))
                nc.vector.tensor_scalar(token[:, w], token_f[:, w], float(T), None, ALU.add).then_inc(tokens_ready, 1)
                link(nc.vector.tensor_reduce(tef[:, 0:n], pk, AX.X, ALU.add))
                link(nc.vector.tensor_scalar(tef[:, 0:n], tef[:, 0:n], float(E - 1), None, ALU.min))
                for r, behind in enumerate((1, 3)):
                    link(nc.vector.tensor_copy(te[:, behind:behind + n, r], tef[:, 0:n]))
                dve.sem_inc(slots_ready[l], 1)

                if l == 0:
                    spread_silu(1)

                else:
                    dve.wait_ge(h_added, B)

                def dve_x(ii, off):
                    i, _, _ = tile_at(ii, off)
                    dve.wait_ge(xT_ps[l], i + 1)
                    if not (isinstance(i, int) and i < 2):
                        dve.wait_ge(h_ps[l], i - 1)
                    nc.vector.tensor_copy(xtT[:, off % 2, :, :].rearrange("p k c -> p (k c)"),
                                          ps[off % 2][:, 0:D]).then_inc(xT_sb[l], 1)

                def dve_hT(ii, off):
                    i, _, _ = tile_at(ii, off)
                    dve.wait_ge(hT_ps[l], i + 1)
                    if not (isinstance(i, int) and i < 2):
                        dve.wait_ge(y_ps[l], i - 1)
                    nc.vector.tensor_copy(hidT[0:HK[0], off % 2, :, :].rearrange("p k c -> p (k c)"),
                                          ps[4 + off % 2][0:HK[0], 0:D]).then_inc(hT_sb[l], 1)

                def dve_gate(ii, off):
                    i, _, _ = tile_at(ii, off)
                    r = off % 2
                    early = isinstance(i, int) and i < 2
                    dve.wait_ge(h_ps[l], i + 1)
                    if not early:
                        dve.wait_ge(hid_ready[l], i - 1)
                        dve.wait_ge(hT_ps[l], i - 1)
                    nc.vector.tensor_scalar(ga_[:, r, :], ps[2 + r][:, 0:HALF], LIMIT, None, ALU.min).then_inc(sig_in, 1)
                    nc.vector.tensor_scalar(gb_[:, r, :], ps[2 + r][:, HALF:2 * HALF], LIMIT, -LIMIT, ALU.min,
                                            ALU.max).then_inc(h_read, 1)
                    dve.wait_ge(h_read, i + 1)
                    nc.vector.scalar_tensor_tensor(gu_[:, r, :], gb_[:, r, :], 1.0, ga_[:, r, :], ALU.add,
                                                   ALU.mult).then_inc(gu_done, 1)
                    dve.wait_ge(gu_done, i + 1)
                    dve.wait_ge(sig_done, i + 1)
                    nc.vector.tensor_tensor(hid[:, r, :], gu_[:, r, :], gs_[:, r, :], ALU.mult).then_inc(hid_ready[l], 1)

                def dve_step(ii, off):
                    n = SLOTS_T[l]
                    known = isinstance(ii, int)
                    if l == 0:
                        if not known or off < n:
                            dve_x(ii, off)
                        if not known or 0 <= off - 2 < n:
                            dve_hT(ii, off - 2)
                    elif not known or 0 <= off - 1 < n:
                        dve_gate(ii, off - 1)

                for s in range(STEADY):
                    dve_step(0, s)
                with dve.Fori(0, (SLOTS_T[l] - STEADY) // UNROLL) as ii:
                    for q in range(UNROLL):
                        dve_step(ii, STEADY + q)
                for s in range(SLOTS_T[l], SLOTS_T[l] + 3):
                    dve_step(0, s)

                if l == 0:
                    modulation_columns(1)
                    modulation_rows(1, 0)
                for m in range(NT // 2):
                    b = m // 2
                    rng = slice(2 * m, 2 * m + 2)
                    if m == NT // 2 - 1:
                        dve.wait_ge(combined, 3 * (l + 1))
                    else:
                        dve.wait_ge(acc_loaded[m], 32 * (l + 1))
                        if l == 1:
                            dve.wait_ge(h_added, b + 1)
                        link(nc.vector.tensor_tensor(acc_in[:, 0, rng, :], acc_in[:, 0, rng, :], acc_in[:, 1, rng, :],
                                                     ALU.add))
                        link(nc.vector.tensor_tensor(acc_in[:, 0, rng, :], acc_in[:, 0, rng, :],
                                                     modbc[:, b, 3, :].unsqueeze(1).broadcast_to([P, 2, D]), ALU.mult))
                        nc.vector.tensor_tensor(x[:, rng, :], x[:, rng, :], acc_in[:, 0, rng, :],
                                                ALU.add).then_inc(x_new[l], 1)
                        dve.wait_ge(x_new[l], m + 1)
                    if l == 0 and m % 2 == 1:
                        normalise(1, 0, b)

        @block.tensor
        def _(pe):
            def modulation_columns(l):
                pe.wait_ge(ld_mod[l], 16)
                pe.wait_ge(silb_done, l + 1)
                if l == 1:
                    pe.wait_ge(y_sb[0], SLOTS_T[0])
                for c in range(4):
                    for k in range(KD):
                        last = nc.tensor.matmul(ps[7][:, 2 * c:2 * c + 2], wmods[l][:, k, c * P:(c + 1) * P], silc[:, l, k, :],
                                                start=(k == 0), stop=(k == KD - 1))
                last.then_inc(mod_ps[l], 1)

            def modulation_rows(l, b):
                if b == 0:
                    if l == 0:
                        pe.wait_ge(ld_mod_rows, 16)
                    pe.wait_ge(mod_sb[l], 1)
                elif l == 0:
                    pe.wait_ge(feat_ready[0], TURNS)
                else:
                    pe.wait_ge(hT_sb[0], SLOTS_T[0])
                for h in range(2):
                    for k in range(KD):
                        last = nc.tensor.matmul(rows_bank[b][h], silb[:, k, b, :],
                                                wmods[l][:, k, (h + 1) * 512:(h + 2) * 512],
                                                start=(k == 0), stop=(k == KD - 1))
                last.then_inc(rows_ps[l], 1)

            def turn_batch(l, which, b, ready, count):
                src = mixture_input(l, b) if which == 2 else tok[:, b * TB:(b + 1) * TB, :]
                pe.wait_ge(ready, count * (b + 1))
                for k in range(KD):
                    n = KD * b + k
                    if n >= 2:
                        pe.wait_ge(feat_ready[l], TURNS * which + n - 1)
                    for i in range(TB):
                        last = nc.tensor.transpose(turned(l, which, n)[:, i * P:(i + 1) * P],
                                                   src[:, i, k * P:(k + 1) * P], ident)
                    last.then_inc(tr_ps[l], 1)

            def project(l, b):
                pe.wait_ge(wo_scaled, B * (l + 1))
                pe.wait_ge(feat_ready[l], TURNS * 1 + KD * (b + 1))
                for m in range(2):
                    if b == 1:
                        pe.wait_ge(wo_read[l], m + 1)
                    for half_t in range(2):
                        t = b * TB + 2 * m + half_t
                        for k in range(KD):
                            last = nc.tensor.matmul(ps[2 + m][:, half_t * D:(half_t + 1) * D],
                                                    feat[:, k, t * P:(t + 1) * P], wo_gated[b][:, k, :],
                                                    start=(k == 0), stop=(k == KD - 1))
                    last.then_inc(wo_ps[l], 1)

            for l in range(2):
                modulation_columns(l)
                pe.wait_ge(ld_const, 16)
                if l == 0:
                    turn_batch(0, 0, 0, xhat_ready[0], TB)
                    modulation_rows(0, 0)
                    turn_batch(0, 0, 1, xhat_ready[0], TB)
                else:
                    modulation_rows(1, 0)
                    modulation_rows(1, 1)
                    pe.wait_ge(xT_sb[0], SLOTS_T[0])
                    turn_batch(1, 0, 0, xhat_ready[1], TB)
                pe.wait_ge(ld_wqkv[l], 16)
                if l == 1:
                    pe.wait_ge(xT_sb[0], SLOTS_T[0])
                    pe.wait_ge(hid_ready[0], SLOTS_T[0])
                def fill(n):
                    kind, b, u = FILLS[n]
                    if 4 <= n < EARLY:
                        wait_fill_read(pe, l, n - 4)
                    if n >= EARLY:
                        if n < EARLY + 2:
                            pe.wait_ge(mod_sb[l], 1 + B)
                        else:
                            wait_fill_read(pe, l, n - 2)
                    pe.wait_ge(feat_ready[l], KD * (b + 1))
                    if kind == "v":
                        for half_t in range(2):
                            t = b * TB + 2 * u + half_t
                            for k in range(KD):
                                last = nc.tensor.matmul(fill_bank(n)[:, half_t * D:(half_t + 1) * D],
                                                        feat[:, k, t * P:(t + 1) * P], wqkv[:, k, 2 * D:3 * D],
                                                        start=(k == 0), stop=(k == KD - 1))
                    else:
                        lo = (0 if kind == "q" else D) + u * P
                        for k in range(KD):
                            last = nc.tensor.matmul(fill_bank(n), wqkv[:, k, lo:lo + P], feat[:, k, b * S:(b + 1) * S],
                                                    start=(k == 0), stop=(k == KD - 1))
                    last.then_inc(qkv_ps[l], 1)

                for n in range(EARLY):
                    if l == 1 and n == TURN1:
                        pe.wait_ge(mod_sb[1], 2)
                        turn_batch(1, 0, 1, xhat_ready[1], TB)
                    fill(n)
                    if l == 0 and n == 3:
                        modulation_rows(0, 1)
                for n in range(4, EARLY):
                    wait_fill_read(pe, l, n)

                def scores_by_query(g, c):
                    i, j0, heads = A_CHUNKS[c]
                    u = g // 2
                    wait_spread(pe, l, u)
                    if NA * g + c >= 2:
                        pe.wait_ge(a_max[l], NA * g + c - 1)
                    w = (i + 1) * P
                    dst = a_view(c)
                    for j in range(heads):
                        hl = (g % 2) * HG + j0 + j
                        nc.tensor.matmul(dst[:, j, :], qr[0:SROWS, u % 2, hl, i * P:(i + 1) * P],
                                         kr[0:SROWS, u % 2, hl, 0:w], start=True, stop=False)
                        last = nc.tensor.matmul(dst[:, j, w - P:w], ident_b, causal_b, start=False, stop=True)
                    last.then_inc(a_ps[l], 1)

                def scores_by_key(g, c):
                    u = g // 2
                    n = NB * g + c
                    if c == 0:
                        pe.wait_ge(m_rows[l][g % 2], 32 * (g // 2 + 1))
                        if g == 0:
                            wait_fill_read(pe, l, len(FILLS) - 1)
                    if n >= 2:
                        pe.wait_ge(b_exp[l], n - 1)
                    for j, k, col in B_CHUNKS[c]:
                        hl = (g % 2) * HG + j
                        nc.tensor.matmul(ps[4 + c % 2][:, col:col + S - k * P],
                                         kr[0:MROWS, u % 2, hl, k * P:(k + 1) * P],
                                         qr[0:MROWS, u % 2, hl, k * P:S], start=True, stop=False)
                        last = nc.tensor.matmul(ps[4 + c % 2][:, col:col + P], causal_b, ident_b,
                                                start=False, stop=True)
                    last.then_inc(b_ps[l], 1)

                def turn_maxima(g):
                    pe.wait_ge(m_ready[l], g + 1)
                    if g == 0:
                        pe.wait_ge(mod_sb[l], 1 + B)
                    if g >= 2:
                        pe.wait_ge(ctx_ready[l], g - 1)
                    nc.tensor.transpose(ps[7][0:32, 0:P // 2].bitcast(BF16), mneg[:, g % 2, :], ident_b).then_inc(m_tr[l], 1)

                def weigh_values(g):
                    b, hg = g // 4, g % 4
                    pe.wait_ge(b_exp[l], NB * (g + 1))
                    if g >= 1:
                        pe.wait_ge(ctxden_ready[l], g)
                    for k in range(TB):
                        for j in range(HG):
                            last = nc.tensor.matmul(ps[6][32 * j:32 * j + 32, k * P:S],
                                                    vaug[:, b * TB + k, hg * HG + j, :],
                                                    pt[:, g % 2, j, PK[k]:PK[k] + S - k * P],
                                                    start=(k == 0), stop=(k == TB - 1))
                    last.then_inc(pv_ps[l], 1)

                def turn_context(g):
                    pe.wait_ge(ctxden_ready[l], g + 1)
                    if g + 1 < NG:
                        pe.wait_ge(mT_ready[l], g + 2)
                    else:
                        pe.wait_ge(ctx_ready[l], g)
                    for i in range(TB):
                        last = nc.tensor.transpose(ps[7][:, i * P:(i + 1) * P], ctxden[:, g % 2, i * P:(i + 1) * P], ident)
                    last.then_inc(c_tr[l], 1)

                pe.wait_ge(ones_set, 2)
                for s in range(NG + 2):
                    if s < NG:
                        scores_by_query(s, 0)
                        scores_by_query(s, 1)
                    if 1 <= s - 1 < NG:
                        turn_maxima(s - 1)
                    if s == NG:
                        pe.wait_ge(a_max[l], NA * NG)
                        turn_batch(l, 1, 0, ctx_ready[l], NG // B)
                    if 0 <= s - 2 < NG:
                        weigh_values(s - 2)
                    if s < NG:
                        scores_by_query(s, 2)
                    if 0 <= s - 2 < NG:
                        turn_context(s - 2)
                    for c in range(NB):
                        if 0 <= s - 1 < NG:
                            scores_by_key(s - 1, c)
                        if s < NG and c in (1, 4, 7):
                            scores_by_query(s, 3 + c // 3)
                            if s == 0 and c == 7:
                                fill(EARLY)
                                fill(EARLY + 1)
                                turn_maxima(0)
                                fill(EARLY + 2)
                                fill(EARLY + 3)
                        if s == NG and c == 4:
                            project(l, 0)

                turn_batch(l, 1, 1, ctx_ready[l], NG // B)
                project(l, 1)

                E, K = EXPERTS[l], TOPK[l]
                pe.wait_ge(ld_small, 64)
                for b in range(B):
                    turn_batch(l, 2, b, tok_ready[l], 1)
                    pe.wait_ge(feat_ready[l], TURNS * 2 + KD * (b + 1))
                    for t in range(b * TB, (b + 1) * TB):
                        for k in range(KD):
                            last = nc.tensor.matmul(gate_bank[b][:, t * 16:t * 16 + E], feat[:, k, t * P:(t + 1) * P],
                                                    gw[:, l, k, 0:E], start=(k == 0), stop=(k == KD - 1))
                    last.then_inc(gate_ps[l], 1)
                pe.wait_ge(chosen_ready, B * (l + 1))
                nc.tensor.matmul(ps[7][:, 0:NT * E], before_b, chosen[:, 0:NT * E], start=True, stop=False)
                for t in range(NT - 1):
                    m = NT - 1 - t
                    nc.tensor.matmul(ps[7][:, (t + 1) * E:NT * E].rearrange("p (m e) -> p m e", m=m), ones_b[:, :],
                                     chosen[:, t * E:(t + 1) * E].unsqueeze(1).broadcast_to([P, m, E]),
                                     start=False, stop=(t == NT - 2))
                for t in range(NT):
                    last = nc.tensor.matmul(ps[5][:, 0:E], ones_b[:, :], chosen[:, t * E:(t + 1) * E],
                                            start=(t == 0), stop=(t == NT - 1))
                last.then_inc(rank_ps, 1)
                for t in range(NT):
                    pe.wait_ge(place_of[l], t + 1)
                    pe.wait_ge(tile_weighed[l], t + 1)
                    for n in range(t * K, (t + 1) * K):
                        last = nc.tensor.matmul(ps[4][:, 0:2 * MT[l]], at_place[:, n * P:(n + 1) * P],
                                                at_tile[:, n * 2 * MT[l]:(n + 1) * 2 * MT[l]],
                                                start=(n == 0), stop=(n == NT * K - 1))
                last.then_inc(placed_ps, 1)

                h_free = hid_ready[l] if l == 0 else h_read

                def pe_x(ii, off):
                    i, r, rnd = tile_at(ii, off)
                    pe.wait_ge(xt_loaded[r], TILES_BEFORE[l][r] + 16 * rnd + 16)
                    if not (isinstance(i, int) and i < 2):
                        pe.wait_ge(xT_sb[l], i - 1)
                    for k in range(KD):
                        last = nc.tensor.transpose(ps[off % 2][:, k * P:(k + 1) * P], xt[:, r, k * P:(k + 1) * P], ident)
                    last.then_inc(xT_ps[l], 1)

                def experts_of(s):
                    _, pair = nc.values_load_multi_w_load_instructions(
                        te[0:1, bass.ds(s, 1), :].rearrange("p a b -> p (a b)"), engines=[mybir.EngineType.PE],
                        min_val=0, max_val=E - 1)
                    return pair

                def pe_h(ii, off, e):
                    i, _, _ = tile_at(ii, off)
                    dst = ps[2 + off % 2][:, 0:HB[l]]
                    if not (isinstance(i, int) and i < 2):
                        pe.wait_ge(h_free, i - 1)
                    nc.tensor.matmul(dst, ones_b[0:BIAS_ROWS, :], moe_bias(l, 0, HB[l], e), start=True, stop=False)
                    pe.wait_ge(xT_sb[l], i + 1)
                    for k in range(KD):
                        last = nc.tensor.matmul(dst, xtT[:, off % 2, k, :], moe_w1(l, k, e), start=False, stop=(k == KD - 1))
                    last.then_inc(h_ps[l], 1)

                def pe_hT(ii, off):
                    i, _, _ = tile_at(ii, off)
                    pe.wait_ge(hid_ready[l], i + 1)
                    if not (isinstance(i, int) and i < 2):
                        pe.wait_ge(hT_sb[l], i - 1)
                    for k in range(2):
                        last = nc.tensor.transpose(ps[4 + off % 2][0:HK[l], k * P:(k + 1) * P],
                                                   hid[:, off % 2, k * HK[l]:(k + 1) * HK[l]], ident)
                    last.then_inc(hT_ps[l], 1)

                def pe_y(ii, off, e):
                    i, _, _ = tile_at(ii, off)
                    dst = ps[6 + off % 2][:, 0:D]
                    if not (isinstance(i, int) and i < 2):
                        pe.wait_ge(y_sb[l], i - 1)
                    nc.tensor.matmul(dst, ones_b[0:BIAS_ROWS, :], moe_bias(l, HB[l], BROW[l], e), start=True, stop=False)
                    pe.wait_ge(hT_sb[l], i + 1)
                    for k in range(2):
                        last = nc.tensor.matmul(dst, hidT[0:HK[l], off % 2, k, :], moe_w2(l, k, e), start=False, stop=(k == 1))
                    last.then_inc(y_ps[l], 1)

                def pe_step(ii, off):
                    n = SLOTS_T[l]
                    known = isinstance(ii, int)
                    if not known or off < n:
                        pe_x(ii, off)
                    e_h, e_y = experts_of(tile_at(ii, off)[0])
                    if not known or 0 <= off - 1 < n:
                        pe_h(ii, off - 1, e_h)
                    if not known or 0 <= off - 2 < n:
                        pe_hT(ii, off - 2)
                    if not known or 0 <= off - 3 < n:
                        pe_y(ii, off - 3, e_y)

                pe.wait_ge(slots_ready[l], 1)
                pe.wait_ge(brows_ready[l], 48)
                pe.wait_ge(ld_w_lo[l], 16 * NG)
                if l == 1:
                    pe.wait_ge(ld_w_hi, 16)
                for s in range(STEADY):
                    pe_step(0, s)
                with pe.Fori(0, (SLOTS_T[l] - STEADY) // UNROLL) as ii:
                    for q in range(UNROLL):
                        pe_step(ii, STEADY + q)
                for s in range(SLOTS_T[l], SLOTS_T[l] + 3):
                    pe_step(0, s)


def _by_k(w, np):
    n, k = w.shape
    return np.ascontiguousarray(w.T.reshape(k // P, P, n).transpose(1, 0, 2))


def _mixture(w1, w2, l, np):
    e, h, d = w1.shape
    if l == 1:
        w1 = np.concatenate([w1[:, 0::2], w1[:, 1::2]], 1)
    a = np.zeros((e, HB[l], d), w1.dtype)
    a[:, :h] = w1
    a = a.transpose(2, 0, 1).reshape(KD, P, e, HB[l]).transpose(1, 2, 0, 3).reshape(P, e, KD * HB[l])
    rows = np.zeros((e, 2 * HK[l], d), w2.dtype)
    rows[:, :w2.shape[2]] = w2.transpose(0, 2, 1)
    rows = rows.reshape(e, 2, HK[l], d).transpose(2, 0, 1, 3).reshape(HK[l], e, 2 * d)
    b = np.zeros((P, e, 2 * d), w2.dtype)
    b[:HK[l]] = rows
    return np.ascontiguousarray(np.concatenate([a, b], 2).reshape(P, -1))


def _biases(b1, b2, l, np):
    e, h = b1.shape
    if l == 1:
        b1 = np.concatenate([b1[:, 0::2], b1[:, 1::2]], 1)
    out = np.zeros((e, BROW[l]), b1.dtype)
    out[:, :h] = b1
    out[:, HB[l]:] = b2
    return out


def kernel(**inputs):
    import numpy as np
    import concourse.bacc as bacc
    from concourse.bass_utils import run_bass_kernel_spmd

    a = {k: np.asarray(v) for k, v in inputs.items()}

    def spread_rows(v):
        return np.broadcast_to(v, (P,) + v.shape)

    consts = np.zeros((P, CONST_W), np.float32)
    consts[:, 0:P] = np.eye(P)
    consts[:, P:P + 16] = np.arange(16)
    consts[:, P + 16:P + 24] = np.arange(8) * P
    consts[:, P + 24:P + 280] = np.tril(np.ones((16, 16)), -1).reshape(-1)
    consts[:, P + 280:P + 328] = np.arange(MT[1])
    consts[:, P + 328:2 * P + 328] = np.arange(P)
    consts[:, 2 * P + 328:2 * P + 328 + NT] = T - np.arange(T).reshape(NT, P).T
    consts[:, 2 * P + 328 + NT] = np.arange(P)
    consts[:, 2 * P + 329 + NT:] = np.arange(MT[1]) * P
    row, col = np.arange(P)[:, None], np.arange(P)[None, :]
    constb = np.concatenate([np.eye(P), np.where(col > row, BIG_NEG, 0.0), row < col], 1).astype(np.float32)

    def pad16(v):
        return np.concatenate([v, np.zeros(16 - len(v), v.dtype)])

    gws = []
    for name in ("L0_ffn_gate_w", "L1_ffn_gate_w"):
        w = a[name]
        w = np.concatenate([w, np.zeros((16 - len(w), D), w.dtype)], 0)
        gws.append(_by_k(w, np))
    def by_dim(w):
        return w.reshape(2, 8, HD, -1).transpose(0, 2, 1, 3).reshape(w.shape)

    arrays = {
        "x": a["L0_attn_x"].reshape(T, D),
        "consts": consts,
        "constb": constb,
        "cT": np.stack([a[f"L{l}_c"].T.reshape(KD, P, B).transpose(1, 0, 2) for l in range(2)], 1).reshape(P, 2 * KD * B),
        "wmod": np.stack([a[f"L{l}_wmod"].reshape(KD, P, 6 * D).transpose(1, 0, 2) for l in range(2)]),
        "wqkv": np.stack([
            _by_k(np.concatenate([by_dim(a["L0_attn_Wq"]), by_dim(a["L0_attn_Wk"]), a["L0_attn_Wv"]], 0), np),
            _by_k(np.concatenate([by_dim(a["L1_attn_wq"]), by_dim(a["L1_attn_wk"]), a["L1_attn_wv"]], 0), np)]),
        "wo": np.stack([_by_k(a["L0_attn_Wo"], np), _by_k(a["L1_attn_wo"], np)]),
        "rows": spread_rows(np.stack([a["L1_attn_bv"], a["L1_attn_bo"], a["L1_ffn_norm_w"]])),
        "qkb": np.concatenate([by_dim(a["L1_attn_bq"]).reshape(KD, P).T, by_dim(a["L1_attn_bk"]).reshape(KD, P).T], 1),
        "gbias": spread_rows(np.stack([pad16(a["L0_ffn_gate_b"]), pad16(a["L1_ffn_gate_b"]), pad16(a["L0_ffn_bias"])])),
        "gw": np.stack(gws, 1),
        "moe0": _mixture(a["L0_ffn_w1"], a["L0_ffn_w2"], 0, np),
        "moe1": _mixture(a["L1_ffn_w1"], a["L1_ffn_w2"], 1, np),
        "bias0": _biases(a["L0_ffn_b1"], a["L0_ffn_b2"], 0, np),
        "bias1": _biases(a["L1_ffn_b1"], a["L1_ffn_b2"], 1, np),
    }
    nc = bacc.Bacc("TRN2", target_bir_lowering=False, num_devices=1)
    arrays = {f"in_{k}_dram": np.ascontiguousarray(v) for k, v in arrays.items()}
    dram = {k[3:-5]: nc.dram_tensor(k, v.shape, mybir.dt.from_np(v.dtype), kind="ExternalInput").ap()
            for k, v in arrays.items()}
    out = nc.dram_tensor("out_dram", (T, D), F32, kind="ExternalOutput").ap()
    build_kernel(nc, dram, out)
    r = run_bass_kernel_spmd(nc, [arrays], core_ids=[0])
    return r.results[0]["out_dram"].reshape(B, S, D)
```
